# Optimizing a Trainium2 kernel written in Bass

```python
import numpy as np
import jax
import jax.numpy as jnp

def _softmax(x, axis=-1):
    return jax.nn.softmax(x, axis=axis)

def _gelu(x):
    return jax.nn.gelu(x, approximate=True)

def _silu(x):
    return jax.nn.silu(x)

def _sigmoid(x):
    return jax.nn.sigmoid(x)

def _layernorm(x, axis=-1, eps=1e-05):
    m = jnp.mean(x, axis=axis, keepdims=True)
    v = jnp.var(x, axis=axis, keepdims=True)
    return (x - m) / jnp.sqrt(v + eps)

def _scatter_add(tgt, idx, src, axis=0):
    return tgt.at[idx].add(src)

def _segment_sum(src, seg, n):
    return jax.ops.segment_sum(src, seg, n)
kernel_name = 'mk_recurrent_d1_jaxref_r4_2a51d3'

def setup_inputs(seed: int=0):
    np.random.seed(seed)
    _w = jnp.asarray

    def _L0_attn_setup():
        import jax, jax.numpy as jnp
        import numpy as np
        D_MODEL = 512
        N_HEAD = 16
        MLP_HIDDEN = 1408
        NORMALIZER = 16.0

        def rmsnorm(x, w, eps=1e-05):
            return x * jax.lax.rsqrt(jnp.mean(x * x, axis=-1, keepdims=True) + eps) * w

        def _reference_tuple_inner(x, Wq, Wk, Wkg1, Wkg2, bkg2, Wv, Wg, bg, Wo, ln1_w, ln2_w, W1, W3, W2):
            B, L, d = x.shape
            H = N_HEAD
            hd = d // H
            kd = d // 2 // H
            scaling = (d // H) ** (-0.5)
            xn = rmsnorm(x, ln1_w)
            q = xn @ Wq
            k = xn @ Wk * scaling
            gk = jax.nn.log_sigmoid(xn @ Wkg1 @ Wkg2 + bkg2) / NORMALIZER
            v = xn @ Wv
            g = xn @ Wg + bg
            split = lambda t, dh: t.reshape(B, L, H, dh).transpose(1, 0, 2, 3)
            qh, kh, gh = (split(q, kd), split(k, kd), split(gk, kd))
            vh = split(v, hd)
            S0 = jnp.zeros((B, H, kd, hd), x.dtype)

            def step(S, inp):
                qt, kt, vt, gt = inp
                S = S * jnp.exp(gt)[..., None] + kt[..., None] * vt[..., None, :]
                ot = jnp.einsum('bhk,bhkd->bhd', qt, S)
                return (S, ot)
            Sf, o = jax.lax.scan(step, S0, (qh, kh, vh, gh))
            mu = jnp.mean(o, axis=-1, keepdims=True)
            var = jnp.var(o, axis=-1, keepdims=True)
            o = (o - mu) * jax.lax.rsqrt(var + 1e-05)
            o = o.transpose(1, 0, 2, 3).reshape(B, L, d)
            o = jax.nn.silu(g) * o
            x = x + o @ Wo
            xn2 = rmsnorm(x, ln2_w)
            x = x + jax.nn.silu(xn2 @ W1) * (xn2 @ W3) @ W2
            return (x, Sf)
        key = jax.random.key(seed)
        d, B, L, Hd = (D_MODEL, 2, 1024, MLP_HIDDEN)
        ks = jax.random.split(key, 12)
        w = lambda k, shape, s=0.02: jax.random.normal(k, shape, jnp.float32) * s
        return {'x': jax.random.normal(ks[0], (B, L, d), jnp.float32), 'Wq': w(ks[1], (d, d // 2)), 'Wk': w(ks[2], (d, d // 2)), 'Wkg1': w(ks[3], (d, 16)), 'Wkg2': w(ks[4], (16, d // 2)), 'bkg2': jnp.zeros((d // 2,), jnp.float32), 'Wv': w(ks[5], (d, d)), 'Wg': w(ks[6], (d, d)), 'bg': jnp.zeros((d,), jnp.float32), 'Wo': w(ks[7], (d, d)), 'ln1_w': jnp.ones((d,), jnp.float32), 'ln2_w': jnp.ones((d,), jnp.float32), 'W1': w(ks[8], (d, Hd)), 'W3': w(ks[9], (d, Hd)), 'W2': w(ks[10], (Hd, d))}
    _L0_attn_in = _L0_attn_setup()

    def _L0_ffn_setup():
        import jax, jax.numpy as jnp
        import numpy as np
        B, S, D, K, R = (4, 512, 512, 8, 64)
        key = jax.random.key(seed)
        ks = jax.random.split(key, 7)
        x = jax.random.normal(ks[0], (B, S, D), dtype=jnp.float32)
        U = jax.random.normal(ks[1], (K, D, R), dtype=jnp.float32) * 0.02
        V = jax.random.normal(ks[2], (K, R, D), dtype=jnp.float32) * 0.02
        W1 = jax.random.normal(ks[3], (D, D), dtype=jnp.float32) * 0.02
        b1 = jnp.zeros((D,), dtype=jnp.float32)
        W2 = jax.random.normal(ks[4], (D, K), dtype=jnp.float32) * 0.02
        b2 = jnp.zeros((K,), dtype=jnp.float32)
        return {'x': x, 'U': U, 'V': V, 'W1': W1, 'b1': b1, 'W2': W2, 'b2': b2}
    _L0_ffn_in = _L0_ffn_setup()
    _d = {'L0_attn_x': _L0_attn_in['x'], 'L0_attn_Wq': _L0_attn_in['Wq'], 'L0_attn_Wk': _L0_attn_in['Wk'], 'L0_attn_Wkg1': _L0_attn_in['Wkg1'], 'L0_attn_Wkg2': _L0_attn_in['Wkg2'], 'L0_attn_bkg2': _L0_attn_in['bkg2'], 'L0_attn_Wv': _L0_attn_in['Wv'], 'L0_attn_Wg': _L0_attn_in['Wg'], 'L0_attn_bg': _L0_attn_in['bg'], 'L0_attn_Wo': _L0_attn_in['Wo'], 'L0_attn_ln1_w': _L0_attn_in['ln1_w'], 'L0_attn_ln2_w': _L0_attn_in['ln2_w'], 'L0_attn_W1': _L0_attn_in['W1'], 'L0_attn_W3': _L0_attn_in['W3'], 'L0_attn_W2': _L0_attn_in['W2'], 'L0_ffn_U': _L0_ffn_in['U'], 'L0_ffn_V': _L0_ffn_in['V'], 'L0_ffn_W1': _L0_ffn_in['W1'], 'L0_ffn_b1': _L0_ffn_in['b1'], 'L0_ffn_W2': _L0_ffn_in['W2'], 'L0_ffn_b2': _L0_ffn_in['b2']}
    _x0 = _d['L0_attn_x']
    _d['L0_attn_x'] = jax.random.normal(jax.random.fold_in(jax.random.key(seed), 1), (8, 512, 512), dtype=_x0.dtype)
    del _x0
    return _d

def reference(L0_attn_x, L0_attn_Wq, L0_attn_Wk, L0_attn_Wkg1, L0_attn_Wkg2, L0_attn_bkg2, L0_attn_Wv, L0_attn_Wg, L0_attn_bg, L0_attn_Wo, L0_attn_ln1_w, L0_attn_ln2_w, L0_attn_W1, L0_attn_W3, L0_attn_W2, L0_ffn_U, L0_ffn_V, L0_ffn_W1, L0_ffn_b1, L0_ffn_W2, L0_ffn_b2):

    def _L0_attn_ref(x, Wq, Wk, Wkg1, Wkg2, bkg2, Wv, Wg, bg, Wo, ln1_w, ln2_w, W1, W3, W2):
        import jax, jax.numpy as jnp
        import numpy as np
        D_MODEL = 512
        N_HEAD = 16
        MLP_HIDDEN = 1408
        NORMALIZER = 16.0

        def rmsnorm(x, w, eps=1e-05):
            return x * jax.lax.rsqrt(jnp.mean(x * x, axis=-1, keepdims=True) + eps) * w

        def _reference_tuple_inner(x, Wq, Wk, Wkg1, Wkg2, bkg2, Wv, Wg, bg, Wo, ln1_w, ln2_w, W1, W3, W2):
            B, L, d = x.shape
            H = N_HEAD
            hd = d // H
            kd = d // 2 // H
            scaling = (d // H) ** (-0.5)
            xn = rmsnorm(x, ln1_w)
            q = xn @ Wq
            k = xn @ Wk * scaling
            gk = jax.nn.log_sigmoid(xn @ Wkg1 @ Wkg2 + bkg2) / NORMALIZER
            v = xn @ Wv
            g = xn @ Wg + bg
            split = lambda t, dh: t.reshape(B, L, H, dh).transpose(1, 0, 2, 3)
            qh, kh, gh = (split(q, kd), split(k, kd), split(gk, kd))
            vh = split(v, hd)
            S0 = jnp.zeros((B, H, kd, hd), x.dtype)

            def step(S, inp):
                qt, kt, vt, gt = inp
                S = S * jnp.exp(gt)[..., None] + kt[..., None] * vt[..., None, :]
                ot = jnp.einsum('bhk,bhkd->bhd', qt, S)
                return (S, ot)
            Sf, o = jax.lax.scan(step, S0, (qh, kh, vh, gh))
            mu = jnp.mean(o, axis=-1, keepdims=True)
            var = jnp.var(o, axis=-1, keepdims=True)
            o = (o - mu) * jax.lax.rsqrt(var + 1e-05)
            o = o.transpose(1, 0, 2, 3).reshape(B, L, d)
            o = jax.nn.silu(g) * o
            x = x + o @ Wo
            xn2 = rmsnorm(x, ln2_w)
            x = x + jax.nn.silu(xn2 @ W1) * (xn2 @ W3) @ W2
            return (x, Sf)
        return _reference_tuple_inner(x, Wq, Wk, Wkg1, Wkg2, bkg2, Wv, Wg, bg, Wo, ln1_w, ln2_w, W1, W3, W2)[0]

    def _L0_ffn_ref(x, U, V, W1, b1, W2, b2):
        import jax, jax.numpy as jnp
        import numpy as np
        B, S, D, K, R = (4, 512, 512, 8, 64)
        h = jax.nn.relu(jnp.einsum('bsd,de->bse', x, W1) + b1)
        alpha = jax.nn.softmax(jnp.einsum('bse,ek->bsk', h, W2) + b2, axis=-1)
        vx = jnp.einsum('krd,bsd->bskr', V, x)
        uvx = jnp.einsum('kdr,bskr->bskd', U, vx)
        out = jnp.einsum('bsk,bskd->bsd', alpha, uvx)
        return out
    x = L0_attn_x
    xn = _layernorm(x, axis=-1)
    s = _L0_attn_ref(xn, L0_attn_Wq, L0_attn_Wk, L0_attn_Wkg1, L0_attn_Wkg2, L0_attn_bkg2, L0_attn_Wv, L0_attn_Wg, L0_attn_bg, L0_attn_Wo, L0_attn_ln1_w, L0_attn_ln2_w, L0_attn_W1, L0_attn_W3, L0_attn_W2)
    g = _silu(_L0_ffn_ref(xn, L0_ffn_U, L0_ffn_V, L0_ffn_W1, L0_ffn_b1, L0_ffn_W2, L0_ffn_b2))
    x = x + s * g
    return x

_drawn_inputs = setup_inputs


def setup_inputs(seed=0):
    import zlib

    import numpy as np

    out = dict(_drawn_inputs(seed))
    spreads = {'L0_attn_bkg2': (0.0, 0.8),
     'L0_attn_bg': (0.0, 0.8),
     'L0_attn_ln1_w': (1.0, 0.6),
     'L0_attn_ln2_w': (1.0, 0.6),
     'L0_ffn_b1': (0.0, 0.8),
     'L0_ffn_b2': (0.0, 0.8)}
    factors = {'L0_attn_Wq': 8.0,
     'L0_attn_Wk': 8.0,
     'L0_attn_Wkg1': 8.0,
     'L0_attn_Wkg2': 8.0,
     'L0_attn_Wv': 8.0,
     'L0_attn_Wg': 8.0,
     'L0_attn_Wo': 8.0,
     'L0_attn_W1': 8.0,
     'L0_attn_W3': 8.0,
     'L0_attn_W2': 8.0,
     'L0_ffn_U': 4.31,
     'L0_ffn_V': 4.314,
     'L0_ffn_W1': 8.0,
     'L0_ffn_W2': 8.0}
    for name, (base, spread) in spreads.items():
        noise = np.random.default_rng([zlib.crc32(name.encode()), seed]).standard_normal(out[name].shape)
        drawn = base * np.exp(spread * noise) if base else spread * noise
        out[name] = jnp.asarray(drawn.astype(out[name].dtype))
    for name, factor in factors.items():
        out[name] = (out[name] * factor).astype(out[name].dtype)
    return out
```

```python
from contextlib import ExitStack

import concourse.bass as bass
from concourse import mybir

F32 = mybir.dt.float32
F32R = mybir.dt.float32r
ALU = mybir.AluOpType
ACT = mybir.ActivationFunctionType
AX = mybir.AxisListType.X
EXP_LN_SET = "natural_log_exp_and_others"
SILU_SET = "silu_and_others"

P = 128
EPS = 1e-5
GATE_SCALE = 1.0 / 16.0


class Event:

    def __init__(self, sem, per):
        self.sem, self.per = sem, per


class Events:

    def __init__(self, nc, ctx, prefix):
        self.nc, self.ctx, self.prefix, self.all = nc, ctx, prefix, {}

    def add(self, name, per=1):
        assert name not in self.all
        self.all[name] = Event(self.ctx.enter_context(self.nc.semaphore(f"{self.prefix}_{name}")), per)

    def at(self, name, i, k=None):
        e = self.all[name]
        return e.sem, i * e.per + (e.per + (e.per if k is None else k))

    def at_before(self, name, i, k=None):
        e = self.all[name]
        return e.sem, i * e.per + (e.per if k is None else k)

    def wait(self, eng, name, i, k=None):
        eng.wait_ge(*self.at(name, i, k))

    def wait_before(self, eng, name, i, k=None):
        eng.wait_ge(*self.at_before(name, i, k))

    def up(self, name, ins):
        ins.then_inc(self.all[name].sem, 1)

    def up_dma(self, name, ins):
        ins.then_inc(self.all[name].sem, 16)

    def give_credits(self, eng):
        for e in self.all.values():
            eng.sem_inc(e.sem, e.per)


class Slots:

    def __init__(self, ev, name, regions, order, early=()):
        self.ev, self.name, self.regions = ev, name, regions
        self.where, used = {}, [0] * len(regions)
        for n, result in enumerate(order):
            r = n % len(regions)
            used[r] += 1
            self.where[result] = (r, used[r], 1 if early and result not in early else 0)
        for r, n in enumerate(used):
            ev.add(f"{name}{r}_ready", n)
            ev.add(f"{name}{r}_taken", n)

    def wait(self, eng, what, result, i, before=0):
        r, k, bodies = self.where[result]
        name = f"{self.name}{r}_{what}"
        per = self.ev.all[name].per
        self.ev.wait(eng, name, i, k + (bodies - before) * per)
        return self.regions[r]

    def open(self, pe, result, i):
        r, k, bodies = self.where[result]
        name = f"{self.name}{r}_taken"
        self.ev.wait(pe, name, i, k - 1 + bodies * self.ev.all[name].per)
        return self.regions[r]

    def complete(self, result, ins):
        self.ev.up(f"{self.name}{self.where[result][0]}_ready", ins)

    def get(self, eng, result, i):
        return self.wait(eng, "ready", result, i)

    def get_before(self, eng, result, i):
        self.wait(eng, "ready", result, i, 1)

    def take(self, result, ins):
        self.ev.up(f"{self.name}{self.where[result][0]}_taken", ins)

    def wait_taken(self, eng, result, i):
        self.wait(eng, "taken", result, i)

    def wait_taken_before(self, eng, result, i):
        self.wait(eng, "taken", result, i, 1)

    def skip(self, pe, results, i):
        for result in results:
            self.open(pe, result, i)
            for what in ("ready", "taken"):
                pe.sem_inc(self.ev.all[f"{self.name}{self.where[result][0]}_{what}"].sem, 1)


def bcast(ap, axis, n):
    shape = list(ap.shape)
    shape.insert(axis, n)
    return ap.unsqueeze(axis).broadcast_to(shape)


def product3(pe, out, terms):
    last = len(terms) - 1
    for n, ((lh, ll), (rh, rl)) in enumerate(terms):
        pe.matmul(out, lh, rh, start=n == 0, stop=False)
        pe.matmul(out, lh, rl, start=False, stop=False)
        ins = pe.matmul(out, ll, rh, start=False, stop=n == last)
    return ins


def loop(eng, n, first, body, peel=False):
    loop_parts(eng, n, {None: first}, lambda i, ahead: body(i, lambda: ahead(None)), peel)


def loop_parts(eng, n, parts, body, peel=False, before=None, skip=None):
    for part, work in parts.items():
        if before:
            before(part)
        work(0)
    if before:
        before("body")
    if peel:
        body(0, lambda part: parts[part](1))
    with eng.Fori(1 if peel else 0, n - 1) as i:
        body(i, lambda part: parts[part](i + 1))
    body(n - 1, skip or (lambda part: None))


def nothing(i):
    pass


def row(dram, i):
    return dram[bass.ds(i, 1)]


def make_constants(nc, consts):
    with ExitStack() as ctx:
        s_fill = ctx.enter_context(nc.semaphore("s_fill"))
        s_row = ctx.enter_context(nc.semaphore("s_row"))
        block = ctx.enter_context(nc.Block())
        ident, hmask, causal, avg32, avg_all, chunk_start, eps = consts

        @block.gpsimd
        def _(pool):
            n = 0

            def step(ins):
                nonlocal n
                n += 1
                ins.then_inc(s_fill, 1)
                pool.wait_ge(s_fill, n)

            def select(ap, op, base, pattern, cm, fill):
                step(pool.affine_select(out=ap, in_=ap, compare_op=op, fill=fill, base=base,
                                        pattern=pattern, channel_multiplier=cm))

            step(pool.memset(ident, 0.0))
            select(ident, ALU.not_equal, 0, [[-1, P]], 1, 1.0)
            step(pool.memset(hmask, 1.0))
            select(hmask, ALU.is_ge, 0, [[-16, 8]], 1, 0.0)
            select(hmask, ALU.is_ge, 15, [[16, 8]], -1, 0.0)
            step(pool.memset(causal, 1.0))
            select(causal, ALU.is_ge, 0, [[1, P]], -1, 0.0)
            step(pool.memset(avg32, 1.0 / 32))
            a = avg32.rearrange("p (a b) -> p a b", b=32)
            select(a, ALU.is_ge, 0, [[-32, 4], [0, 32]], 1, 0.0)
            select(a, ALU.is_ge, 31, [[32, 4], [0, 32]], -1, 0.0)
            step(pool.memset(avg_all, 1.0 / 512))
            step(pool.memset(eps, EPS))
            step(pool.memset(chunk_start, 1.0))
            step(pool.memset(chunk_start.rearrange("p (c t) -> p c t", t=P)[:, :, 0:1], 0.0))


def flat(ap):
    return ap.rearrange("p a b -> p (a b)")


def attention_weights(nc, ctx, KT, D, KD):
    def sb(name, shape, dt=F32):
        return ctx.enter_context(nc.sbuf_tensor("a_" + name, shape, dt))[:]

    w = {name: [sb(name + part, [P, KT, n], F32R) for part in ("hi", "lo")]
         for name, n in (("wkg1", P), ("wk", KD), ("wq", KD), ("wv", D), ("wg", D), ("wo", D))}
    w.update(wkg2=sb("wkg2", [P, KD]), bkg2=sb("bkg2", [P, KD // P]), bg=sb("bg", [P, KT]), ln1=sb("ln1", [P, KT]),
             stage=[sb(f"stage{n}", [P, D]) for n in range(2)], mean=sb("mean", [P, D // 32]), fold=sb("fold", [P, D // 32, 16]))
    return w


def prepare_attention_weights(nc, ctx, pool, w, Wq, Wk, Wkg1, Wkg2, bkg2, Wv, Wg, bg, Wo, ln1_w):
    s_small, s_step = (ctx.enter_context(nc.semaphore(f"aw_{n}")) for n in ("small", "step"))
    s_load = [ctx.enter_context(nc.semaphore(f"aw_load{n}")) for n in range(2)]
    steps = [0]

    def step(ins):
        steps[0] += 1
        ins.then_inc(s_step, 1)
        pool.wait_ge(s_step, steps[0])

    step(pool.memset(w["wkg2"], 0.0))
    for part in w["wkg1"]:
        step(pool.memset(part.bitcast(F32), 0.0))
    pool.dma_start(w["wkg2"][0:Wkg2.shape[0], :], Wkg2).then_inc(s_small, 16)
    for dst, src in ((w["bkg2"], bkg2), (w["bg"], bg), (w["ln1"], ln1_w)):
        pool.dma_start(dst, src.rearrange("(m p) -> p m", p=P), allow_slow_non_contiguous=True).then_inc(s_small, 16)
    jobs = [(name, src, kt) for name, src in (("wkg1", Wkg1), ("wk", Wk), ("wq", Wq), ("wv", Wv), ("wg", Wg), ("wo", Wo))
            for kt in range(src.shape[0] // P)]

    def load(n):
        _, src, kt = jobs[n]
        pool.dma_start(w["stage"][n % 2][:, 0:src.shape[1]], src[kt * P:(kt + 1) * P, :]).then_inc(s_load[n % 2], 16)

    load(0)
    pool.wait_ge(s_small, 64)
    for n, (name, src, kt) in enumerate(jobs):
        if n + 1 < len(jobs):
            load(n + 1)
        cols = src.shape[1]
        s = w["stage"][n % 2][:, 0:cols]
        pool.wait_ge(s_load[n % 2], 16 * (n // 2 + 1))
        if name == "wv":
            heads = s.rearrange("p (a b) -> p a b", b=32)
            step(pool.tensor_tensor(w["fold"][:, :, 0:16], heads[:, :, 0:16], heads[:, :, 16:32], ALU.add))
            for half in (8, 4, 2, 1):
                step(pool.tensor_tensor(w["fold"][:, :, 0:half], w["fold"][:, :, 0:half],
                                        w["fold"][:, :, half:2 * half], ALU.add))
            step(pool.tensor_scalar(w["mean"], w["fold"][:, :, 0], 1.0 / 32, None, ALU.mult))
            step(pool.tensor_tensor(heads, heads, bcast(w["mean"], 2, 32), ALU.subtract))
        if name != "wo":
            step(pool.tensor_scalar(s, s, w["ln1"][:, kt:kt + 1], None, ALU.mult))
        hi, lo = (part[:, kt, 0:cols] for part in w[name])
        step(pool.tensor_copy(hi, s))
        step(pool.tensor_tensor(lo, s, hi.bitcast(F32), ALU.subtract))


def phase_f(nc, background, consts, x, U, V, W1, b1, W2, b2, xn_d, xa_d, gate_d):
    ident, eps = consts[0], consts[-1]
    NB, T, D = x.shape
    KT, TT = D // P, T // P
    E, R = U.shape[0], U.shape[2]
    ctx = ExitStack()
    with ctx:
        def sb(name, shape, dt=F32):
            return ctx.enter_context(nc.sbuf_tensor("f_" + name, shape, dt))[:]

        w1 = [sb(f"w1{a}", [P, KT, D], F32R) for a in ("hi", "lo")]
        vt = [sb(f"vt{a}", [P, KT, E * R], F32R) for a in ("hi", "lo")]
        ut = [sb(f"ut{a}", [P, KT, D], F32R) for a in ("hi", "lo")]
        w2 = sb("w2", [P, KT, E])
        b1_sb, b2_sb = sb("b1", [P, KT]), sb("b2", [P, E])
        xt = sb("xt", [P, TT, D])
        xs = sb("xs", [P, TT, D])
        xn = sb("xn", [P, KT, T])
        xa = sb("xa", [P, KT, T])
        xn_hl = [sb(f"xn{a}", [P, KT, T], F32R) for a in ("hi", "lo")]
        h1 = sb("h1", [P, KT, T])
        assert T == E * R == KT * P == TT * P
        alpha = h1
        vx = gate = alpha_b = sb("gate", [P, KT, T])
        vx_hl = [sb(f"vx{a}", [P, KT, T], F32R) for a in ("hi", "lo")]
        stats, mv = sb("stats", [P, TT, 6]), sb("mv", [P, TT, 2])
        rstd, r1 = sb("rstd", [P, TT]), sb("r1", [P, TT])
        logit, top = sb("logit", [P, TT, E]), sb("top", [P, TT])
        psum = [ctx.enter_context(nc.psum_tensor(f"f_ps{b}", [P, 512], F32))[:] for b in range(8)]

        w1_in, v_in, u_in = xs, xn, xa
        s_w1, s_v, s_u, s_small, s_turned, s_whi, s_wlo = (
            ctx.enter_context(nc.semaphore(f"fw_{n}")) for n in ("w1", "v", "u", "small", "turned", "hi", "lo"))
        pieces = ([(psum[m], vt[0][:, m, :], vt[1][:, m, :]) for m in range(KT)]
                  + [(psum[KT + m], ut[0][:, m, :], ut[1][:, m, :]) for m in range(KT)]
                  + [(w1_in[:, k, :], w1[0][:, k, :], w1[1][:, k, :]) for k in range(KT)])

        ev = Events(nc, ctx, "f")
        for name, per in (("stats", TT), ("mv", TT), ("rstd", 2), ("m2", 2), ("r1", 2), ("norm", TT), ("norm2", TT),
                          ("xnhi", KT), ("xnlo", KT), ("softmax", 4), ("exp", 1), ("alpha", 1), ("vxhi", KT),
                          ("vxlo", KT), ("x_in", 16), ("xn_out", 16), ("xa_out", 16), ("gate_out", 16)):
            ev.add(name, per)
        xn_parts, xa_parts, alphas, hs, vs, us = ([f"{n}{m}" for m in range(KT)]
                                                  for n in ("xn", "xa", "alpha", "h", "v", "u"))
        turn = Slots(ev, "turn", psum[0:3], xn_parts + alphas + xa_parts, xn_parts + xa_parts)
        dense = Slots(ev, "dense", psum[3:8], ["logit"] + vs + hs + us, hs)
        LAST = KT - 1
        block = ctx.enter_context(nc.Block())

        @block.gpsimd
        def _(pool):
            background(ctx, pool)

        @block.sync
        def _(sp):
            ev.give_credits(sp)
            sp.dma_start(v_in, V.rearrange("(m a) r d -> (a r) m d", a=P // R)).then_inc(s_v, 16)
            for m in range(KT):
                sp.dma_start(u_in[:, m, :].rearrange("p (k r) -> p k r", r=R),
                             U[:, m * P:(m + 1) * P, :].rearrange("k p r -> p k r")).then_inc(s_u, 16)

            def load(i):
                turn.get_before(sp, f"xa{LAST}", i)
                ev.up_dma("x_in", sp.dma_start(xt, row(x, i).rearrange("o (tt p) d -> p (o tt) d", p=P)))

            def weights(_):
                sp.dma_start(w1_in, W1.rearrange("(k p) n -> p k n", p=P)).then_inc(s_w1, 16)
                sp.dma_start(b1_sb, b1.rearrange("(kt p) -> p kt", p=P), allow_slow_non_contiguous=True).then_inc(s_small, 16)
                sp.dma_start(w2, W2.rearrange("(kt p) e -> p kt e", p=P)).then_inc(s_small, 16)
                sp.dma_start(b2_sb, b2.partition_broadcast(P)).then_inc(s_small, 16)

            def store_xn(i):
                turn.wait_taken(sp, f"xn{LAST}", i)
                ev.up_dma("xn_out", sp.dma_start(row(xn_d, i).rearrange("o p m t -> p (o m) t"), xn))

            def store_xa(i):
                turn.wait_taken(sp, f"xa{LAST}", i)
                ev.up_dma("xa_out", sp.dma_start(row(xa_d, i).rearrange("o p m t -> p (o m) t"), xa))

            def body(i, ahead):
                ahead("x")
                ahead("xn")
                ahead("xa")

            loop_parts(sp, NB, {"x": load, "weights": weights, "xn": store_xn, "xa": store_xa}, body)
            ev.wait(sp, "xn_out", NB - 1)
            ev.wait(sp, "xa_out", NB - 1)

        @block.vector
        def _(dve):
            def norm(i):
                ev.wait(dve, "x_in", i)
                for t in range(TT):
                    ev.up("stats", dve.bn_stats(stats[:, t, :], xt[:, t, :]))
                ev.wait(dve, "stats", i)
                dve.memset(top, 0.0)
                for t in range(TT):
                    ev.up("mv", dve.bn_aggr(mv[:, t, :], stats[:, t, :]))
                ev.wait(dve, "rstd", i)
                ev.up("m2", dve.tensor_tensor(r1, mv[:, :, 1], rstd, ALU.mult))
                ev.wait(dve, "m2", i, 1)
                ev.up("m2", dve.tensor_tensor(r1, r1, rstd, ALU.mult))
                for t in range(TT):
                    ev.up("norm", dve.tensor_scalar(xt[:, t, :], xt[:, t, :], mv[:, t, 0:1], rstd[:, t:t + 1],
                                                    ALU.subtract, ALU.mult))
                ev.wait(dve, "r1", i)
                turn.get_before(dve, f"xa{LAST}", i)
                for t in range(TT):
                    ev.wait(dve, "norm", i, t + 1)
                    ev.up("norm2", dve.tensor_scalar(xs[:, t, :], xt[:, t, :], r1[:, t:t + 1], None, ALU.mult))

            def split(i):
                dense.get_before(dve, f"v{LAST}", i)
                for m in range(KT):
                    turn.wait_taken(dve, f"xn{m}", i)
                    ev.up("xnhi", dve.tensor_copy(xn_hl[0][:, m, :], xn[:, m, :]))
                    ev.wait(dve, "xnhi", i, m + 1)
                    ev.up("xnlo", dve.tensor_tensor(xn_hl[1][:, m, :], xn[:, m, :],
                                                    xn_hl[0][:, m, :].bitcast(F32), ALU.subtract))

            def weights(_):
                for n, (src, hi, lo) in enumerate(pieces):
                    dve.wait_ge(s_whi, n + 1)
                    dve.tensor_tensor(lo, src, hi.bitcast(F32), ALU.subtract).then_inc(s_wlo, 1)
                dve.wait_ge(s_small, 48)

            def body(i, ahead):
                ahead("norm")
                lg = dense.get(dve, "logit", i)[:, 0:TT * E].rearrange("p (t e) -> p t e", e=E)
                dense.take("logit", dve.tensor_tensor(logit, lg, bcast(b2_sb, 1, TT), ALU.add))
                dense.wait_taken(dve, "logit", i)
                ev.up("softmax", dve.tensor_reduce(top, logit, AX, ALU.max))
                ev.wait(dve, "softmax", i, 1)
                ev.up("softmax", dve.tensor_tensor(logit, logit, bcast(top, 2, E), ALU.subtract))
                ev.wait(dve, "exp", i)
                ev.up("softmax", dve.tensor_reduce(top, logit, AX, ALU.add))
                ev.wait(dve, "softmax", i, 3)
                ev.up("softmax", dve.reciprocal(top, top))
                ev.wait(dve, "softmax", i, 4)
                ev.up("alpha", dve.tensor_tensor(alpha.rearrange("p t (e r) -> p t e r", r=R), bcast(logit, 3, R),
                                                 bcast(bcast(top, 2, E), 3, R), ALU.mult))
                ahead("split")
                dense.get_before(dve, f"u{LAST}", i)
                for m in range(KT):
                    turn.wait_taken(dve, f"alpha{m}", i)
                    dense.take(f"v{m}", dve.tensor_tensor(vx[:, m, :], dense.get(dve, f"v{m}", i), alpha_b[:, m, :],
                                                          ALU.mult))
                    dense.wait_taken(dve, f"v{m}", i)
                    ev.up("vxhi", dve.tensor_copy(vx_hl[0][:, m, :], vx[:, m, :]))
                    ev.wait(dve, "vxhi", i, m + 1)
                    ev.up("vxlo", dve.tensor_tensor(vx_hl[1][:, m, :], vx[:, m, :],
                                                    vx_hl[0][:, m, :].bitcast(F32), ALU.subtract))

            loop_parts(dve, NB, {"weights": weights, "norm": norm, "split": split}, body)

        @block.scalar
        def _(act):
            def norm(i):
                act.preload_act_table_set(EXP_LN_SET)
                ev.wait(act, "mv", i)
                ev.up("rstd", act.activation(rstd, mv[:, :, 1], ACT.Ln, bias=eps))
                ev.wait(act, "rstd", i, 1)
                ev.up("rstd", act.activation(rstd, rstd, ACT.Exp, scale=-0.5))
                ev.wait(act, "m2", i)
                ev.up("r1", act.activation(r1, r1, ACT.Ln, bias=eps))
                ev.wait(act, "r1", i, 1)
                ev.up("r1", act.activation(r1, r1, ACT.Exp, scale=-0.5))

            def fill_xn(i):
                ev.wait_before(act, "xn_out", i)
                ev.wait_before(act, "xnlo", i)
                for m in range(KT):
                    turn.take(f"xn{m}", act.activation(xn[:, m, :], turn.get(act, f"xn{m}", i), ACT.Copy))

            def fill_xa(i):
                ev.wait_before(act, "xa_out", i)
                for m in range(KT):
                    turn.take(f"xa{m}", act.activation(xa[:, m, :], turn.get(act, f"xa{m}", i), ACT.Copy))

            def hidden(i):
                for m in range(KT):
                    dense.take(f"h{m}", act.activation(h1[:, m, :], dense.get(act, f"h{m}", i), ACT.Relu,
                                                       bias=b1_sb[:, m:m + 1]))

            def weights(_):
                act.wait_ge(s_small, 48)
                for n, (src, hi, lo) in enumerate(pieces):
                    if n < 2 * KT:
                        act.wait_ge(s_turned, n + 1)
                    elif n == 2 * KT:
                        act.wait_ge(s_w1, 16)
                    act.activation(hi, src, ACT.Copy).then_inc(s_whi, 1)

            def body(i, ahead):
                ahead("norm")
                ev.wait(act, "softmax", i, 2)
                ev.up("exp", act.activation(logit, logit, ACT.Exp))
                ahead("xn")
                act.preload_act_table_set(SILU_SET)
                ev.wait_before(act, "gate_out", i)
                for m in range(KT):
                    turn.take(f"alpha{m}", act.activation(alpha_b[:, m, :], turn.get(act, f"alpha{m}", i), ACT.Copy))
                ahead("xa")
                ahead("h")
                for m in range(KT):
                    dense.take(f"u{m}", act.activation(gate[:, m, :], dense.get(act, f"u{m}", i), ACT.Silu))
                dense.wait_taken(act, f"u{LAST}", i)
                ev.up_dma("gate_out", act.dma_start(row(gate_d, i).rearrange("o p m t -> p (o m) t"), gate))

            loop_parts(act, NB, {"weights": weights, "norm": norm, "xn": fill_xn, "xa": fill_xa, "h": hidden}, body)
            ev.wait(act, "gate_out", NB - 1)

        @block.tensor
        def _(pe):
            def turn_weights():
                for s_in, need, src, first in ((s_v, 16, v_in, 0), (s_u, 16 * KT, u_in, KT)):
                    pe.wait_ge(s_in, need)
                    for m in range(KT):
                        for k in range(KT):
                            ins = pe.transpose(psum[first + m][:, k * P:(k + 1) * P], src[:, k, m * P:(m + 1) * P],
                                               ident)
                        ins.then_inc(s_turned, 1)
                pe.wait_ge(s_wlo, len(pieces))

            def turn_row(i, name, src, done):
                ev.wait(pe, done, i)
                for m in range(KT):
                    ps = turn.open(pe, f"{name}{m}", i)
                    for t in range(TT):
                        ins = pe.transpose(ps[:, t * P:(t + 1) * P], src[:, t, m * P:(m + 1) * P], ident)
                    turn.complete(f"{name}{m}", ins)

            def linear(i, name, w, src, m, split=None):
                ps = dense.open(pe, f"{name}{m}", i)
                for k in range(KT):
                    if m == 0 and split:
                        ev.wait(pe, split, i, k + 1)
                    wh, wl = (a[:, k, m * P:(m + 1) * P] for a in w)
                    sh, sl = (a[:, k, :] for a in src)
                    pe.matmul(ps, wh, sh, start=k == 0, stop=False)
                    pe.matmul(ps, wh, sl, start=False, stop=False)
                    ins = pe.matmul(ps, wl, sh, start=False, stop=k == LAST)
                dense.complete(f"{name}{m}", ins)

            def hidden(i):
                for m in range(KT):
                    linear(i, "h", w1, xn_hl, m, "xnlo")

            def body(i, ahead):
                dense.wait_taken(pe, f"h{LAST}", i)
                ps = dense.open(pe, "logit", i)
                for t in range(TT):
                    for k in range(KT):
                        ins = pe.matmul(ps[:, t * E:(t + 1) * E], h1[:, k, t * P:(t + 1) * P], w2[:, k, :],
                                        start=k == 0, stop=k == KT - 1)
                dense.complete("logit", ins)
                for m in range(KT):
                    linear(i, "v", vt, xn_hl, m)
                    if m == 1:
                        ahead("xn")
                ev.wait(pe, "alpha", i)
                for m in range(KT):
                    ps = turn.open(pe, f"alpha{m}", i)
                    for t in range(TT):
                        ins = pe.transpose(ps[:, t * P:(t + 1) * P], alpha[:, t, m * P:(m + 1) * P], ident)
                    turn.complete(f"alpha{m}", ins)
                ahead("xa")
                ahead("h")
                for m in range(KT):
                    linear(i, "u", ut, vx_hl, m, "vxlo")

            parts = {"xn": lambda i: turn_row(i, "xn", xt, "norm"), "xa": lambda i: turn_row(i, "xa", xs, "norm2"),
                     "h": hidden}

            def before(part):
                if part == "xa":
                    turn.skip(pe, alphas, -1)
                if part in ("h", "body"):
                    dense.skip(pe, {"h": ["logit"] + vs, "body": us}[part], -1)

            def skip(part):
                slots, results = {"xn": (turn, xn_parts), "xa": (turn, xa_parts), "h": (dense, hs)}[part]
                slots.skip(pe, results, NB)

            turn_weights()
            loop_parts(pe, NB, parts, body, before=before, skip=skip)


def phase_a(nc, consts, w, xn_d, xa_d, xmid_d):
    ident, hmask, causal, avg32, _, chunk_start, eps = consts
    NB, _, KT, T = xn_d.shape
    D = KT * P
    KD = w["wkg2"].shape[1]
    GR = KD // P
    NC = T // P
    KH, VH = 16, 32
    HG = P // KH
    QD = D // P
    HQ = P // VH
    H64, H32 = P // 2, P // 4
    ctx = ExitStack()
    with ctx:
        def sb(name, shape, dt=F32):
            return ctx.enter_context(nc.sbuf_tensor("a_" + name, shape, dt))[:]

        def pair(name, shape):
            return [sb(name + part, shape, F32R) for part in ("hi", "lo")]

        wkg1, wq, wk, wv, wg, wo = (w[name] for name in ("wkg1", "wq", "wk", "wv", "wg", "wo"))
        wkg2, bkg2_sb, bg_sb = w["wkg2"], w["bkg2"], w["bg"]
        xa = sb("xa", [P, KT, T])
        k_sb = xa[:, 0:GR, :].rearrange("p g (c t) -> p (g c) t", t=P)
        q_sb = xa[:, GR:2 * GR, :].rearrange("p g (c t) -> p (g c) t", t=P)
        xn = sb("xn", [P, KT, T])
        xa_hl = pair("xa", [P, KT, T])
        u = sb("u", [P, T])
        shape = [P, GR * NC, P]
        neg, soft, cum = sb("neg", shape), sb("soft", shape), sb("cum", shape)
        lv64, lv32, dq, dk = sb("lv64", shape), sb("lv32", shape), sb("dq", shape), sb("dk", shape)
        khat, qhat = soft, neg
        decay = sb("decay", [P, GR * NC])
        v_tok = sb("v_tok", [P, NC, D])
        gsilu = sb("gsilu", [P, KT, T])
        qx64 = [sb(f"qx64_{g}", [P, HG, H64]) for g in range(GR)]
        qx32 = [sb(f"qx32_{g}", [P, 2, HG, H32]) for g in range(GR)]
        qxd = [sb(f"qxd_{g}", [P, 4, HG, H32]) for g in range(GR)]
        a_sb = [sb(f"a{g}", [P, 2, HG, H64]) for g in range(GR)]
        kt_sb = sb("kt", [P, GR, P])
        state = [sb(f"state{n}", [P, GR, HG * VH]) for n in range(2)]
        sq, oc, rn = sb("sq", [P, QD, P]), sb("oc", [P, QD, P]), sb("rn", [P, QD, P])
        og_hl = pair("og", [P, KT, T])
        psum = [ctx.enter_context(nc.psum_tensor(f"a_ps{b}", [P, 512], F32))[:] for b in range(4)]
        ps_att = [ctx.enter_context(nc.psum_tensor(f"a_att{g}", [P, 2, HG, H64], F32))[:] for g in range(2)]

        with nc.Block() as block:
            @block.vector
            def _(dve):
                for ps in ps_att:
                    for half in range(2):
                        dve.memset(ps[:, half], 0.0)

        ev = Events(nc, ctx, "a")
        for name, per in (("xa_in", 16), ("xn_in", 16), ("xmid_out", 16), ("xahi", KT), ("xalo", KT), ("absz", GR),
                          ("expz", GR), ("softz", GR), ("negz", GR), ("logg", GR), ("cum", GR), ("offs", 3),
                          ("offk", 1), ("e64", 2), ("e32", 2), ("edk", 1), ("edq", 1), ("ekh", 1), ("eqh", 1),
                          ("decay", 1), ("m64", 2), ("m32", 2), ("mdk", 1), ("mdq", 1), ("mkh", 1), ("mqh", 1),
                          ("qxs", 2 * GR * NC), ("qxd", GR * NC), ("state", GR * (NC - 2)),
                          ("sq", NC), ("rn", NC), ("og", 2 * NC), ("oghi", NC), ("oglo", NC)):
            ev.add(name, per)
        dense = Slots(ev, "dense", psum[0:3], ["u"] + [f"z{g}" for g in range(GR)] + [f"k{g}" for g in range(GR)]
                      + [f"q{g}" for g in range(GR)] + [f"v{c}" for c in range(NC)] + [f"g{m}" for m in range(KT)]
                      + ["kt0", "ds0", "kt1", "ds1", "var0", "kt2", "ds2", "var1", "var2", "var3"]
                      + [f"o{m}" for m in range(KT)])
        att = Slots(ev, "att", ps_att, [f"{c}_{g}" for c in range(NC) for g in range(GR)])
        mix = Slots(ev, "mix", psum[3:4], list(range(NC)))
        LAST = KT - 1
        gc_all = range(GR * NC)
        block = ctx.enter_context(nc.Block())

        def tokens(c):
            return slice(c * P, (c + 1) * P)

        @block.sync
        def _(sp):
            ev.give_credits(sp)

            def load(i):
                ev.wait_before(sp, "mdq", i)
                ev.wait_before(sp, "mqh", i)
                ev.up_dma("xa_in", sp.dma_start(xa, row(xa_d, i).rearrange("o p m t -> p (o m) t")))

            def body(i, ahead):
                ev.wait_before(sp, "xmid_out", i)
                ev.up_dma("xn_in", sp.dma_start(xn, row(xn_d, i).rearrange("o p m t -> p (o m) t")))
                ahead()
                dense.wait_taken(sp, f"o{LAST}", i)
                ev.up_dma("xmid_out", sp.dma_start(row(xmid_d, i).rearrange("o p m t -> p (o m) t"), xn))

            loop(sp, NB, load, body)
            ev.wait(sp, "xmid_out", NB - 1)

        @block.vector
        def _(dve):
            def split(i):
                ev.wait(dve, "xa_in", i)
                dense.get_before(dve, f"g{LAST}", i)
                for m in range(KT):
                    ev.up("xahi", dve.tensor_copy(xa_hl[0][:, m, :], xa[:, m, :]))
                for m in range(KT):
                    ev.wait(dve, "xahi", i, m + 1)
                    ev.up("xalo", dve.tensor_tensor(xa_hl[1][:, m, :], xa[:, m, :],
                                                    xa_hl[0][:, m, :].bitcast(F32), ALU.subtract))

            def spread_d(i, c, g):
                gc = g * NC + c
                q = dq[:, gc, :].rearrange("p (b t) -> p b t", t=H32)
                ev.up("qxd", dve.tensor_tensor(qxd[g], bcast(q, 2, HG), bcast(bcast(hmask, 1, 4), 3, H32), ALU.mult))

            def body(i, ahead):
                dense.take("u", dve.tensor_copy(u, dense.get(dve, "u", i)))
                for g in range(GR):
                    ev.wait(dve, "absz", i, g + 1)
                    ng = neg[:, g * NC:(g + 1) * NC, :].rearrange("p c t -> p (c t)")
                    cg = cum[:, g * NC:(g + 1) * NC, :].rearrange("p c t -> p (c t)")
                    sg = soft[:, g * NC:(g + 1) * NC, :].rearrange("p c t -> p (c t)")
                    dense.take(f"z{g}", dve.tensor_scalar(ng, dense.get(dve, f"z{g}", i), bkg2_sb[:, g:g + 1], 0.0,
                                                          ALU.add, ALU.min))
                    dense.wait_taken(dve, f"z{g}", i)
                    ev.wait(dve, "softz", i, g + 1)
                    ev.up("logg", dve.tensor_tensor(ng, ng, sg, ALU.subtract))
                    ev.wait(dve, "logg", i, g + 1)
                    ev.up("cum", dve.tensor_tensor_scan(cg, chunk_start, ng, 0.0, ALU.mult, ALU.add))
                ev.wait(dve, "cum", i)
                for dst, n, ref in ((lv64, P, H64 - 1), (lv32, H64, H32 - 1), (dq, H32, H32 // 2 - 1)):
                    cv = flat(cum).rearrange("p (b t) -> p b t", t=n)
                    dv = flat(dst).rearrange("p (b t) -> p b t", t=n)
                    at = cv[:, :, ref]
                    ev.up("offs", dve.tensor_tensor(dv, cv, bcast(at, 2, n), ALU.subtract))
                dense.wait_taken(dve, f"q{GR - 1}", i)
                for name, buf, n in (("64", lv64, P), ("32", lv32, H64)):
                    for part, src in ((0, k_sb), (1, q_sb)):
                        b = flat(buf).rearrange("p (b a t) -> p b a t", a=2, t=n // 2)[:, :, part, :]
                        s = flat(src).rearrange("p (b a t) -> p b a t", a=2, t=n // 2)[:, :, part, :]
                        ev.wait(dve, "e" + name, i, part + 1)
                        ev.up("m" + name, dve.tensor_tensor(b, b, s, ALU.mult))
                ev.wait(dve, "edk", i)
                ev.up("mdk", dve.tensor_tensor(dk, dk, k_sb, ALU.mult))
                ev.wait(dve, "edq", i)
                ev.up("mdq", dve.tensor_tensor(dq, dq, q_sb, ALU.mult))
                ev.wait(dve, "mdq", i)
                for g in range(GR):
                    spread_d(i, 0, g)
                for c in range(NC):
                    if c > 0:
                        mix.get(dve, c - 1, i)
                    for g in range(GR):
                        ps = att.get(dve, f"{c}_{g}", i)
                        cz = causal.rearrange("p (a t) -> p a t", a=2)
                        att.take(f"{c}_{g}", dve.tensor_tensor(a_sb[g], ps, bcast(cz, 2, HG), ALU.mult))
                        if c + 1 < NC:
                            spread_d(i, c + 1, g)
                    if c + 1 < NC:
                        new, old = state[(c + 1) % 2], state[c % 2]
                        ds = dense.get(dve, f"ds{c}", i).rearrange("p (g h v) -> p g h v", g=GR, v=VH)
                        dense.take(f"ds{c}", dve.tensor_tensor(new.rearrange("p g (h v) -> p g h v", v=VH), ds,
                                                               bcast(bcast(hmask, 1, GR), 3, VH), ALU.mult))
                        dense.wait_taken(dve, f"ds{c}", i)
                        if c > 0:
                            ev.wait(dve, "decay", i)
                            for g in range(GR):
                                gc = g * NC + c
                                ev.up("state", dve.scalar_tensor_tensor(new[:, g, :], old[:, g, :],
                                                                        decay[:, gc:gc + 1], new[:, g, :],
                                                                        ALU.mult, ALU.add))
                            ev.wait(dve, "state", i, GR * c)
                    if c > 0:
                        gated(i, c - 1)
                gated(i, NC - 1)
                ahead()
                ev.wait(dve, "xn_in", i)
                for m in range(KT):
                    dense.take(f"o{m}", dve.tensor_tensor(xn[:, m, :], dense.get(dve, f"o{m}", i), xn[:, m, :],
                                                          ALU.add))

            def gated(i, c):
                ev.wait(dve, "rn", i, c + 1)
                ev.up("og", dve.tensor_tensor(rn, rn, oc, ALU.mult))
                dense.wait_taken(dve, f"g{LAST}", i)
                ev.wait(dve, "og", i, 2 * c + 1)
                ev.up("og", dve.tensor_tensor(rn, rn, gsilu[:, :, tokens(c)], ALU.mult))
                ev.wait(dve, "og", i, 2 * c + 2)
                ev.up("oghi", dve.tensor_copy(og_hl[0][:, :, tokens(c)], rn))
                ev.wait(dve, "oghi", i, c + 1)
                ev.up("oglo", dve.tensor_tensor(og_hl[1][:, :, tokens(c)], rn,
                                                og_hl[0][:, :, tokens(c)].bitcast(F32), ALU.subtract))

            loop(dve, NB, split, body)

        @block.gpsimd
        def _(pool):
            def spread(i, c, g):
                gc = g * NC + c
                ev.up("qxs", pool.tensor_tensor(qx64[g], bcast(lv64[:, gc, H64:P], 1, HG), bcast(hmask, 2, H64),
                                                ALU.mult))
                q = lv32[:, gc, :].rearrange("p (b a t) -> p b a t", a=2, t=H32)[:, :, 1, :]
                ev.up("qxs", pool.tensor_tensor(qx32[g], bcast(q, 2, HG), bcast(bcast(hmask, 1, 2), 3, H32),
                                                ALU.mult))

            def body(i, ahead):
                ev.wait(pool, "cum", i)
                ev.up("offk", pool.tensor_tensor(khat, cum, bcast(cum[:, :, P - 1], 2, P), ALU.subtract))
                ev.wait(pool, "m64", i)
                ev.wait(pool, "m32", i)
                for g in range(GR):
                    spread(i, 0, g)
                dense.wait_taken(pool, f"q{GR - 1}", i)
                ev.wait(pool, "ekh", i)
                ev.up("mkh", pool.tensor_tensor(khat, khat, k_sb, ALU.mult))
                ev.wait(pool, "eqh", i)
                ev.up("mqh", pool.tensor_tensor(qhat, qhat, q_sb, ALU.mult))
                for c in range(1, NC):
                    for g in range(GR):
                        att.get(pool, f"{c - 1}_{g}", i)
                        spread(i, c, g)

            loop(pool, NB, nothing, body)

        @block.scalar
        def _(act):
            def half(buf, n, part):
                return flat(buf).rearrange("p (b a t) -> p b a t", a=2, t=n // 2)[:, :, part, :]

            def body(i, ahead):
                act.preload_act_table_set(EXP_LN_SET)
                for g in range(GR):
                    s = soft[:, g * NC:(g + 1) * NC, :].rearrange("p c t -> p (c t)")
                    ps = dense.get(act, f"z{g}", i)
                    ev.up("absz", act.activation(s, ps, ACT.Abs, bias=bkg2_sb[:, g:g + 1]))
                for g in range(GR):
                    s = soft[:, g * NC:(g + 1) * NC, :].rearrange("p c t -> p (c t)")
                    ev.wait(act, "absz", i, g + 1)
                    ev.up("expz", act.activation(s, s, ACT.Exp, scale=-1.0))
                    ev.wait(act, "expz", i, g + 1)
                    ev.up("softz", act.activation(s, s, ACT.Ln, bias=1.0))
                for g in range(GR):
                    rows = slice(g * NC, (g + 1) * NC)
                    dense.take(f"k{g}", act.activation(k_sb[:, rows, :].rearrange("p c t -> p (c t)"),
                                                       dense.get(act, f"k{g}", i), ACT.Copy, scale=VH ** -0.5))
                for g in range(GR):
                    rows = slice(g * NC, (g + 1) * NC)
                    dense.take(f"q{g}", act.activation(q_sb[:, rows, :].rearrange("p c t -> p (c t)"),
                                                       dense.get(act, f"q{g}", i), ACT.Copy))

                def value(c):
                    dense.take(f"v{c}", act.activation(v_tok[:, c, :], dense.get(act, f"v{c}", i), ACT.Copy))

                for n, (name, buf, length) in enumerate((("e64", lv64, P), ("e32", lv32, H64))):
                    ev.wait(act, "offs", i, n + 1)
                    for part, sign in ((0, -1), (1, 1)):
                        b = half(buf, length, part)
                        ev.up(name, act.activation(b, b, ACT.Exp, scale=sign * GATE_SCALE))
                    value(n)
                ev.wait(act, "offs", i, 3)
                ev.up("edk", act.activation(dk, dq, ACT.Exp, scale=-GATE_SCALE))
                ev.wait(act, "edk", i)
                ev.up("edq", act.activation(dq, dq, ACT.Exp, scale=GATE_SCALE))
                value(2)
                ev.wait(act, "offk", i)
                ev.up("ekh", act.activation(khat, khat, ACT.Exp, scale=-GATE_SCALE))
                value(3)
                ev.up("eqh", act.activation(qhat, cum, ACT.Exp, scale=GATE_SCALE))
                ev.up("decay", act.activation(decay, cum[:, :, P - 1], ACT.Exp, scale=GATE_SCALE))
                act.preload_act_table_set(SILU_SET)
                for m in range(KT):
                    dense.take(f"g{m}", act.activation(gsilu[:, m, :], dense.get(act, f"g{m}", i), ACT.Silu,
                                                       bias=bg_sb[:, m:m + 1]))
                act.preload_act_table_set(EXP_LN_SET)
                for c in range(NC):
                    if c + 1 < NC:
                        dense.take(f"kt{c}", act.activation(flat(kt_sb), dense.get(act, f"kt{c}", i)[:, 0:GR * P],
                                                            ACT.Copy))
                    if c > 0:
                        inverse_deviation(i, c - 1)
                    ps = mix.get(act, c, i)
                    ev.up("sq", act.activation(flat(sq), ps, ACT.Square))
                    if c > 0:
                        ev.wait(act, "og", i, 2 * (c - 1) + 1)
                    mix.take(c, act.activation(flat(oc), ps, ACT.Copy))
                inverse_deviation(i, NC - 1)

            def inverse_deviation(i, c):
                ps = dense.get(act, f"var{c}", i)
                if c > 0:
                    ev.wait(act, "oglo", i, c)
                dense.take(f"var{c}", act.activation(flat(rn), ps, ACT.Ln, bias=eps))
                dense.wait_taken(act, f"var{c}", i)
                ev.up("rn", act.activation(rn, rn, ACT.Exp, scale=-0.5))

            loop(act, NB, nothing, body)

        @block.tensor
        def _(pe):
            def linear(i, name, w, src, m):
                ps = dense.open(pe, f"{name}{m}", i)
                dense.complete(f"{name}{m}", product3(pe, ps, [
                    (tuple(a[:, k, m * P:(m + 1) * P] for a in w), tuple(a[:, k, :] for a in src)) for k in range(KT)]))

            def weights(i, c, g):
                gc = g * NC + c
                ps = att.open(pe, f"{c}_{g}", i)
                ev.wait(pe, "m64", i)
                ev.wait(pe, "m32", i)
                ev.wait(pe, "mdk", i)
                ev.wait(pe, "qxs", i, 2 * (GR * c + g) + 2)
                ev.wait(pe, "qxd", i, GR * c + g + 1)

                def block_product(s, half, at, n, keys, q):
                    return pe.matmul(ps[s:s + H32, half, :, at:at + n], keys[:, gc, s:s + H32], q, start=True,
                                     stop=True, tile_position=(0, s))

                for s in (0, H32):
                    block_product(s, 1, 0, H64, lv64, qx64[g])
                for b in range(2):
                    block_product(H64 * b, b, H32, H32, lv32, qx32[g][:, b])
                for b in range(4):
                    ins = block_product(H32 * b, b // 2, H32 * (b % 2), H32, dk, qxd[g][:, b])
                att.complete(f"{c}_{g}", ins)

            def variance(i, c):
                ev.wait(pe, "sq", i, c + 1)
                ps = dense.open(pe, f"var{c}", i)
                dense.complete(f"var{c}", pe.matmul(ps, avg32, flat(sq), start=True, stop=True))

            def body(i, ahead):
                ev.wait(pe, "xalo", i)
                ps = dense.open(pe, "u", i)
                dense.complete("u", product3(pe, ps, [
                    (tuple(a[:, k, :] for a in wkg1), tuple(a[:, k, :] for a in xa_hl)) for k in range(KT)]))
                dense.wait_taken(pe, "u", i)
                for g in range(GR):
                    ps = dense.open(pe, f"z{g}", i)
                    dense.complete(f"z{g}", pe.matmul(ps, wkg2[:, g * P:(g + 1) * P], u, start=True, stop=True))
                for g in range(GR):
                    linear(i, "k", wk, xa_hl, g)
                for g in range(GR):
                    linear(i, "q", wq, xa_hl, g)
                for c in range(NC):
                    ps = dense.open(pe, f"v{c}", i)
                    dense.complete(f"v{c}", product3(pe, ps, [
                        (tuple(a[:, k, tokens(c)] for a in xa_hl), tuple(a[:, k, :] for a in wv)) for k in range(KT)]))
                for m in range(KT):
                    linear(i, "g", wg, xa_hl, m)
                for g in range(GR):
                    weights(i, 0, g)
                for c in range(NC):
                    gcs = [g * NC + c for g in range(GR)]
                    if c + 1 < NC:
                        ev.wait(pe, "mkh", i)
                        ps = dense.open(pe, f"kt{c}", i)
                        for g in range(GR):
                            ins = pe.transpose(ps[:, g * P:(g + 1) * P], khat[:, gcs[g], :], ident)
                        dense.complete(f"kt{c}", ins)
                        for g in range(GR):
                            weights(i, c + 1, g)
                        dense.wait_taken(pe, f"kt{c}", i)
                        ps = dense.open(pe, f"ds{c}", i)
                        for g in range(GR):
                            n = HG * VH
                            ins = pe.matmul(ps[:, g * n:(g + 1) * n], kt_sb[:, g, :], v_tok[:, c, g * n:(g + 1) * n],
                                            start=True, stop=True)
                        dense.complete(f"ds{c}", ins)
                    if c > 0:
                        variance(i, c - 1)
                    ps = mix.open(pe, c, i).rearrange("p (q t) -> p q t", t=P)
                    for g in range(GR):
                        att.wait_taken(pe, f"{c}_{g}", i)
                    if c > 0:
                        ev.wait(pe, "mqh", i)
                    if c == 1:
                        dense.wait_taken(pe, "ds0", i)
                    if c > 1:
                        ev.wait(pe, "state", i, GR * (c - 1))
                    for quad in range(QD):
                        g, first_head = quad * HQ // HG, quad * HQ % HG
                        if c > 0:
                            pe.matmul(ps[:, quad, :], state[c % 2][:, g, first_head * VH:(first_head + HQ) * VH],
                                      qhat[:, gcs[g], :], start=True, stop=True, skip_group_check=True)
                        for j in range(HQ):
                            h = quad * HQ + j
                            ins = pe.matmul(ps[VH * j:VH * (j + 1), quad, :], v_tok[:, c, VH * h:VH * (h + 1)],
                                            a_sb[g][:, :, first_head + j, :], start=c == 0, stop=True,
                                            tile_position=(0, VH * j), skip_group_check=c > 0)
                    mix.complete(c, ins)
                variance(i, NC - 1)
                ahead()
                ev.wait(pe, "oglo", i)
                for m in range(KT):
                    linear(i, "o", wo, og_hl, m)

            loop(pe, NB, nothing, body)


def phase_m(nc, consts, x, xmid_d, gate_d, W1, W3, W2, ln2_w, out):
    ident, avg_all, eps = consts[0], consts[4], consts[-1]
    NB, _, KT, T = xmid_d.shape
    D, F = W1.shape
    FT = F // P
    TT = T // P
    AHEAD = 2
    STAGES = 4
    ctx = ExitStack()
    with ctx:
        def sb(name, shape, dt=F32):
            return ctx.enter_context(nc.sbuf_tensor("m_" + name, shape, dt))[:]

        def pair(name, shape):
            return [sb(name + part, shape, F32R) for part in ("hi", "lo")]

        w1, w3 = pair("w1", [P, KT, F]), pair("w3", [P, KT, F])
        w2 = pair("w2", [P, FT, D])
        ln2 = sb("ln2", [P, KT])
        xm, xres = sb("xm", [P, KT, T]), sb("xres", [P, KT, T])
        stage = [xres[:, n, :].rearrange("p (m n) -> p m n", n=P) for n in range(STAGES)]
        xs_hl = pair("xs", [P, KT, T])
        sq, r2 = [sb(f"sq{n}", [P, T]) for n in range(2)], sb("r2", [P, T])
        gate, xt = sb("gate", [P, KT, T]), sb("xt", [P, TT, D])
        silu, h = [sb(f"silu{n}", [P, T]) for n in range(2)], [sb(f"h{n}", [P, T]) for n in range(2)]
        h_hl = [pair(f"h{n}", [P, T]) for n in range(2)]
        psum = [ctx.enter_context(nc.psum_tensor(f"m_ps{b}", [P, 512], F32))[:] for b in range(8)]

        ev = Events(nc, ctx, "m")
        for name, per in (("xm_in", 16), ("xres_in", 16), ("gate_in", 16), ("x_in", 16), ("out_out", 16), ("sq", KT),
                          ("sqdone", KT - 1), ("r2", 1), ("xs", KT), ("xshi", KT), ("xslo", KT), ("hhi", FT),
                          ("hlo", FT), ("w2", FT - 1), ("y", KT)):
            ev.add(name, per)
        mean = Slots(ev, "mean", psum[0:1], ["ms"])
        early = [f"{ab}{j}" for j in range(AHEAD) for ab in "ab"]
        late = [f"{ab}{j}" for j in range(AHEAD, FT) for ab in "ab"]
        turned = [f"t{t}" for t in range(TT)]
        dense = Slots(ev, "dense", psum[1:4], late + early + turned, early)
        acc = Slots(ev, "acc", psum[4:8], list(range(KT)))

        jobs = []
        for j in range(FT):
            cols = slice(j * P, (j + 1) * P)
            for w, parts in ((W1, w1), (W3, w3)):
                jobs.append((w[:, cols].rearrange("(kt p) n -> p kt n", p=P), ln2, *(a[:, :, cols] for a in parts)))
            jobs.append((W2[j * P:(j + 1) * P, :].rearrange("p (m n) -> p m n", n=P), None,
                         *(a[:, j, :].rearrange("p (m n) -> p m n", n=P) for a in w2)))
        s_ln2 = ctx.enter_context(nc.semaphore("m_ln2"))
        s_load = [ctx.enter_context(nc.semaphore(f"m_wload{n}")) for n in range(STAGES)]
        s_scaled, s_whi, s_wlo = (ctx.enter_context(nc.semaphore(f"m_w{n}")) for n in ("scaled", "hi", "lo"))
        block = ctx.enter_context(nc.Block())

        def scaled_so_far(n):
            return sum(scale is not None for _, scale, _, _ in jobs[:n + 1])

        @block.sync
        def _(sp):
            ev.give_credits(sp)
            sp.dma_start(ln2, ln2_w.rearrange("(m p) -> p m", p=P), allow_slow_non_contiguous=True).then_inc(s_ln2, 16)

            def load(i):
                ev.wait_before(sp, "xslo", i)
                ev.up_dma("xm_in", sp.dma_start(xm, row(xmid_d, i).rearrange("o p m t -> p (o m) t")))

            def weights(first, end):
                for n in range(first, end):
                    src = jobs[n][0]
                    if n >= STAGES:
                        sp.wait_ge(s_wlo, n - STAGES + 1)
                    sp.dma_start(stage[n % STAGES], src).then_inc(s_load[n % STAGES], 16)

            def body(i, ahead):
                ahead("xm")
                if isinstance(i, int) and i == 0:
                    weights(STAGES, len(jobs))
                sp.wait_ge(s_wlo, len(jobs))
                ev.wait_before(sp, "y", i)
                ev.up_dma("xres_in", sp.dma_start(xres, row(xmid_d, i).rearrange("o p m t -> p (o m) t")))
                dense.get_before(sp, f"t{TT - 1}", i)
                ev.up_dma("gate_in", sp.dma_start(gate, row(gate_d, i).rearrange("o p m t -> p (o m) t")))
                ev.wait_before(sp, "out_out", i)
                ev.up_dma("x_in", sp.dma_start(xt, row(x, i).rearrange("o (tt p) d -> p (o tt) d", p=P)))
                dense.wait_taken(sp, f"t{TT - 1}", i)
                ev.up_dma("out_out", sp.dma_start(row(out, i).rearrange("o (tt p) d -> p (o tt) d", p=P), xt))

            weights(0, STAGES)
            loop_parts(sp, NB, {"xm": load}, body, peel=True)
            ev.wait(sp, "out_out", NB - 1)

        @block.vector
        def _(dve):
            def weights(j):
                if j >= FT:
                    return
                for n in range(3 * j, 3 * j + 3):
                    _, scale, hi, lo = jobs[n]
                    if scale is not None:
                        dve.wait_ge(s_load[n % STAGES], 16 * (n // STAGES + 1))
                        dve.tensor_tensor(stage[n % STAGES], stage[n % STAGES], bcast(scale, 2, P),
                                          ALU.mult).then_inc(s_scaled, 1)
                for n in range(3 * j, 3 * j + 3):
                    _, scale, hi, lo = jobs[n]
                    dve.wait_ge(s_whi, n + 1)
                    dve.tensor_tensor(lo, stage[n % STAGES], hi.bitcast(F32), ALU.subtract).then_inc(s_wlo, 1)

            def scale(i):
                ev.wait(dve, "r2", i)
                for m in range(KT):
                    ev.up("xs", dve.tensor_tensor(xm[:, m, :], xm[:, m, :], r2, ALU.mult))

            def split(i):
                dense.get_before(dve, f"b{FT - 1}", i)
                for m in range(KT):
                    ev.wait(dve, "xs", i, m + 1)
                    ev.up("xshi", dve.tensor_copy(xs_hl[0][:, m, :], xm[:, m, :]))
                for m in range(KT):
                    ev.wait(dve, "xshi", i, m + 1)
                    ev.up("xslo", dve.tensor_tensor(xs_hl[1][:, m, :], xm[:, m, :],
                                                    xs_hl[0][:, m, :].bitcast(F32), ALU.subtract))

            def hidden(i, j):
                n = j % 2
                dense.wait_taken(dve, f"a{j}", i)
                dense.take(f"b{j}", dve.tensor_tensor(h[n], dense.get(dve, f"b{j}", i), silu[n], ALU.mult))
                ev.wait(dve, "hhi", i, j + 1)
                ev.up("hlo", dve.tensor_tensor(h_hl[n][1], h[n], h_hl[n][0].bitcast(F32), ALU.subtract))

            def first_hidden(i):
                for j in range(AHEAD):
                    hidden(i, j)

            def body(i, ahead):
                first = isinstance(i, int) and i == 0
                for j in range(AHEAD, FT):
                    if first:
                        weights(j + 1)
                    hidden(i, j)
                    if j == FT - 2:
                        ahead("scale")
                ahead("split")
                ev.wait(dve, "gate_in", i)
                ev.wait(dve, "xres_in", i)
                for m in range(KT):
                    acc.take(m, dve.tensor_tensor(xres[:, m, :], acc.get(dve, m, i), xres[:, m, :], ALU.add))
                for m in range(KT):
                    acc.wait_taken(dve, m, i)
                    ev.up("y", dve.tensor_tensor(gate[:, m, :], xres[:, m, :], gate[:, m, :], ALU.mult))
                ahead("hidden")
                ev.wait(dve, "x_in", i)
                for t in range(TT):
                    dense.take(f"t{t}", dve.tensor_tensor(xt[:, t, :], dense.get(dve, f"t{t}", i), xt[:, t, :],
                                                          ALU.add))

            def first_weights(_):
                dve.wait_ge(s_ln2, 16)
                for j in range(AHEAD + 1):
                    weights(j)

            parts = {"scale": scale, "split": split, "weights": first_weights, "hidden": first_hidden}
            loop_parts(dve, NB, parts, body, peel=True)

        @block.scalar
        def _(act):
            def weights(j):
                if j >= FT:
                    return
                for n in range(3 * j, 3 * j + 3):
                    _, scale, hi, _ = jobs[n]
                    if scale is not None:
                        act.wait_ge(s_scaled, scaled_so_far(n))
                    else:
                        act.wait_ge(s_load[n % STAGES], 16 * (n // STAGES + 1))
                    act.activation(hi, stage[n % STAGES], ACT.Copy).then_inc(s_whi, 1)

            def rms(i):
                act.preload_act_table_set(EXP_LN_SET)
                ev.wait(act, "xm_in", i)
                for m in range(KT):
                    if m >= 2:
                        ev.wait(act, "sqdone", i, m - 1)
                    ev.up("sq", act.activation(sq[m % 2], xm[:, m, :], ACT.Square))
                mean.take("ms", act.activation(r2, mean.get(act, "ms", i), ACT.Ln, bias=eps))
                mean.wait_taken(act, "ms", i)
                ev.up("r2", act.activation(r2, r2, ACT.Exp, scale=-0.5))
                act.preload_act_table_set(SILU_SET)

            def silu_part(i, j):
                n = j % 2
                if j >= 2:
                    dense.wait_taken(act, f"b{j - 2}", i)
                else:
                    dense.wait_taken_before(act, f"b{FT - 1}", i)
                dense.take(f"a{j}", act.activation(silu[n], dense.get(act, f"a{j}", i), ACT.Silu))

            def hi_part(i, j):
                n = j % 2
                dense.wait_taken(act, f"b{j}", i)
                if j >= 2:
                    ev.wait(act, "w2", i, j - 1)
                else:
                    acc.get_before(act, KT - 1, i)
                ev.up("hhi", act.activation(h_hl[n][0], h[n], ACT.Copy))

            def first_hidden(i):
                for j in range(AHEAD):
                    silu_part(i, j)
                for j in range(AHEAD):
                    hi_part(i, j)

            def body(i, ahead):
                first = isinstance(i, int) and i == 0
                for j in range(AHEAD, FT):
                    if first:
                        weights(j + 1)
                    silu_part(i, j)
                    hi_part(i, j)
                    if j == FT - 4:
                        ahead("rms")
                ahead("hidden")

            def first_weights(_):
                for j in range(AHEAD + 1):
                    weights(j)

            loop_parts(act, NB, {"rms": rms, "weights": first_weights, "hidden": first_hidden}, body, peel=True)

        @block.tensor
        def _(pe):
            def mean_square(i):
                ps = mean.open(pe, "ms", i)
                for m in range(KT):
                    ev.wait(pe, "sq", i, m + 1)
                    ins = pe.matmul(ps, avg_all, sq[m % 2], start=m == 0, stop=m == KT - 1)
                    if m < KT - 1:
                        ev.up("sqdone", ins)
                mean.complete("ms", ins)

            def up(i, j):
                for n, (ab, w) in enumerate((("a", w1), ("b", w3))):
                    pe.wait_ge(s_wlo, 3 * j + n + 1)
                    ps = dense.open(pe, f"{ab}{j}", i)
                    for k in range(KT):
                        if j == 0 and n == 0:
                            ev.wait(pe, "xslo", i, k + 1)
                        wh, wl = (a[:, k, j * P:(j + 1) * P] for a in w)
                        xh, xl = (a[:, k, :] for a in xs_hl)
                        pe.matmul(ps, wh, xh, start=k == 0, stop=False)
                        pe.matmul(ps, wh, xl, start=False, stop=False)
                        ins = pe.matmul(ps, wl, xh, start=False, stop=k == KT - 1)
                    dense.complete(f"{ab}{j}", ins)

            def down(i, j):
                ev.wait(pe, "hlo", i, j + 1)
                pe.wait_ge(s_wlo, 3 * j + 3)
                n = j % 2
                for m in range(KT):
                    ps = acc.open(pe, m, i) if j == 0 else acc.regions[m]
                    lh, ll = (w[:, j, m * P:(m + 1) * P] for w in w2)
                    rh, rl = h_hl[n]
                    pe.matmul(ps, lh, rh, start=j == 0, stop=False)
                    pe.matmul(ps, lh, rl, start=False, stop=False)
                    ins = pe.matmul(ps, ll, rh, start=False, stop=j == FT - 1)
                    if j == FT - 1:
                        acc.complete(m, ins)
                if j < FT - 1:
                    ev.up("w2", ins)

            def first_up(i):
                for j in range(AHEAD):
                    up(i, j)

            def body(i, ahead):
                down(i, 0)
                for j in range(AHEAD, FT):
                    up(i, j)
                    down(i, j - 1)
                    if j == FT - 4:
                        ahead("ms")
                down(i, FT - 1)
                ahead("up")
                ev.wait(pe, "y", i)
                for t in range(TT):
                    ps = dense.open(pe, f"t{t}", i)
                    for m in range(KT):
                        ins = pe.transpose(ps[:, m * P:(m + 1) * P], gate[:, m, t * P:(t + 1) * P], ident)
                    dense.complete(f"t{t}", ins)

            def before(part):
                if part in ("up", "body"):
                    dense.skip(pe, {"up": late, "body": turned}[part], -1)

            def skip(part):
                if part == "up":
                    dense.skip(pe, early, NB)

            loop_parts(pe, NB, {"ms": mean_square, "up": first_up}, body, before=before, skip=skip)


_INS = ["L0_attn_x", "L0_attn_Wq", "L0_attn_Wk", "L0_attn_Wkg1", "L0_attn_Wkg2", "L0_attn_bkg2", "L0_attn_Wv",
        "L0_attn_Wg", "L0_attn_bg", "L0_attn_Wo", "L0_attn_ln1_w", "L0_attn_ln2_w", "L0_attn_W1", "L0_attn_W3",
        "L0_attn_W2", "L0_ffn_U", "L0_ffn_V", "L0_ffn_W1", "L0_ffn_b1", "L0_ffn_W2", "L0_ffn_b2"]


def build(nc, x, Wq, Wk, Wkg1, Wkg2, bkg2, Wv, Wg, bg, Wo, ln1_w, ln2_w, W1, W3, W2, U, V, fW1, fb1, fW2, fb2, out):
    NB, T, D = x.shape
    KT = D // P
    scratch = [nc.dram_tensor(f"scratch_{n}", (NB, P, KT, T), F32, kind="Internal").ap()
               for n in ("xn", "xa", "gate", "xmid")]
    xn_d, xa_d, gate_d, xmid_d = scratch
    with ExitStack() as ctx:
        consts = [ctx.enter_context(nc.sbuf_tensor(n, s, F32))[:] for n, s in (
            ("ident", [P, P]), ("hmask", [P, 8]), ("causal", [P, P]), ("avg32", [P, P]), ("avg_all", [P, P]),
            ("chunk_start", [P, T]), ("eps", [P, 1]))]
        make_constants(nc, consts)
        with ExitStack() as actx:
            aw = attention_weights(nc, actx, KT, D, Wk.shape[1])

            def background(sems, pool):
                prepare_attention_weights(nc, sems, pool, aw, Wq, Wk, Wkg1, Wkg2, bkg2, Wv, Wg, bg, Wo, ln1_w)

            phase_f(nc, background, consts, x, U, V, fW1, fb1, fW2, fb2, xn_d, xa_d, gate_d)
            phase_a(nc, consts, aw, xn_d, xa_d, xmid_d)
        phase_m(nc, consts, x, xmid_d, gate_d, W1, W3, W2, ln2_w, out)


def kernel(**inputs):
    import numpy as _np
    import concourse.bacc as _bacc
    from concourse.bass_utils import run_bass_kernel_spmd as _run

    nc = _bacc.Bacc("TRN2", target_bir_lowering=False, num_devices=1)
    arrays, args = {}, []
    for name in _INS:
        a = _np.ascontiguousarray(inputs[name])
        arrays[f"in_{name}"] = a
        args.append(nc.dram_tensor(f"in_{name}", a.shape, mybir.dt.from_np(a.dtype), kind="ExternalInput").ap())
    shape = inputs["L0_attn_x"].shape
    out = nc.dram_tensor("out", shape, F32, kind="ExternalOutput").ap()
    build(nc, *args, out)
    r = _run(nc, [arrays], core_ids=[0])
    return r.results[0]["out"]
```

```python
from contextlib import ExitStack

import concourse.bass as bass
from concourse import mybir

F32 = mybir.dt.float32
F32R = mybir.dt.float32r
ALU = mybir.AluOpType
ACT = mybir.ActivationFunctionType
AX = mybir.AxisListType.X
EXP_LN_SET = "natural_log_exp_and_others"
SILU_SET = "silu_and_others"

P = 128
EPS = 1e-5
GATE_SCALE = 1.0 / 16.0


class Event:

    def __init__(self, sem, per):
        self.sem, self.per = sem, per


class Events:

    def __init__(self, nc, ctx, prefix):
        self.nc, self.ctx, self.prefix, self.all = nc, ctx, prefix, {}

    def add(self, name, per=1, ctx=None):
        assert name not in self.all
        self.all[name] = Event((ctx or self.ctx).enter_context(self.nc.semaphore(f"{self.prefix}_{name}")), per)

    def at(self, name, i, k=None):
        e = self.all[name]
        return e.sem, i * e.per + (e.per + (e.per if k is None else k))

    def at_before(self, name, i, k=None):
        e = self.all[name]
        return e.sem, i * e.per + (e.per if k is None else k)

    def wait(self, eng, name, i, k=None):
        eng.wait_ge(*self.at(name, i, k))

    def wait_before(self, eng, name, i, k=None):
        eng.wait_ge(*self.at_before(name, i, k))

    def up(self, name, ins):
        ins.then_inc(self.all[name].sem, 1)

    def up_dma(self, name, ins):
        ins.then_inc(self.all[name].sem, 16)

    def landed(self, name, eng):
        eng.sem_inc(self.all[name].sem, 16)

    def give_credits(self, eng):
        for e in self.all.values():
            eng.sem_inc(e.sem, e.per)


class Slots:

    def __init__(self, ev, name, regions, order, early=()):
        self.ev, self.name, self.regions = ev, name, regions
        self.where, used = {}, [0] * len(regions)
        for n, result in enumerate(order):
            r = n % len(regions)
            used[r] += 1
            self.where[result] = (r, used[r], 1 if early and result not in early else 0)
        for r, n in enumerate(used):
            ev.add(f"{name}{r}_ready", n)
            ev.add(f"{name}{r}_taken", n)

    def wait(self, eng, what, result, i, before=0):
        r, k, bodies = self.where[result]
        name = f"{self.name}{r}_{what}"
        per = self.ev.all[name].per
        self.ev.wait(eng, name, i, k + (bodies - before) * per)
        return self.regions[r]

    def open(self, pe, result, i):
        r, k, bodies = self.where[result]
        name = f"{self.name}{r}_taken"
        self.ev.wait(pe, name, i, k - 1 + bodies * self.ev.all[name].per)
        return self.regions[r]

    def complete(self, result, ins):
        self.ev.up(f"{self.name}{self.where[result][0]}_ready", ins)

    def get(self, eng, result, i):
        return self.wait(eng, "ready", result, i)

    def get_before(self, eng, result, i):
        self.wait(eng, "ready", result, i, 1)

    def take(self, result, ins):
        self.ev.up(f"{self.name}{self.where[result][0]}_taken", ins)

    def wait_taken(self, eng, result, i):
        self.wait(eng, "taken", result, i)

    def wait_taken_before(self, eng, result, i):
        self.wait(eng, "taken", result, i, 1)

    def skip(self, pe, results, i):
        for result in results:
            self.open(pe, result, i)
            for what in ("ready", "taken"):
                pe.sem_inc(self.ev.all[f"{self.name}{self.where[result][0]}_{what}"].sem, 1)


def bcast(ap, axis, n):
    shape = list(ap.shape)
    shape.insert(axis, n)
    return ap.unsqueeze(axis).broadcast_to(shape)


def product3(pe, out, terms):
    last = len(terms) - 1
    for n, ((lh, ll), (rh, rl)) in enumerate(terms):
        pe.matmul(out, lh, rh, start=n == 0, stop=False)
        pe.matmul(out, lh, rl, start=False, stop=False)
        ins = pe.matmul(out, ll, rh, start=False, stop=n == last)
    return ins


def loop(eng, n, first, body, peel=False):
    loop_parts(eng, n, {None: first}, lambda i, ahead: body(i, lambda: ahead(None)), peel)


def loop_parts(eng, n, parts, body, peel=False, before=None, skip=None, first=True):
    for part, work in parts.items() if first else ():
        if before:
            before(part)
        work(0)
    if before:
        before("body")
    if peel:
        body(0, lambda part: parts[part](1))
    with eng.Fori(1 if peel else 0, n - 1) as i:
        body(i, lambda part: parts[part](i + 1))
    body(n - 1, skip or (lambda part: None))


def nothing(i):
    pass


def row(dram, i):
    return dram[bass.ds(i, 1)]


def make_constants(nc, consts):
    with ExitStack() as ctx:
        s_fill = ctx.enter_context(nc.semaphore("s_fill"))
        s_row = ctx.enter_context(nc.semaphore("s_row"))
        block = ctx.enter_context(nc.Block())
        ident, hmask, causal, avg32, avg_all, chunk_start, eps = consts

        @block.gpsimd
        def _(pool):
            n = 0

            def step(ins):
                nonlocal n
                n += 1
                ins.then_inc(s_fill, 1)
                pool.wait_ge(s_fill, n)

            def select(ap, op, base, pattern, cm, fill):
                step(pool.affine_select(out=ap, in_=ap, compare_op=op, fill=fill, base=base,
                                        pattern=pattern, channel_multiplier=cm))

            step(pool.memset(ident, 0.0))
            select(ident, ALU.not_equal, 0, [[-1, P]], 1, 1.0)
            step(pool.memset(hmask, 1.0))
            select(hmask, ALU.is_ge, 0, [[-16, 8]], 1, 0.0)
            select(hmask, ALU.is_ge, 15, [[16, 8]], -1, 0.0)
            step(pool.memset(causal, 1.0))
            select(causal, ALU.is_ge, 0, [[1, P]], -1, 0.0)
            step(pool.memset(avg32, 1.0 / 32))
            a = avg32.rearrange("p (a b) -> p a b", b=32)
            select(a, ALU.is_ge, 0, [[-32, 4], [0, 32]], 1, 0.0)
            select(a, ALU.is_ge, 31, [[32, 4], [0, 32]], -1, 0.0)
            step(pool.memset(avg_all, 1.0 / 512))
            step(pool.memset(eps, EPS))
            step(pool.memset(chunk_start, 1.0))
            step(pool.memset(chunk_start.rearrange("p (c t) -> p c t", t=P)[:, :, 0:1], 0.0))


def flat(ap):
    return ap.rearrange("p a b -> p (a b)")


def attention_weights(nc, ctx, KT, D, KD):
    def sb(name, shape, dt=F32):
        return ctx.enter_context(nc.sbuf_tensor("a_" + name, shape, dt))[:]

    w = {name: [sb(name + part, [P, KT, n], F32R) for part in ("hi", "lo")]
         for name, n in (("wkg1", 32), ("wk", KD), ("wq", KD), ("wv", D), ("wg", D), ("wo", D))}
    stage = sb("stage", [P, 2, D])
    w.update(stage=stage, fold=sb("fold", [P, D // 32, 16]), wkg2=sb("wkg2", [P, KD]), bkg2=sb("bkg2", [P, KD // P]), bg=sb("bg", [P, KT]), ln1=sb("ln1", [P, KT]),
             mean=sb("mean", [P, D // 32]))
    return w


def prepare_attention_weights(nc, ctx, pool, w, Wq, Wk, Wkg1, Wkg2, bkg2, Wv, Wg, bg, Wo, ln1_w):
    s_small, s_step = (ctx.enter_context(nc.semaphore(f"aw_{n}")) for n in ("small", "step"))
    s_load = [ctx.enter_context(nc.semaphore(f"aw_load{n}")) for n in range(2)]
    steps = [0]

    def step(ins):
        steps[0] += 1
        ins.then_inc(s_step, 1)
        pool.wait_ge(s_step, steps[0])

    step(pool.memset(w["wkg2"], 0.0))
    for part in w["wkg1"]:
        step(pool.memset(part.bitcast(F32), 0.0))
    pool.dma_start(w["wkg2"][0:Wkg2.shape[0], :], Wkg2).then_inc(s_small, 16)
    for dst, src in ((w["bkg2"], bkg2), (w["bg"], bg), (w["ln1"], ln1_w)):
        pool.dma_start(dst, src.rearrange("(m p) -> p m", p=P), allow_slow_non_contiguous=True).then_inc(s_small, 16)
    jobs = [(name, src, kt) for name, src in (("wkg1", Wkg1), ("wk", Wk), ("wq", Wq), ("wv", Wv), ("wg", Wg), ("wo", Wo))
            for kt in range(src.shape[0] // P)]

    def load(n):
        _, src, kt = jobs[n]
        pool.dma_start(w["stage"][:, n % 2, 0:src.shape[1]], src[kt * P:(kt + 1) * P, :]).then_inc(s_load[n % 2], 16)

    load(0)
    pool.wait_ge(s_small, 64)
    for n, (name, src, kt) in enumerate(jobs):
        if n + 1 < len(jobs):
            load(n + 1)
        cols = src.shape[1]
        s = w["stage"][:, n % 2, 0:cols]
        pool.wait_ge(s_load[n % 2], 16 * (n // 2 + 1))
        if name == "wv":
            heads = s.rearrange("p (a b) -> p a b", b=32)
            step(pool.tensor_tensor(w["fold"][:, :, 0:16], heads[:, :, 0:16], heads[:, :, 16:32], ALU.add))
            for half in (8, 4, 2, 1):
                step(pool.tensor_tensor(w["fold"][:, :, 0:half], w["fold"][:, :, 0:half],
                                        w["fold"][:, :, half:2 * half], ALU.add))
            step(pool.tensor_scalar(w["mean"], w["fold"][:, :, 0], 1.0 / 32, None, ALU.mult))
            step(pool.tensor_tensor(heads, heads, bcast(w["mean"], 2, 32), ALU.subtract))
        if name != "wo":
            step(pool.tensor_scalar(s, s, w["ln1"][:, kt:kt + 1], None, ALU.mult))
        hi, lo = (part[:, kt, 0:cols] for part in w[name])
        step(pool.tensor_copy(hi, s))
        step(pool.tensor_tensor(lo, s, hi.bitcast(F32), ALU.subtract))


def phase_f(nc, outer, background, consts, shared, x, U, V, W1, b1, W2, b2, xn_d, xa_d, gate_d):
    ident, eps = consts[0], consts[-1]
    NB, T, D = x.shape
    KT, TT = D // P, T // P
    E, R = U.shape[0], U.shape[2]
    ctx = ExitStack()
    with ctx:
        def sb(name, shape, dt=F32):
            return ctx.enter_context(nc.sbuf_tensor("f_" + name, shape, dt))[:]

        w1 = [sb(f"w1{a}", [P, KT, D], F32R) for a in ("hi", "lo")]
        vt = [sb(f"vt{a}", [P, KT, E * R], F32R) for a in ("hi", "lo")]
        ut = [sb(f"ut{a}", [P, KT, D], F32R) for a in ("hi", "lo")]
        w2 = sb("w2", [P, KT, E])
        b1_sb, b2_sb = sb("b1", [P, KT]), sb("b2", [P, E])
        xt = sb("xt", [P, TT, D])
        xs = sb("xs", [P, TT, D])
        xn, xa, gate = shared
        xn_hl = [sb(f"xn{a}", [P, KT, T], F32R) for a in ("hi", "lo")]
        h1 = sb("h1", [P, KT, T])
        assert T == E * R == KT * P == TT * P
        alpha = h1
        vx = alpha_b = gate
        vx_hl = [sb(f"vx{a}", [P, KT, T], F32R) for a in ("hi", "lo")]
        stats, mv = sb("stats", [P, TT, 6]), sb("mv", [P, TT, 2])
        rstd, r1 = sb("rstd", [P, TT]), sb("r1", [P, TT])
        logit, top = sb("logit", [P, TT, E]), sb("top", [P, TT])
        psum = [ctx.enter_context(nc.psum_tensor(f"f_ps{b}", [P, 512], F32))[:] for b in range(8)]

        w1_in, v_in, u_in = h1, gate, xs
        turned = [psum[n] for n in (0, 1, 2, 7)]
        s_w1, s_v, s_u, s_small, s_turned, s_whi, s_wlo, s_next = (
            ctx.enter_context(nc.semaphore(f"fw_{n}")) for n in ("w1", "v", "u", "small", "turned", "hi", "lo", "next"))
        w1_pieces = [(w1_in[:, k, :], w1[0][:, k, :], w1[1][:, k, :]) for k in range(KT)]
        vu_pieces = [(turned[m], w[0][:, m, :], w[1][:, m, :]) for w in (vt, ut) for m in range(KT)]

        ev = Events(nc, ctx, "f")
        for name, per in (("stats", TT), ("mv", TT), ("rstd", 2), ("m2", 2), ("r1", 2), ("norm", TT), ("norm2", TT),
                          ("xnhi", KT), ("xnlo", KT), ("softmax", 4), ("exp", 1), ("alpha", 1), ("vxhi", KT),
                          ("vxlo", KT), ("x_in", 16), ("xn_out", 16), ("xa_out", 16)):
            ev.add(name, per)
        ev.add("gate_out", 16, outer)
        xn_parts, xa_parts, alphas, hs, vs, us = ([f"{n}{m}" for m in range(KT)]
                                                  for n in ("xn", "xa", "alpha", "h", "v", "u"))
        turn = Slots(ev, "turn", psum[0:3], xn_parts + alphas + xa_parts, xn_parts + xa_parts)
        dense = Slots(ev, "dense", psum[3:8], ["logit"] + vs + hs + us, hs)
        LAST = KT - 1
        block = ctx.enter_context(nc.Block())

        @block.gpsimd
        def _(pool):
            background(ctx, pool)

        @block.sync
        def _(sp):
            ev.give_credits(sp)
            def load(i):
                turn.get_before(sp, f"xa{LAST}", i)
                ev.up_dma("x_in", sp.dma_start(xt, row(x, i).rearrange("o (tt p) d -> p (o tt) d", p=P)))

            def weights(_):
                sp.dma_start(w1_in, W1.rearrange("(k p) n -> p k n", p=P)).then_inc(s_w1, 16)
                sp.dma_start(b1_sb, b1.rearrange("(kt p) -> p kt", p=P), allow_slow_non_contiguous=True).then_inc(s_small, 16)
                sp.dma_start(w2, W2.rearrange("(kt p) e -> p kt e", p=P)).then_inc(s_small, 16)
                sp.dma_start(b2_sb, b2.partition_broadcast(P)).then_inc(s_small, 16)
                sp.dma_start(v_in, V.rearrange("(m a) r d -> (a r) m d", a=P // R)).then_inc(s_v, 16)
                turn.get(sp, f"xa{LAST}", 0)
                for m in range(KT):
                    sp.dma_start(u_in[:, m, :].rearrange("p (k r) -> p k r", r=R),
                                 U[:, m * P:(m + 1) * P, :].rearrange("k p r -> p k r")).then_inc(s_u, 16)

            def store_xn(i):
                turn.wait_taken(sp, f"xn{LAST}", i)
                ev.up_dma("xn_out", sp.dma_start(row(xn_d, i).rearrange("o p m t -> p (o m) t"), xn))

            def store_xa(i):
                turn.wait_taken(sp, f"xa{LAST}", i)
                ev.up_dma("xa_out", sp.dma_start(row(xa_d, i).rearrange("o p m t -> p (o m) t"), xa))

            def body(i, ahead):
                ahead("x")
                ahead("xn")
                ahead("xa")

            loop_parts(sp, NB, {"x": load, "weights": weights, "xn": store_xn, "xa": store_xa}, body)
            ev.wait(sp, "xn_out", NB - 1)
            ev.wait(sp, "xa_out", NB - 1)
            sp.dma_start(xa, row(xa_d, 0).rearrange("o p m t -> p (o m) t")).then_inc(s_next, 16)
            sp.wait_ge(s_next, 16)

        @block.vector
        def _(dve):
            def norm(i):
                ev.wait(dve, "x_in", i)
                for t in range(TT):
                    ev.up("stats", dve.bn_stats(stats[:, t, :], xt[:, t, :]))
                ev.wait(dve, "stats", i)
                dve.memset(top, 0.0)
                for t in range(TT):
                    ev.up("mv", dve.bn_aggr(mv[:, t, :], stats[:, t, :]))
                ev.wait(dve, "rstd", i)
                ev.up("m2", dve.tensor_tensor(r1, mv[:, :, 1], rstd, ALU.mult))
                ev.wait(dve, "m2", i, 1)
                ev.up("m2", dve.tensor_tensor(r1, r1, rstd, ALU.mult))
                for t in range(TT):
                    ev.up("norm", dve.tensor_scalar(xt[:, t, :], xt[:, t, :], mv[:, t, 0:1], rstd[:, t:t + 1],
                                                    ALU.subtract, ALU.mult))
                ev.wait(dve, "r1", i)
                turn.get_before(dve, f"xa{LAST}", i)
                for t in range(TT):
                    ev.wait(dve, "norm", i, t + 1)
                    ev.up("norm2", dve.tensor_scalar(xs[:, t, :], xt[:, t, :], r1[:, t:t + 1], None, ALU.mult))

            def split(i):
                dense.get_before(dve, f"v{LAST}", i)
                for m in range(KT):
                    turn.wait_taken(dve, f"xn{m}", i)
                    ev.up("xnhi", dve.tensor_copy(xn_hl[0][:, m, :], xn[:, m, :]))
                    ev.wait(dve, "xnhi", i, m + 1)
                    ev.up("xnlo", dve.tensor_tensor(xn_hl[1][:, m, :], xn[:, m, :],
                                                    xn_hl[0][:, m, :].bitcast(F32), ALU.subtract))

            def split_weights(pieces, first):
                for n, (src, hi, lo) in enumerate(pieces, first):
                    dve.wait_ge(s_whi, n + 1)
                    dve.tensor_tensor(lo, src, hi.bitcast(F32), ALU.subtract).then_inc(s_wlo, 1)

            def w1_parts(_):
                split_weights(w1_pieces, 0)

            def vu_parts(_):
                split_weights(vu_pieces, KT)
                dve.wait_ge(s_small, 48)

            def body(i, ahead):
                ahead("norm")
                lg = dense.get(dve, "logit", i)[:, 0:TT * E].rearrange("p (t e) -> p t e", e=E)
                dense.take("logit", dve.tensor_tensor(logit, lg, bcast(b2_sb, 1, TT), ALU.add))
                dense.wait_taken(dve, "logit", i)
                ev.up("softmax", dve.tensor_reduce(top, logit, AX, ALU.max))
                ev.wait(dve, "softmax", i, 1)
                ev.up("softmax", dve.tensor_tensor(logit, logit, bcast(top, 2, E), ALU.subtract))
                ev.wait(dve, "exp", i)
                ev.up("softmax", dve.tensor_reduce(top, logit, AX, ALU.add))
                ev.wait(dve, "softmax", i, 3)
                ev.up("softmax", dve.reciprocal(top, top))
                ev.wait(dve, "softmax", i, 4)
                ev.up("alpha", dve.tensor_tensor(alpha.rearrange("p t (e r) -> p t e r", r=R), bcast(logit, 3, R),
                                                 bcast(bcast(top, 2, E), 3, R), ALU.mult))
                ahead("split")
                dense.get_before(dve, f"u{LAST}", i)
                for m in range(KT):
                    turn.wait_taken(dve, f"alpha{m}", i)
                    dense.take(f"v{m}", dve.tensor_tensor(vx[:, m, :], dense.get(dve, f"v{m}", i), alpha_b[:, m, :],
                                                          ALU.mult))
                    dense.wait_taken(dve, f"v{m}", i)
                    ev.up("vxhi", dve.tensor_copy(vx_hl[0][:, m, :], vx[:, m, :]))
                    ev.wait(dve, "vxhi", i, m + 1)
                    ev.up("vxlo", dve.tensor_tensor(vx_hl[1][:, m, :], vx[:, m, :],
                                                    vx_hl[0][:, m, :].bitcast(F32), ALU.subtract))

            loop_parts(dve, NB, {"norm": norm, "w1": w1_parts, "split": split, "vu": vu_parts}, body)

        @block.scalar
        def _(act):
            def norm(i):
                act.preload_act_table_set(EXP_LN_SET)
                ev.wait(act, "mv", i)
                ev.up("rstd", act.activation(rstd, mv[:, :, 1], ACT.Ln, bias=eps))
                ev.wait(act, "rstd", i, 1)
                ev.up("rstd", act.activation(rstd, rstd, ACT.Exp, scale=-0.5))
                ev.wait(act, "m2", i)
                ev.up("r1", act.activation(r1, r1, ACT.Ln, bias=eps))
                ev.wait(act, "r1", i, 1)
                ev.up("r1", act.activation(r1, r1, ACT.Exp, scale=-0.5))

            def fill_xn(i):
                ev.wait_before(act, "xn_out", i)
                ev.wait_before(act, "xnlo", i)
                for m in range(KT):
                    turn.take(f"xn{m}", act.activation(xn[:, m, :], turn.get(act, f"xn{m}", i), ACT.Copy))

            def fill_xa(i):
                ev.wait_before(act, "xa_out", i)
                for m in range(KT):
                    turn.take(f"xa{m}", act.activation(xa[:, m, :], turn.get(act, f"xa{m}", i), ACT.Copy))

            def hidden(i):
                for m in range(KT):
                    dense.take(f"h{m}", act.activation(h1[:, m, :], dense.get(act, f"h{m}", i), ACT.Relu,
                                                       bias=b1_sb[:, m:m + 1]))

            def w1_parts(_):
                act.wait_ge(s_w1, 16)
                for src, hi, lo in w1_pieces:
                    act.activation(hi, src, ACT.Copy).then_inc(s_whi, 1)
                act.wait_ge(s_small, 48)

            def vu_parts(_):
                for n, (src, hi, lo) in enumerate(vu_pieces):
                    act.wait_ge(s_turned, n + 1)
                    act.activation(hi, src, ACT.Copy).then_inc(s_whi, 1)

            def body(i, ahead):
                ahead("norm")
                ev.wait(act, "softmax", i, 2)
                ev.up("exp", act.activation(logit, logit, ACT.Exp))
                ahead("xn")
                act.preload_act_table_set(SILU_SET)
                ev.wait_before(act, "gate_out", i)
                for m in range(KT):
                    turn.take(f"alpha{m}", act.activation(alpha_b[:, m, :], turn.get(act, f"alpha{m}", i), ACT.Copy))
                ahead("xa")
                ahead("h")
                for m in range(KT):
                    dense.take(f"u{m}", act.activation(gate[:, m, :], dense.get(act, f"u{m}", i), ACT.Silu))
                dense.wait_taken(act, f"u{LAST}", i)
                ev.up_dma("gate_out", act.dma_start(row(gate_d, i).rearrange("o p m t -> p (o m) t"), gate))

            loop_parts(act, NB, {"norm": norm, "w1": w1_parts, "xn": fill_xn, "xa": fill_xa, "h": hidden, "vu": vu_parts},
                       body)
        @block.tensor
        def _(pe):
            def turn_weights(_):
                turn.wait_taken(pe, f"xa{LAST}", 0)
                for w, (s_in, need, src) in enumerate(((s_v, 16, v_in), (s_u, 16 * KT, u_in))):
                    pe.wait_ge(s_in, need)
                    for m in range(KT):
                        if w > 0:
                            pe.wait_ge(s_wlo, KT + m + 1)
                        for k in range(KT):
                            ins = pe.transpose(turned[m][:, k * P:(k + 1) * P], src[:, k, m * P:(m + 1) * P], ident)
                        ins.then_inc(s_turned, 1)
                pe.wait_ge(s_wlo, KT + len(vu_pieces))

            def turn_row(i, name, src, done):
                ev.wait(pe, done, i)
                for m in range(KT):
                    ps = turn.open(pe, f"{name}{m}", i)
                    for t in range(TT):
                        ins = pe.transpose(ps[:, t * P:(t + 1) * P], src[:, t, m * P:(m + 1) * P], ident)
                    turn.complete(f"{name}{m}", ins)

            def linear(i, name, w, src, m, split=None):
                ps = dense.open(pe, f"{name}{m}", i)
                for k in range(KT):
                    if m == 0 and split:
                        ev.wait(pe, split, i, k + 1)
                    wh, wl = (a[:, k, m * P:(m + 1) * P] for a in w)
                    sh, sl = (a[:, k, :] for a in src)
                    pe.matmul(ps, wh, sh, start=k == 0, stop=False)
                    pe.matmul(ps, wh, sl, start=False, stop=False)
                    ins = pe.matmul(ps, wl, sh, start=False, stop=k == LAST)
                dense.complete(f"{name}{m}", ins)

            def hidden(i):
                for m in range(KT):
                    linear(i, "h", w1, xn_hl, m, "xnlo")

            def body(i, ahead):
                dense.wait_taken(pe, f"h{LAST}", i)
                ps = dense.open(pe, "logit", i)
                for t in range(TT):
                    for k in range(KT):
                        ins = pe.matmul(ps[:, t * E:(t + 1) * E], h1[:, k, t * P:(t + 1) * P], w2[:, k, :],
                                        start=k == 0, stop=k == KT - 1)
                dense.complete("logit", ins)
                for m in range(KT):
                    linear(i, "v", vt, xn_hl, m)
                    if m == 1:
                        ahead("xn")
                ev.wait(pe, "alpha", i)
                for m in range(KT):
                    ps = turn.open(pe, f"alpha{m}", i)
                    for t in range(TT):
                        ins = pe.transpose(ps[:, t * P:(t + 1) * P], alpha[:, t, m * P:(m + 1) * P], ident)
                    turn.complete(f"alpha{m}", ins)
                ahead("xa")
                ahead("h")
                for m in range(KT):
                    linear(i, "u", ut, vx_hl, m, "vxlo")

            parts = {"xn": lambda i: turn_row(i, "xn", xt, "norm"), "xa": lambda i: turn_row(i, "xa", xs, "norm2"),
                     "h": hidden, "vu": turn_weights}

            def before(part):
                if part == "xa":
                    turn.skip(pe, alphas, -1)
                if part == "h":
                    pe.wait_ge(s_wlo, KT)
                if part in ("h", "body"):
                    dense.skip(pe, {"h": ["logit"] + vs, "body": us}[part], -1)

            def skip(part):
                slots, results = {"xn": (turn, xn_parts), "xa": (turn, xa_parts), "h": (dense, hs)}[part]
                slots.skip(pe, results, NB)

            loop_parts(pe, NB, parts, body, before=before, skip=skip)

        return ev.at("gate_out", NB - 1)


def phase_a(nc, outer, consts, gate_stored, shared, w, xn_d, xa_d, xmid_d):
    ident, hmask, causal, avg32, _, chunk_start, eps = consts
    NB, _, KT, T = xn_d.shape
    D = KT * P
    KD = w["wkg2"].shape[1]
    GR = KD // P
    NC = T // P
    KH, VH = 16, 32
    HG = P // KH
    QD = D // P
    HQ = P // VH
    H64, H32 = P // 2, P // 4
    ctx = ExitStack()
    with ctx:
        def sb(name, shape, dt=F32):
            return ctx.enter_context(nc.sbuf_tensor("a_" + name, shape, dt))[:]

        def pair(name, shape):
            return [sb(name + part, shape, F32R) for part in ("hi", "lo")]

        wkg1, wq, wk, wv, wg, wo = (w[name] for name in ("wkg1", "wq", "wk", "wv", "wg", "wo"))
        UR = wkg1[0].shape[2]
        wkg2, bkg2_sb, bg_sb = w["wkg2"], w["bkg2"], w["bg"]
        xn, xa, gsilu = shared
        xa_hl = pair("xa", [P, KT, T])
        u = sb("u", [P, T])
        shape = [P, GR * NC, P]
        k_sb, q_sb = flat(w["stage"]).rearrange("p (c t) -> p c t", t=P), sb("q", shape)
        neg, soft, cum = sb("neg", shape), sb("soft", shape), sb("cum", shape)
        lv64, lv32, dq, dk = sb("lv64", shape), sb("lv32", shape), sb("dq", shape), sb("dk", shape)
        khat, qhat = soft, neg
        decay = sb("decay", [P, GR * NC])
        v_tok = sb("v_tok", [P, NC, D])
        qx64 = [sb(f"qx64_{g}", [P, HG, H64]) for g in range(GR)]
        qx32 = [sb(f"qx32_{g}", [P, 2, HG, H32]) for g in range(GR)]
        qxd = [sb(f"qxd_{g}", [P, 4, HG, H32]) for g in range(GR)]
        a_sb = [sb(f"a{g}", [P, 2, HG, H64]) for g in range(GR)]
        kt_sb = flat(w["fold"]).rearrange("p (g t) -> p g t", g=GR)
        state = [sb(f"state{n}", [P, GR, HG * VH]) for n in range(2)]
        sq, oc, rn = sb("sq", [P, QD, P]), sb("oc", [P, QD, P]), sb("rn", [P, QD, P])
        og_hl = pair("og", [P, KT, T])
        psum = [ctx.enter_context(nc.psum_tensor(f"a_ps{b}", [P, 512], F32))[:] for b in range(4)]
        ps_att = [ctx.enter_context(nc.psum_tensor(f"a_att{g}", [P, 2, HG, H64], F32))[:] for g in range(2)]

        ev = Events(nc, ctx, "a")
        for name, per in (("xa_in", 16), ("xn_in", 16), ("xahi", KT), ("xalo", KT), ("absz", GR),
                          ("expz", GR), ("softz", GR), ("negz", GR), ("logg", GR), ("cum", GR), ("offs", 3),
                          ("offk", 1), ("e64", 2), ("e32", 2), ("edk", 1), ("edq", 1), ("ekh", 1), ("eqh", 1),
                          ("decay", 1), ("m64", 2), ("m32", 2), ("mdk", 1), ("mdq", 1), ("mkh", 1), ("mqh", 1),
                          ("qxs", 2 * GR * NC), ("qxd", GR * NC), ("state", GR * (NC - 2)),
                          ("sq", NC), ("rn", NC), ("og", 2 * NC), ("oghi", NC), ("oglo", NC)):
            ev.add(name, per)
        ev.add("xmid_out", 16, outer)
        zs, values = [f"z{g}" for g in range(GR)], [f"v{c}" for c in range(NC)]
        gates, outs = [f"g{m}" for m in range(KT)], [f"o{m}" for m in range(KT)]
        assert GR == 2 and NC == 4
        order = [(None, ["kt0"]), ("k0", ["k0"]), (None, ["ds0", "kt1"]), ("k1", ["k1"]),
                 (None, ["ds1", "var0", "kt2"]), ("q0", ["q0"]), (None, ["ds2", "var1"]), ("q1", ["q1"]),
                 ("u", ["u"]), (None, ["var2"]), ("z", zs), (None, ["var3"]), ("v", values), (None, outs),
                 ("g", gates)]
        early = {part: results for part, results in order if part}
        late = {order[n + 1][0]: results for n, (part, results) in enumerate(order) if not part}
        dense = Slots(ev, "dense", psum[0:3], sum((results for _, results in order), []), sum(early.values(), []))
        att = Slots(ev, "att", ps_att, [f"{c}_{g}" for c in range(NC) for g in range(GR)])
        mix = Slots(ev, "mix", psum[3:4], list(range(NC)))
        LAST = KT - 1
        s_next = ctx.enter_context(nc.semaphore("a_next"))
        block = ctx.enter_context(nc.Block())

        def tokens(c):
            return slice(c * P, (c + 1) * P)

        @block.sync
        def _(sp):
            ev.give_credits(sp)

            def load(i):
                ev.wait_before(sp, "xalo", i)
                ev.up_dma("xa_in", sp.dma_start(xa, row(xa_d, i).rearrange("o p m t -> p (o m) t")))

            def body(i, ahead):
                ahead("xa")
                ev.wait_before(sp, "xmid_out", i)
                ev.up_dma("xn_in", sp.dma_start(xn, row(xn_d, i).rearrange("o p m t -> p (o m) t")))
                dense.wait_taken(sp, f"o{LAST}", i)
                ev.up_dma("xmid_out", sp.dma_start(row(xmid_d, i).rearrange("o p m t -> p (o m) t"), xn))

            def next_phase(_):
                ev.wait(sp, "xalo", NB - 1)
                sp.dma_start(xa, row(xmid_d, 0).rearrange("o p m t -> p (o m) t")).then_inc(s_next, 16)

            ev.landed("xa_in", sp)
            loop_parts(sp, NB, {"xa": load}, body, skip=next_phase, first=False)
            sp.wait_ge(s_next, 16)

        @block.vector
        def _(dve):
            def split(i):
                for m in range(KT):
                    ev.wait(dve, "xahi", i, m + 1)
                    ev.up("xalo", dve.tensor_tensor(xa_hl[1][:, m, :], xa[:, m, :],
                                                    xa_hl[0][:, m, :].bitcast(F32), ALU.subtract))

            def spread_d(i, c, g):
                gc = g * NC + c
                q = dq[:, gc, :].rearrange("p (b t) -> p b t", t=H32)
                ev.up("qxd", dve.tensor_tensor(qxd[g], bcast(q, 2, HG), bcast(bcast(hmask, 1, 4), 3, H32), ALU.mult))

            def inner_gate(i):
                dense.take("u", dve.tensor_copy(u[0:UR], dense.get(dve, "u", i)[0:UR]))

            def sum_gates(i):
                def group(buf, g):
                    return flat(buf[:, g * NC:(g + 1) * NC, :])

                for g in range(GR):
                    ev.wait(dve, "absz", i, g + 1)
                    dense.take(f"z{g}", dve.tensor_scalar(group(neg, g), dense.get(dve, f"z{g}", i),
                                                          bkg2_sb[:, g:g + 1], 0.0, ALU.add, ALU.min))
                for g in range(GR):
                    dense.wait_taken(dve, f"z{g}", i)
                    ev.wait(dve, "softz", i, g + 1)
                    ev.up("logg", dve.tensor_tensor(group(neg, g), group(neg, g), group(soft, g), ALU.subtract))
                    ev.wait(dve, "logg", i, g + 1)
                    ev.up("cum", dve.tensor_tensor_scan(group(cum, g), chunk_start, group(neg, g), 0.0, ALU.mult,
                                                        ALU.add))
                ev.wait(dve, "cum", i)
                for dst, n, ref in ((lv64, P, H64 - 1), (lv32, H64, H32 - 1), (dq, H32, H32 // 2 - 1)):
                    cv = flat(cum).rearrange("p (b t) -> p b t", t=n)
                    dv = flat(dst).rearrange("p (b t) -> p b t", t=n)
                    at = cv[:, :, ref]
                    ev.up("offs", dve.tensor_tensor(dv, cv, bcast(at, 2, n), ALU.subtract))

            def weigh_upper(i):
                dense.wait_taken(dve, f"q{GR - 1}", i)
                for name, buf, n in (("64", lv64, P), ("32", lv32, H64)):
                    for part, src in ((0, k_sb), (1, q_sb)):
                        b = flat(buf).rearrange("p (b a t) -> p b a t", a=2, t=n // 2)[:, :, part, :]
                        s = flat(src).rearrange("p (b a t) -> p b a t", a=2, t=n // 2)[:, :, part, :]
                        ev.wait(dve, "e" + name, i, part + 1)
                        ev.up("m" + name, dve.tensor_tensor(b, b, s, ALU.mult))

            def weigh_last(i):
                ev.wait(dve, "edk", i)
                ev.up("mdk", dve.tensor_tensor(dk, dk, k_sb, ALU.mult))
                ev.wait(dve, "edq", i)
                ev.up("mdq", dve.tensor_tensor(dq, dq, q_sb, ALU.mult))

            def first_spread(i):
                ev.wait(dve, "mdq", i)
                for g in range(GR):
                    spread_d(i, 0, g)

            def clear(_):
                dve.memset(u, 0.0)
                for ps in ps_att:
                    for half in range(2):
                        dve.memset(ps[:, half], 0.0)

            def body(i, ahead):
                ahead("split")
                for c in range(NC):
                    if c > 0:
                        mix.get(dve, c - 1, i)
                    for g in range(GR):
                        ps = att.get(dve, f"{c}_{g}", i)
                        cz = causal.rearrange("p (a t) -> p a t", a=2)
                        att.take(f"{c}_{g}", dve.tensor_tensor(a_sb[g], ps, bcast(cz, 2, HG), ALU.mult))
                        if c + 1 < NC:
                            spread_d(i, c + 1, g)
                    if c + 1 < NC:
                        new, old = state[(c + 1) % 2], state[c % 2]
                        ds = dense.get(dve, f"ds{c}", i).rearrange("p (g h v) -> p g h v", g=GR, v=VH)
                        dense.take(f"ds{c}", dve.tensor_tensor(new.rearrange("p g (h v) -> p g h v", v=VH), ds,
                                                               bcast(bcast(hmask, 1, GR), 3, VH), ALU.mult))
                        dense.wait_taken(dve, f"ds{c}", i)
                        if c > 0:
                            ev.wait(dve, "decay", i)
                            for g in range(GR):
                                gc = g * NC + c
                                ev.up("state", dve.scalar_tensor_tensor(new[:, g, :], old[:, g, :],
                                                                        decay[:, gc:gc + 1], new[:, g, :],
                                                                        ALU.mult, ALU.add))
                            ev.wait(dve, "state", i, GR * c)
                    else:
                        ahead("u")
                    if c > 0:
                        gated(i, c - 1)
                ahead("gates")
                gated(i, NC - 1)
                ahead("upper")
                ev.wait(dve, "xn_in", i)
                for m in range(KT):
                    dense.take(f"o{m}", dve.tensor_tensor(xn[:, m, :], dense.get(dve, f"o{m}", i), xn[:, m, :],
                                                          ALU.add))
                    if m == 1:
                        ahead("last")
                ahead("spread")

            def gated(i, c):
                ev.wait(dve, "rn", i, c + 1)
                ev.up("og", dve.tensor_tensor(rn, rn, oc, ALU.mult))
                dense.wait_taken(dve, f"g{LAST}", i)
                ev.wait(dve, "og", i, 2 * c + 1)
                ev.up("og", dve.tensor_tensor(rn, rn, gsilu[:, :, tokens(c)], ALU.mult))
                ev.wait(dve, "og", i, 2 * c + 2)
                ev.up("oghi", dve.tensor_copy(og_hl[0][:, :, tokens(c)], rn))
                ev.wait(dve, "oghi", i, c + 1)
                ev.up("oglo", dve.tensor_tensor(og_hl[1][:, :, tokens(c)], rn,
                                                og_hl[0][:, :, tokens(c)].bitcast(F32), ALU.subtract))

            loop_parts(dve, NB, {"clear": clear, "split": split, "u": inner_gate, "gates": sum_gates,
                                 "upper": weigh_upper, "last": weigh_last, "spread": first_spread}, body)

        @block.gpsimd
        def _(pool):
            def spread(i, c, g):
                gc = g * NC + c
                ev.up("qxs", pool.tensor_tensor(qx64[g], bcast(lv64[:, gc, H64:P], 1, HG), bcast(hmask, 2, H64),
                                                ALU.mult))
                q = lv32[:, gc, :].rearrange("p (b a t) -> p b a t", a=2, t=H32)[:, :, 1, :]
                ev.up("qxs", pool.tensor_tensor(qx32[g], bcast(q, 2, HG), bcast(bcast(hmask, 1, 2), 3, H32),
                                                ALU.mult))

            def body(i, ahead):
                ev.wait(pool, "cum", i)
                ev.up("offk", pool.tensor_tensor(khat, cum, bcast(cum[:, :, P - 1], 2, P), ALU.subtract))
                ev.wait(pool, "m64", i)
                ev.wait(pool, "m32", i)
                for g in range(GR):
                    spread(i, 0, g)
                dense.wait_taken(pool, f"q{GR - 1}", i)
                ev.wait(pool, "ekh", i)
                ev.up("mkh", pool.tensor_tensor(khat, khat, k_sb, ALU.mult))
                ev.wait(pool, "eqh", i)
                ev.up("mqh", pool.tensor_tensor(qhat, qhat, q_sb, ALU.mult))
                for c in range(1, NC):
                    for g in range(GR):
                        att.get(pool, f"{c - 1}_{g}", i)
                        spread(i, c, g)

            loop(pool, NB, nothing, body)

        @block.scalar
        def _(act):
            def half(buf, n, part):
                return flat(buf).rearrange("p (b a t) -> p b a t", a=2, t=n // 2)[:, :, part, :]

            def split(i):
                ev.wait(act, "xa_in", i)
                dense.get_before(act, f"g{LAST}", i)
                for m in range(KT):
                    ev.up("xahi", act.activation(xa_hl[0][:, m, :], xa[:, m, :], ACT.Copy))

            def fill(name, buf, g, scale):
                def part(i):
                    dense.take(f"{name}{g}", act.activation(flat(buf[:, g * NC:(g + 1) * NC, :]),
                                                            dense.get(act, f"{name}{g}", i), ACT.Copy, scale=scale))
                return part

            def soft_gates(i):
                def group(g):
                    return flat(soft[:, g * NC:(g + 1) * NC, :])

                for g in range(GR):
                    ps = dense.get(act, f"z{g}", i)
                    ev.up("absz", act.activation(group(g), ps, ACT.Abs, bias=bkg2_sb[:, g:g + 1]))
                for g in range(GR):
                    ev.wait(act, "absz", i, g + 1)
                    ev.up("expz", act.activation(group(g), group(g), ACT.Exp, scale=-1.0))
                    ev.wait(act, "expz", i, g + 1)
                    ev.up("softz", act.activation(group(g), group(g), ACT.Ln, bias=1.0))

            def exponentials(i):
                def value(c):
                    dense.take(f"v{c}", act.activation(v_tok[:, c, :], dense.get(act, f"v{c}", i), ACT.Copy))

                for n, (name, buf, length) in enumerate((("e64", lv64, P), ("e32", lv32, H64))):
                    ev.wait(act, "offs", i, n + 1)
                    for part, sign in ((0, -1), (1, 1)):
                        b = half(buf, length, part)
                        ev.up(name, act.activation(b, b, ACT.Exp, scale=sign * GATE_SCALE))
                    value(n)
                ev.wait(act, "offs", i, 3)
                ev.up("edk", act.activation(dk, dq, ACT.Exp, scale=-GATE_SCALE))
                ev.wait(act, "edk", i)
                ev.up("edq", act.activation(dq, dq, ACT.Exp, scale=GATE_SCALE))
                value(2)
                ev.wait(act, "offk", i)
                ev.up("ekh", act.activation(khat, khat, ACT.Exp, scale=-GATE_SCALE))
                value(3)
                ev.up("eqh", act.activation(qhat, cum, ACT.Exp, scale=GATE_SCALE))
                ev.up("decay", act.activation(decay, cum[:, :, P - 1], ACT.Exp, scale=GATE_SCALE))

            def output_gate(i):
                act.preload_act_table_set(SILU_SET)
                if isinstance(i, int) and i == 0:
                    act.wait_ge(*gate_stored)
                ev.wait_before(act, "oglo", i)
                for m in range(KT):
                    dense.take(f"g{m}", act.activation(gsilu[:, m, :], dense.get(act, f"g{m}", i), ACT.Silu,
                                                       bias=bg_sb[:, m:m + 1]))
                act.preload_act_table_set(EXP_LN_SET)

            def body(i, ahead):
                ahead("split")
                for c in range(NC):
                    if c + 1 < NC:
                        dense.take(f"kt{c}", act.activation(flat(kt_sb), dense.get(act, f"kt{c}", i)[:, 0:GR * P],
                                                            ACT.Copy))
                    ahead(("k0", "k1", "q0", "q1")[c])
                    if c > 0:
                        inverse_deviation(i, c - 1)
                    ps = mix.get(act, c, i)
                    ev.up("sq", act.activation(flat(sq), ps, ACT.Square))
                    if c > 0:
                        ev.wait(act, "og", i, 2 * (c - 1) + 1)
                    mix.take(c, act.activation(flat(oc), ps, ACT.Copy))
                ahead("z")
                inverse_deviation(i, NC - 1)
                ahead("exponentials")
                ahead("g")

            def inverse_deviation(i, c):
                ps = dense.get(act, f"var{c}", i)
                if c > 0:
                    ev.wait(act, "oglo", i, c)
                dense.take(f"var{c}", act.activation(flat(rn), ps, ACT.Ln, bias=eps))
                dense.wait_taken(act, f"var{c}", i)
                ev.up("rn", act.activation(rn, rn, ACT.Exp, scale=-0.5))

            parts = {"split": split}
            for name, buf, scale in (("k", k_sb, VH ** -0.5), ("q", q_sb, 1.0)):
                for g in range(GR):
                    parts[f"{name}{g}"] = fill(name, buf, g, scale)
            parts.update({"z": soft_gates, "exponentials": exponentials, "g": output_gate})
            act.preload_act_table_set(EXP_LN_SET)
            loop_parts(act, NB, parts, body)

        @block.tensor
        def _(pe):
            def linear(i, name, w, src, m):
                ps = dense.open(pe, f"{name}{m}", i)
                dense.complete(f"{name}{m}", product3(pe, ps, [
                    (tuple(a[:, k, m * P:(m + 1) * P] for a in w), tuple(a[:, k, :] for a in src)) for k in range(KT)]))

            def weights(i, c, g):
                gc = g * NC + c
                ps = att.open(pe, f"{c}_{g}", i)
                ev.wait(pe, "m64", i)
                ev.wait(pe, "m32", i)
                ev.wait(pe, "mdk", i)
                ev.wait(pe, "qxs", i, 2 * (GR * c + g) + 2)
                ev.wait(pe, "qxd", i, GR * c + g + 1)

                def block_product(s, half, at, n, keys, q):
                    return pe.matmul(ps[s:s + H32, half, :, at:at + n], keys[:, gc, s:s + H32], q, start=True,
                                     stop=True, tile_position=(0, s))

                for s in (0, H32):
                    block_product(s, 1, 0, H64, lv64, qx64[g])
                for b in range(2):
                    block_product(H64 * b, b, H32, H32, lv32, qx32[g][:, b])
                for b in range(4):
                    ins = block_product(H32 * b, b // 2, H32 * (b % 2), H32, dk, qxd[g][:, b])
                att.complete(f"{c}_{g}", ins)

            def variance(i, c):
                ev.wait(pe, "sq", i, c + 1)
                ps = dense.open(pe, f"var{c}", i)
                dense.complete(f"var{c}", pe.matmul(ps, avg32, flat(sq), start=True, stop=True))

            def keys(i):
                ev.wait(pe, "xalo", i)
                linear(i, "k", wk, xa_hl, 0)

            def inner_gate(i):
                ps = dense.open(pe, "u", i)
                dense.complete("u", product3(pe, ps[0:UR], [
                    (tuple(a[:, k, :] for a in wkg1), tuple(a[:, k, :] for a in xa_hl)) for k in range(KT)]))

            def key_gates(i):
                dense.wait_taken(pe, "u", i)
                for g in range(GR):
                    ps = dense.open(pe, f"z{g}", i)
                    dense.complete(f"z{g}", pe.matmul(ps, wkg2[:, g * P:(g + 1) * P], u, start=True, stop=True))

            def value_rows(i):
                for c in range(NC):
                    ps = dense.open(pe, f"v{c}", i)
                    dense.complete(f"v{c}", product3(pe, ps, [
                        (tuple(a[:, k, tokens(c)] for a in xa_hl), tuple(a[:, k, :] for a in wv)) for k in range(KT)]))

            def output_gates(i):
                for m in range(KT):
                    linear(i, "g", wg, xa_hl, m)

            def body(i, ahead):
                for g in range(GR):
                    weights(i, 0, g)
                for c in range(NC):
                    gcs = [g * NC + c for g in range(GR)]
                    if c + 1 < NC:
                        ev.wait(pe, "mkh", i)
                        ps = dense.open(pe, f"kt{c}", i)
                        for g in range(GR):
                            ins = pe.transpose(ps[:, g * P:(g + 1) * P], khat[:, gcs[g], :], ident)
                        dense.complete(f"kt{c}", ins)
                        ahead(("k0", "k1", "q0")[c])
                        for g in range(GR):
                            weights(i, c + 1, g)
                        dense.wait_taken(pe, f"kt{c}", i)
                        ps = dense.open(pe, f"ds{c}", i)
                        for g in range(GR):
                            n = HG * VH
                            ins = pe.matmul(ps[:, g * n:(g + 1) * n], kt_sb[:, g, :], v_tok[:, c, g * n:(g + 1) * n],
                                            start=True, stop=True)
                        dense.complete(f"ds{c}", ins)
                    if c + 1 == NC:
                        ahead("q1")
                        ahead("u")
                    if c > 0:
                        variance(i, c - 1)
                    ps = mix.open(pe, c, i).rearrange("p (q t) -> p q t", t=P)
                    for g in range(GR):
                        att.wait_taken(pe, f"{c}_{g}", i)
                    if c > 0:
                        ev.wait(pe, "mqh", i)
                    if c == 1:
                        dense.wait_taken(pe, "ds0", i)
                    if c > 1:
                        ev.wait(pe, "state", i, GR * (c - 1))
                    for quad in range(QD):
                        g, first_head = quad * HQ // HG, quad * HQ % HG
                        if c > 0:
                            pe.matmul(ps[:, quad, :], state[c % 2][:, g, first_head * VH:(first_head + HQ) * VH],
                                      qhat[:, gcs[g], :], start=True, stop=True, skip_group_check=True)
                        for j in range(HQ):
                            h = quad * HQ + j
                            ins = pe.matmul(ps[VH * j:VH * (j + 1), quad, :], v_tok[:, c, VH * h:VH * (h + 1)],
                                            a_sb[g][:, :, first_head + j, :], start=c == 0, stop=True,
                                            tile_position=(0, VH * j), skip_group_check=c > 0)
                    mix.complete(c, ins)
                ahead("z")
                variance(i, NC - 1)
                ahead("v")
                ev.wait(pe, "oglo", i)
                for m in range(KT):
                    linear(i, "o", wo, og_hl, m)
                ahead("g")

            parts = {"k0": keys, "k1": lambda i: linear(i, "k", wk, xa_hl, 1),
                     "q0": lambda i: linear(i, "q", wq, xa_hl, 0), "q1": lambda i: linear(i, "q", wq, xa_hl, 1),
                     "u": inner_gate, "z": key_gates, "v": value_rows, "g": output_gates}
            loop_parts(pe, NB, parts, body, before=lambda part: dense.skip(pe, late.get(part, []), -1),
                       skip=lambda part: dense.skip(pe, early[part], NB))

        return ev.at("xmid_out", NB - 1)


def phase_m(nc, consts, xmid_stored, shared, x, xmid_d, gate_d, W1, W3, W2, ln2_w, out):
    ident, avg_all, eps = consts[0], consts[4], consts[-1]
    NB, _, KT, T = xmid_d.shape
    D, F = W1.shape
    FT = F // P
    TT = T // P
    AHEAD = 2
    STAGES = 4
    ctx = ExitStack()
    with ctx:
        def sb(name, shape, dt=F32):
            return ctx.enter_context(nc.sbuf_tensor("m_" + name, shape, dt))[:]

        def pair(name, shape):
            return [sb(name + part, shape, F32R) for part in ("hi", "lo")]

        w1, w3 = pair("w1", [P, KT, F]), pair("w3", [P, KT, F])
        w2 = pair("w2", [P, FT, D])
        ln2 = sb("ln2", [P, KT])
        xres, xm, gate = shared
        xt = sb("xt", [P, TT, D])
        stage = [xt[:, n, :].rearrange("p (m n) -> p m n", n=P) for n in range(STAGES)]
        xs_hl = pair("xs", [P, KT, T])
        sq, sq_sum = [sb(f"sq{n}", [P, T]) for n in range(2)], sb("sq_sum", [P, T])
        r2 = sq_sum
        silu, h = [sb(f"silu{n}", [P, T]) for n in range(2)], [sb(f"h{n}", [P, T]) for n in range(2)]
        h_hl = [pair(f"h{n}", [P, T]) for n in range(2)]
        psum = [ctx.enter_context(nc.psum_tensor(f"m_ps{b}", [P, 512], F32))[:] for b in range(8)]

        ev = Events(nc, ctx, "m")
        for name, per in (("xm_in", 16), ("xres_in", 16), ("gate_in", 16), ("x_in", 16), ("out_out", 16), ("sq", KT),
                          ("sqsum", KT - 1), ("r2", 1), ("xs", KT), ("xshi", KT), ("xslo", KT), ("hhi", FT),
                          ("hlo", FT), ("w2", FT - 1), ("y", KT)):
            ev.add(name, per)
        mean = Slots(ev, "mean", psum[0:1], ["ms"])
        early = [f"{ab}{j}" for j in range(AHEAD) for ab in "ab"]
        late = [f"{ab}{j}" for j in range(AHEAD, FT) for ab in "ab"]
        turned = [f"t{t}" for t in range(TT)]
        dense = Slots(ev, "dense", psum[1:4], late + early + turned, early)
        acc = Slots(ev, "acc", psum[4:8], list(range(KT)))

        jobs = []
        for j in range(FT):
            cols = slice(j * P, (j + 1) * P)
            for w, parts in ((W1, w1), (W3, w3)):
                jobs.append((w[:, cols].rearrange("(kt p) n -> p kt n", p=P), ln2, *(a[:, :, cols] for a in parts)))
            jobs.append((W2[j * P:(j + 1) * P, :].rearrange("p (m n) -> p m n", n=P), None,
                         *(a[:, j, :].rearrange("p (m n) -> p m n", n=P) for a in w2)))
        s_ln2 = ctx.enter_context(nc.semaphore("m_ln2"))
        s_load = [ctx.enter_context(nc.semaphore(f"m_wload{n}")) for n in range(STAGES)]
        s_scaled, s_whi, s_wlo = (ctx.enter_context(nc.semaphore(f"m_w{n}")) for n in ("scaled", "hi", "lo"))
        block = ctx.enter_context(nc.Block())

        def scaled_so_far(n):
            return sum(scale is not None for _, scale, _, _ in jobs[:n + 1])

        @block.sync
        def _(sp):
            ev.give_credits(sp)
            sp.dma_start(ln2, ln2_w.rearrange("(m p) -> p m", p=P), allow_slow_non_contiguous=True).then_inc(s_ln2, 16)

            def load(i):
                ev.wait_before(sp, "xslo", i)
                ev.up_dma("xm_in", sp.dma_start(xm, row(xmid_d, i).rearrange("o p m t -> p (o m) t")))

            def weights(first, end):
                for n in range(first, end):
                    src = jobs[n][0]
                    if n >= STAGES:
                        sp.wait_ge(s_wlo, n - STAGES + 1)
                    sp.dma_start(stage[n % STAGES], src).then_inc(s_load[n % STAGES], 16)

            def body(i, ahead):
                ahead("xm")
                if isinstance(i, int) and i == 0:
                    weights(STAGES, len(jobs))
                    sp.wait_ge(*xmid_stored)
                sp.wait_ge(s_wlo, len(jobs))
                ev.wait_before(sp, "y", i)
                ev.up_dma("xres_in", sp.dma_start(xres, row(xmid_d, i).rearrange("o p m t -> p (o m) t")))
                dense.get_before(sp, f"t{TT - 1}", i)
                ev.up_dma("gate_in", sp.dma_start(gate, row(gate_d, i).rearrange("o p m t -> p (o m) t")))
                ev.wait_before(sp, "out_out", i)
                ev.up_dma("x_in", sp.dma_start(xt, row(x, i).rearrange("o (tt p) d -> p (o tt) d", p=P)))
                dense.wait_taken(sp, f"t{TT - 1}", i)
                ev.up_dma("out_out", sp.dma_start(row(out, i).rearrange("o (tt p) d -> p (o tt) d", p=P), xt))

            weights(0, STAGES)
            ev.landed("xm_in", sp)
            loop_parts(sp, NB, {"xm": load}, body, peel=True, first=False)
            ev.wait(sp, "out_out", NB - 1)

        @block.vector
        def _(dve):
            def weights(j):
                if j >= FT:
                    return
                for n in range(3 * j, 3 * j + 3):
                    _, scale, hi, lo = jobs[n]
                    if scale is not None:
                        dve.wait_ge(s_load[n % STAGES], 16 * (n // STAGES + 1))
                        dve.tensor_tensor(stage[n % STAGES], stage[n % STAGES], bcast(scale, 2, P),
                                          ALU.mult).then_inc(s_scaled, 1)
                for n in range(3 * j, 3 * j + 3):
                    _, scale, hi, lo = jobs[n]
                    dve.wait_ge(s_whi, n + 1)
                    dve.tensor_tensor(lo, stage[n % STAGES], hi.bitcast(F32), ALU.subtract).then_inc(s_wlo, 1)

            def scale(i):
                ev.wait(dve, "r2", i)
                for m in range(KT):
                    ev.up("xs", dve.tensor_tensor(xm[:, m, :], xm[:, m, :], r2, ALU.mult))

            def split(i):
                dense.get_before(dve, f"b{FT - 1}", i)
                for m in range(KT):
                    ev.wait(dve, "xs", i, m + 1)
                    ev.up("xshi", dve.tensor_copy(xs_hl[0][:, m, :], xm[:, m, :]))
                for m in range(KT):
                    ev.wait(dve, "xshi", i, m + 1)
                    ev.up("xslo", dve.tensor_tensor(xs_hl[1][:, m, :], xm[:, m, :],
                                                    xs_hl[0][:, m, :].bitcast(F32), ALU.subtract))

            def hidden(i, j):
                n = j % 2
                dense.wait_taken(dve, f"a{j}", i)
                dense.take(f"b{j}", dve.tensor_tensor(h[n], dense.get(dve, f"b{j}", i), silu[n], ALU.mult))
                ev.wait(dve, "hhi", i, j + 1)
                ev.up("hlo", dve.tensor_tensor(h_hl[n][1], h[n], h_hl[n][0].bitcast(F32), ALU.subtract))

            def first_hidden(i):
                for j in range(AHEAD):
                    hidden(i, j)

            def body(i, ahead):
                first = isinstance(i, int) and i == 0
                for j in range(AHEAD, FT):
                    if first:
                        weights(j + 1)
                    hidden(i, j)
                    if j == FT - 2:
                        ahead("scale")
                ahead("split")
                ev.wait(dve, "gate_in", i)
                ev.wait(dve, "xres_in", i)
                for m in range(KT):
                    acc.take(m, dve.tensor_tensor(xres[:, m, :], acc.get(dve, m, i), xres[:, m, :], ALU.add))
                for m in range(KT):
                    acc.wait_taken(dve, m, i)
                    ev.up("y", dve.tensor_tensor(gate[:, m, :], xres[:, m, :], gate[:, m, :], ALU.mult))
                ahead("hidden")
                ev.wait(dve, "x_in", i)
                for t in range(TT):
                    dense.take(f"t{t}", dve.tensor_tensor(xt[:, t, :], dense.get(dve, f"t{t}", i), xt[:, t, :],
                                                          ALU.add))

            def first_weights(_):
                dve.wait_ge(s_ln2, 16)
                for j in range(AHEAD + 1):
                    weights(j)

            parts = {"scale": scale, "split": split, "weights": first_weights, "hidden": first_hidden}
            loop_parts(dve, NB, parts, body, peel=True)

        @block.scalar
        def _(act):
            def weights(j):
                if j >= FT:
                    return
                for n in range(3 * j, 3 * j + 3):
                    _, scale, hi, _ = jobs[n]
                    if scale is not None:
                        act.wait_ge(s_scaled, scaled_so_far(n))
                    else:
                        act.wait_ge(s_load[n % STAGES], 16 * (n // STAGES + 1))
                    act.activation(hi, stage[n % STAGES], ACT.Copy).then_inc(s_whi, 1)

            def squares(i):
                ev.wait(act, "xm_in", i)
                for m in range(KT):
                    if m >= 2:
                        ev.wait(act, "sqsum", i, m - 1)
                    ev.up("sq", act.activation(sq[m % 2], xm[:, m, :], ACT.Square))

            def rms(i):
                act.preload_act_table_set(EXP_LN_SET)
                mean.take("ms", act.activation(r2, mean.get(act, "ms", i), ACT.Ln, bias=eps))
                mean.wait_taken(act, "ms", i)
                ev.up("r2", act.activation(r2, r2, ACT.Exp, scale=-0.5))
                act.preload_act_table_set(SILU_SET)

            def silu_part(i, j):
                n = j % 2
                if j >= 2:
                    dense.wait_taken(act, f"b{j - 2}", i)
                else:
                    dense.wait_taken_before(act, f"b{FT - 1}", i)
                dense.take(f"a{j}", act.activation(silu[n], dense.get(act, f"a{j}", i), ACT.Silu))

            def hi_part(i, j):
                n = j % 2
                dense.wait_taken(act, f"b{j}", i)
                if j >= 2:
                    ev.wait(act, "w2", i, j - 1)
                else:
                    acc.get_before(act, KT - 1, i)
                ev.up("hhi", act.activation(h_hl[n][0], h[n], ACT.Copy))

            def first_hidden(i):
                for j in range(AHEAD):
                    silu_part(i, j)
                for j in range(AHEAD):
                    hi_part(i, j)

            def body(i, ahead):
                first = isinstance(i, int) and i == 0
                for j in range(AHEAD, FT):
                    if first:
                        weights(j + 1)
                    silu_part(i, j)
                    hi_part(i, j)
                    if j == FT - 7:
                        ahead("squares")
                    if j == FT - 4:
                        ahead("rms")
                ahead("hidden")

            def first_weights(_):
                for j in range(AHEAD + 1):
                    weights(j)

            loop_parts(act, NB, {"squares": squares, "rms": rms, "weights": first_weights, "hidden": first_hidden}, body, peel=True)

        @block.gpsimd
        def _(pool):
            def add_squares(i, ahead):
                ev.wait_before(pool, "xs", i)
                ev.wait(pool, "sq", i, 2)
                ev.up("sqsum", pool.tensor_tensor(sq_sum, sq[0], sq[1], ALU.add))
                for m in range(2, KT):
                    ev.wait(pool, "sqsum", i, m - 1)
                    ev.wait(pool, "sq", i, m + 1)
                    ev.up("sqsum", pool.tensor_tensor(sq_sum, sq_sum, sq[m % 2], ALU.add))

            loop(pool, NB, nothing, add_squares)

        @block.tensor
        def _(pe):
            def mean_square(i):
                ps = mean.open(pe, "ms", i)
                ev.wait(pe, "sqsum", i)
                mean.complete("ms", pe.matmul(ps, avg_all, sq_sum, start=True, stop=True))

            def up(i, j):
                for n, (ab, w) in enumerate((("a", w1), ("b", w3))):
                    pe.wait_ge(s_wlo, 3 * j + n + 1)
                    ps = dense.open(pe, f"{ab}{j}", i)
                    for k in range(KT):
                        if j == 0 and n == 0:
                            ev.wait(pe, "xslo", i, k + 1)
                        wh, wl = (a[:, k, j * P:(j + 1) * P] for a in w)
                        xh, xl = (a[:, k, :] for a in xs_hl)
                        pe.matmul(ps, wh, xh, start=k == 0, stop=False)
                        pe.matmul(ps, wh, xl, start=False, stop=False)
                        ins = pe.matmul(ps, wl, xh, start=False, stop=k == KT - 1)
                    dense.complete(f"{ab}{j}", ins)

            def down(i, j):
                ev.wait(pe, "hlo", i, j + 1)
                pe.wait_ge(s_wlo, 3 * j + 3)
                n = j % 2
                for m in range(KT):
                    ps = acc.open(pe, m, i) if j == 0 else acc.regions[m]
                    lh, ll = (w[:, j, m * P:(m + 1) * P] for w in w2)
                    rh, rl = h_hl[n]
                    pe.matmul(ps, lh, rh, start=j == 0, stop=False)
                    pe.matmul(ps, lh, rl, start=False, stop=False)
                    ins = pe.matmul(ps, ll, rh, start=False, stop=j == FT - 1)
                    if j == FT - 1:
                        acc.complete(m, ins)
                if j < FT - 1:
                    ev.up("w2", ins)

            def first_up(i):
                for j in range(AHEAD):
                    up(i, j)

            def body(i, ahead):
                down(i, 0)
                for j in range(AHEAD, FT):
                    up(i, j)
                    down(i, j - 1)
                    if j == FT - 4:
                        ahead("ms")
                down(i, FT - 1)
                ahead("up")
                ev.wait(pe, "y", i)
                for t in range(TT):
                    ps = dense.open(pe, f"t{t}", i)
                    for m in range(KT):
                        ins = pe.transpose(ps[:, m * P:(m + 1) * P], gate[:, m, t * P:(t + 1) * P], ident)
                    dense.complete(f"t{t}", ins)

            def before(part):
                if part in ("up", "body"):
                    dense.skip(pe, {"up": late, "body": turned}[part], -1)

            def skip(part):
                if part == "up":
                    dense.skip(pe, early, NB)

            loop_parts(pe, NB, {"ms": mean_square, "up": first_up}, body, before=before, skip=skip)


_INS = ["L0_attn_x", "L0_attn_Wq", "L0_attn_Wk", "L0_attn_Wkg1", "L0_attn_Wkg2", "L0_attn_bkg2", "L0_attn_Wv",
        "L0_attn_Wg", "L0_attn_bg", "L0_attn_Wo", "L0_attn_ln1_w", "L0_attn_ln2_w", "L0_attn_W1", "L0_attn_W3",
        "L0_attn_W2", "L0_ffn_U", "L0_ffn_V", "L0_ffn_W1", "L0_ffn_b1", "L0_ffn_W2", "L0_ffn_b2"]


def build(nc, x, Wq, Wk, Wkg1, Wkg2, bkg2, Wv, Wg, bg, Wo, ln1_w, ln2_w, W1, W3, W2, U, V, fW1, fb1, fW2, fb2, out):
    NB, T, D = x.shape
    KT = D // P
    scratch = [nc.dram_tensor(f"scratch_{n}", (NB, P, KT, T), F32, kind="Internal").ap()
               for n in ("xn", "xa", "gate", "xmid")]
    xn_d, xa_d, gate_d, xmid_d = scratch
    with ExitStack() as ctx:
        consts = [ctx.enter_context(nc.sbuf_tensor(n, s, F32))[:] for n, s in (
            ("ident", [P, P]), ("hmask", [P, 8]), ("causal", [P, P]), ("avg32", [P, P]), ("avg_all", [P, P]),
            ("chunk_start", [P, T]), ("eps", [P, 1]))]
        make_constants(nc, consts)
        shared = [ctx.enter_context(nc.sbuf_tensor(n, [P, KT, T], F32))[:] for n in ("row0", "row1", "row2")]
        with ExitStack() as actx:
            aw = attention_weights(nc, actx, KT, D, Wk.shape[1])

            def background(sems, pool):
                prepare_attention_weights(nc, sems, pool, aw, Wq, Wk, Wkg1, Wkg2, bkg2, Wv, Wg, bg, Wo, ln1_w)

            gate_stored = phase_f(nc, ctx, background, consts, shared, x, U, V, fW1, fb1, fW2, fb2, xn_d, xa_d, gate_d)
            xmid_stored = phase_a(nc, ctx, consts, gate_stored, shared, aw, xn_d, xa_d, xmid_d)
        phase_m(nc, consts, xmid_stored, shared, x, xmid_d, gate_d, W1, W3, W2, ln2_w, out)


def kernel(**inputs):
    import numpy as _np
    import concourse.bacc as _bacc
    from concourse.bass_utils import run_bass_kernel_spmd as _run

    nc = _bacc.Bacc("TRN2", target_bir_lowering=False, num_devices=1)
    arrays, args = {}, []
    for name in _INS:
        a = _np.ascontiguousarray(inputs[name])
        arrays[f"in_{name}"] = a
        args.append(nc.dram_tensor(f"in_{name}", a.shape, mybir.dt.from_np(a.dtype), kind="ExternalInput").ap())
    shape = inputs["L0_attn_x"].shape
    out = nc.dram_tensor("out", shape, F32, kind="ExternalOutput").ap()
    build(nc, *args, out)
    r = _run(nc, [arrays], core_ids=[0])
    return r.results[0]["out"]
```

```python
from contextlib import ExitStack

import concourse.bass as bass
from concourse import mybir

F32 = mybir.dt.float32
F32R = mybir.dt.float32r
ALU = mybir.AluOpType
ACT = mybir.ActivationFunctionType
AX = mybir.AxisListType.X
EXP_LN_SET = "natural_log_exp_and_others"
SILU_SET = "silu_and_others"

P = 128
EPS = 1e-5
GATE_SCALE = 1.0 / 16.0


class Event:

    def __init__(self, sem, per):
        self.sem, self.per = sem, per


class Events:

    def __init__(self, nc, ctx, prefix):
        self.nc, self.ctx, self.prefix, self.all = nc, ctx, prefix, {}

    def add(self, name, per=1, ctx=None):
        assert name not in self.all
        self.all[name] = Event((ctx or self.ctx).enter_context(self.nc.semaphore(f"{self.prefix}_{name}")), per)

    def at(self, name, i, k=None):
        e = self.all[name]
        return e.sem, i * e.per + (e.per + (e.per if k is None else k))

    def at_before(self, name, i, k=None):
        e = self.all[name]
        return e.sem, i * e.per + (e.per if k is None else k)

    def wait(self, eng, name, i, k=None):
        eng.wait_ge(*self.at(name, i, k))

    def wait_before(self, eng, name, i, k=None):
        eng.wait_ge(*self.at_before(name, i, k))

    def up(self, name, ins):
        ins.then_inc(self.all[name].sem, 1)

    def up_dma(self, name, ins):
        ins.then_inc(self.all[name].sem, 16)

    def landed(self, name, eng):
        eng.sem_inc(self.all[name].sem, 16)

    def give_credits(self, eng):
        for e in self.all.values():
            eng.sem_inc(e.sem, e.per)


class Slots:

    def __init__(self, ev, name, regions, order, early=()):
        self.ev, self.name, self.regions = ev, name, regions
        self.where, used = {}, [0] * len(regions)
        for n, result in enumerate(order):
            r = n % len(regions)
            used[r] += 1
            self.where[result] = (r, used[r], 1 if early and result not in early else 0)
        for r, n in enumerate(used):
            ev.add(f"{name}{r}_ready", n)
            ev.add(f"{name}{r}_taken", n)

    def wait(self, eng, what, result, i, before=0):
        r, k, bodies = self.where[result]
        name = f"{self.name}{r}_{what}"
        per = self.ev.all[name].per
        self.ev.wait(eng, name, i, k + (bodies - before) * per)
        return self.regions[r]

    def open(self, pe, result, i):
        r, k, bodies = self.where[result]
        name = f"{self.name}{r}_taken"
        self.ev.wait(pe, name, i, k - 1 + bodies * self.ev.all[name].per)
        return self.regions[r]

    def complete(self, result, ins):
        self.ev.up(f"{self.name}{self.where[result][0]}_ready", ins)

    def get(self, eng, result, i):
        return self.wait(eng, "ready", result, i)

    def get_before(self, eng, result, i):
        self.wait(eng, "ready", result, i, 1)

    def take(self, result, ins):
        self.ev.up(f"{self.name}{self.where[result][0]}_taken", ins)

    def wait_taken(self, eng, result, i):
        self.wait(eng, "taken", result, i)

    def wait_taken_before(self, eng, result, i):
        self.wait(eng, "taken", result, i, 1)

    def skip(self, pe, results, i):
        for result in results:
            self.open(pe, result, i)
            for what in ("ready", "taken"):
                pe.sem_inc(self.ev.all[f"{self.name}{self.where[result][0]}_{what}"].sem, 1)


def bcast(ap, axis, n):
    shape = list(ap.shape)
    shape.insert(axis, n)
    return ap.unsqueeze(axis).broadcast_to(shape)


def product3(pe, out, terms, first=True, last=True):
    end = len(terms) - 1
    for n, ((lh, ll), (rh, rl)) in enumerate(terms):
        pe.matmul(out, lh, rh, start=first and n == 0, stop=False)
        pe.matmul(out, lh, rl, start=False, stop=False)
        ins = pe.matmul(out, ll, rh, start=False, stop=last and n == end)
    return ins


def loop(eng, n, first, body, peel=False):
    loop_parts(eng, n, {None: first}, lambda i, ahead: body(i, lambda: ahead(None)), peel)


def loop_parts(eng, n, parts, body, peel=False, before=None, skip=None, first=True):
    for part, work in parts.items() if first else ():
        if before:
            before(part)
        work(0)
    if before:
        before("body")
    if peel:
        body(0, lambda part: parts[part](1))
    with eng.Fori(1 if peel else 0, n - 1) as i:
        body(i, lambda part: parts[part](i + 1))
    body(n - 1, skip or (lambda part: None))


def nothing(i):
    pass


def row(dram, i):
    return dram[bass.ds(i, 1)]


def make_constants(nc, consts, D):
    with ExitStack() as ctx:
        s_fill = ctx.enter_context(nc.semaphore("s_fill"))
        block = ctx.enter_context(nc.Block())
        ident, hmask, causal, avg32, avg_all, ones, eps = consts

        @block.gpsimd
        def _(pool):
            n = 0

            def step(ins):
                nonlocal n
                n += 1
                ins.then_inc(s_fill, 1)
                pool.wait_ge(s_fill, n)

            def select(ap, op, base, pattern, cm, fill):
                step(pool.affine_select(out=ap, in_=ap, compare_op=op, fill=fill, base=base,
                                        pattern=pattern, channel_multiplier=cm))

            step(pool.memset(ident, 0.0))
            select(ident, ALU.not_equal, 0, [[-1, P]], 1, 1.0)
            step(pool.memset(hmask, 1.0))
            select(hmask, ALU.is_ge, 0, [[-16, 8]], 1, 0.0)
            select(hmask, ALU.is_ge, 15, [[16, 8]], -1, 0.0)
            step(pool.memset(causal, 1.0))
            select(causal, ALU.is_ge, 0, [[1, P]], -1, 0.0)
            step(pool.memset(avg32, 1.0 / 32))
            a = avg32.rearrange("p (a b) -> p a b", b=32)
            select(a, ALU.is_ge, 0, [[-32, 4], [0, 32]], 1, 0.0)
            select(a, ALU.is_ge, 31, [[32, 4], [0, 32]], -1, 0.0)
            step(pool.memset(avg_all, 1.0 / D))
            step(pool.memset(eps, EPS))
            step(pool.memset(ones, 1.0))


def flat(ap):
    return ap.rearrange("p a b -> p (a b)")


def attention_weights(nc, ctx, KT, D, KD, RANK):
    def sb(name, shape, dt=F32):
        return ctx.enter_context(nc.sbuf_tensor("a_" + name, shape, dt))[:]

    w = {name: [sb(name + part, [P, KT, n], F32R) for part in ("hi", "lo")]
         for name, n in (("wkg1", RANK), ("wk", KD), ("wq", KD), ("wv", D), ("wg", D), ("wo", D))}
    w["wkg2"] = sb("wkg2", [P, KD], F32R)
    for name, shape in (("bkg2", [P, KD // P]), ("bg", [P, KT]), ("ln1", [P, KT]),
                        ("stage", [P, 2, D]), ("fold", [P, D // 32, 16]), ("mean", [P, D // 32])):
        w[name] = sb(name, shape)
    return w


def prepare_attention_weights(nc, ctx, pool, w, Wq, Wk, Wkg1, Wkg2, bkg2, Wv, Wg, bg, Wo, ln1_w):
    s_small, s_step = (ctx.enter_context(nc.semaphore(f"aw_{n}")) for n in ("small", "step"))
    s_load = [ctx.enter_context(nc.semaphore(f"aw_load{n}")) for n in range(2)]
    steps = [0]

    def step(ins):
        steps[0] += 1
        ins.then_inc(s_step, 1)
        pool.wait_ge(s_step, steps[0])

    step(pool.memset(w["wkg2"].bitcast(F32), 0.0))
    RANK, KD = Wkg2.shape
    small = w["stage"][0:RANK, 1, 0:KD]
    pool.dma_start(small, Wkg2).then_inc(s_small, 16)
    for dst, src in ((w["bkg2"], bkg2), (w["bg"], bg), (w["ln1"], ln1_w)):
        pool.dma_start(dst, src.rearrange("(m p) -> p m", p=P), allow_slow_non_contiguous=True).then_inc(s_small, 16)
    sources = {"wkg1": Wkg1, "wk": Wk, "wq": Wq, "wv": Wv, "wg": Wg, "wo": Wo}
    jobs = [(name, src, kt) for name, src in sources.items() for kt in range(src.shape[0] // P)]

    def load(n):
        _, src, kt = jobs[n]
        pool.dma_start(w["stage"][:, n % 2, 0:src.shape[1]], src[kt * P:(kt + 1) * P, :]).then_inc(s_load[n % 2], 16)

    load(0)
    pool.wait_ge(s_small, 64)
    for at in (0, 32):
        step(pool.tensor_copy(w["wkg2"][at:at + RANK, :], small))
    step(pool.tensor_tensor(w["wkg2"][64:64 + RANK, :], small, w["wkg2"][0:RANK, :].bitcast(F32), ALU.subtract))
    for n, (name, src, kt) in enumerate(jobs):
        if n + 1 < len(jobs):
            load(n + 1)
        cols = src.shape[1]
        s = w["stage"][:, n % 2, 0:cols]
        pool.wait_ge(s_load[n % 2], 16 * (n // 2 + 1))
        if name == "wv":
            heads = s.rearrange("p (a b) -> p a b", b=32)
            step(pool.tensor_tensor(w["fold"][:, :, 0:16], heads[:, :, 0:16], heads[:, :, 16:32], ALU.add))
            for half in (8, 4, 2, 1):
                step(pool.tensor_tensor(w["fold"][:, :, 0:half], w["fold"][:, :, 0:half],
                                        w["fold"][:, :, half:2 * half], ALU.add))
            step(pool.tensor_scalar(w["mean"], w["fold"][:, :, 0], 1.0 / 32, None, ALU.mult))
            step(pool.tensor_tensor(heads, heads, bcast(w["mean"], 2, 32), ALU.subtract))
        if name != "wo":
            step(pool.tensor_scalar(s, s, w["ln1"][:, kt:kt + 1], None, ALU.mult))
        hi, lo = (part[:, kt, 0:cols] for part in w[name])
        step(pool.tensor_copy(hi, s))
        step(pool.tensor_tensor(lo, s, hi.bitcast(F32), ALU.subtract))


def phase_f(nc, outer, background, consts, shared, x, U, V, W1, b1, W2, b2, xn_d, r1_d, gate_d):
    ident, eps = consts[0], consts[-1]
    NB, T, D = x.shape
    KT, TT = D // P, T // P
    E, R = U.shape[0], U.shape[2]
    ctx = ExitStack()
    with ctx:
        def sb(name, shape, dt=F32):
            return ctx.enter_context(nc.sbuf_tensor("f_" + name, shape, dt))[:]

        w1 = [sb(f"w1{a}", [P, KT, D], F32R) for a in ("hi", "lo")]
        vt = [sb(f"vt{a}", [P, KT, E * R], F32R) for a in ("hi", "lo")]
        ut = [sb(f"ut{a}", [P, KT, D], F32R) for a in ("hi", "lo")]
        w2 = sb("w2", [P, KT, E])
        b1_sb, b2_sb = sb("b1", [P, KT]), sb("b2", [P, E])
        xt = sb("xt", [P, TT, D])
        xn, u_in, gate = shared
        xn_hl = [sb(f"xn{a}", [P, KT, T], F32R) for a in ("hi", "lo")]
        h1 = sb("h1", [P, KT, T])
        assert T == E * R == KT * P == TT * P
        alpha = h1
        vx = alpha_b = gate
        vx_hl = [sb(f"vx{a}", [P, KT, T], F32R) for a in ("hi", "lo")]
        stats, mv = sb("stats", [P, TT, 6]), sb("mv", [P, TT, 2])
        rstd, r1 = sb("rstd", [P, TT]), sb("r1", [P, TT])
        logit, top = sb("logit", [P, TT, E]), sb("top", [P, TT])
        psum = [ctx.enter_context(nc.psum_tensor(f"f_ps{b}", [P, 512], F32))[:] for b in range(8)]

        w1_in, v_in = h1, gate
        turned = [psum[n] for n in (0, 1, 2, 7)]
        s_w1, s_v, s_u, s_small, s_turned, s_whi, s_wlo, s_next = (
            ctx.enter_context(nc.semaphore(f"fw_{n}")) for n in ("w1", "v", "u", "small", "turned", "hi", "lo", "next"))
        w1_pieces = [(w1_in[:, k, :], w1[0][:, k, :], w1[1][:, k, :]) for k in range(KT)]
        vu_pieces = [(turned[m], w[0][:, m, :], w[1][:, m, :]) for w in (vt, ut) for m in range(KT)]

        ev = Events(nc, ctx, "f")
        for name, per in (("stats", TT), ("mv", TT), ("rstd", 2), ("m2", 2), ("r1", 2), ("norm", TT),
                          ("xnhi", KT), ("xnlo", KT), ("softmax", 4), ("exp", 1), ("alpha", 1), ("vxhi", KT),
                          ("vxlo", KT), ("x_in", 16), ("xn_out", 16), ("r1_out", 16)):
            ev.add(name, per)
        ev.add("gate_out", 16, outer)
        xn_parts, alphas, hs, vs, us = ([f"{n}{m}" for m in range(KT)] for n in ("xn", "alpha", "h", "v", "u"))
        turn = Slots(ev, "turn", psum[0:3], xn_parts + alphas, xn_parts)
        dense = Slots(ev, "dense", psum[3:8], ["logit"] + vs + hs + us, hs)
        LAST = KT - 1
        block = ctx.enter_context(nc.Block())

        @block.gpsimd
        def _(pool):
            background(ctx, pool)

        @block.sync
        def _(sp):
            ev.give_credits(sp)
            def load(i):
                turn.get_before(sp, f"xn{LAST}", i)
                ev.up_dma("x_in", sp.dma_start(xt, row(x, i).rearrange("o (tt p) d -> p (o tt) d", p=P)))

            def weights(_):
                sp.dma_start(w1_in, W1.rearrange("(k p) n -> p k n", p=P)).then_inc(s_w1, 16)
                sp.dma_start(b1_sb, b1.rearrange("(kt p) -> p kt", p=P),
                             allow_slow_non_contiguous=True).then_inc(s_small, 16)
                sp.dma_start(w2, W2.rearrange("(kt p) e -> p kt e", p=P)).then_inc(s_small, 16)
                sp.dma_start(b2_sb, b2.partition_broadcast(P)).then_inc(s_small, 16)
                sp.dma_start(v_in, V.rearrange("(m a) r d -> (a r) m d", a=P // R)).then_inc(s_v, 16)
                for m in range(KT):
                    sp.dma_start(u_in[:, m, :].rearrange("p (k r) -> p k r", r=R),
                                 U[:, m * P:(m + 1) * P, :].rearrange("k p r -> p k r")).then_inc(s_u, 16)

            def store_xn(i):
                turn.wait_taken(sp, f"xn{LAST}", i)
                ev.up_dma("xn_out", sp.dma_start(row(xn_d, i).rearrange("o p m t -> p (o m) t"), xn))

            def store_r1(i):
                ev.wait(sp, "r1", i)
                ev.up_dma("r1_out", sp.dma_start(row(r1_d, i).rearrange("o (t p) -> p (o t)", p=P), r1,
                                                 allow_slow_non_contiguous=True))

            def body(i, ahead):
                ahead("x")
                ahead("r1")
                ahead("xn")

            loop_parts(sp, NB, {"x": load, "weights": weights, "r1": store_r1, "xn": store_xn}, body)
            ev.wait(sp, "xn_out", NB - 1)
            ev.wait(sp, "r1_out", NB - 1)
            sp.dma_start(u_in, row(xn_d, 0).rearrange("o p m t -> p (o m) t")).then_inc(s_next, 16)
            sp.wait_ge(s_next, 16)

        @block.vector
        def _(dve):
            def norm(i):
                ev.wait(dve, "x_in", i)
                for t in range(TT):
                    ev.up("stats", dve.bn_stats(stats[:, t, :], xt[:, t, :]))
                ev.wait(dve, "stats", i)
                dve.memset(top, 0.0)
                for t in range(TT):
                    ev.up("mv", dve.bn_aggr(mv[:, t, :], stats[:, t, :]))
                ev.wait(dve, "rstd", i)
                ev.wait_before(dve, "r1_out", i)
                ev.up("m2", dve.tensor_tensor(r1, mv[:, :, 1], rstd, ALU.mult))
                ev.wait(dve, "m2", i, 1)
                ev.up("m2", dve.tensor_tensor(r1, r1, rstd, ALU.mult))
                for t in range(TT):
                    ev.up("norm", dve.tensor_scalar(xt[:, t, :], xt[:, t, :], mv[:, t, 0:1], rstd[:, t:t + 1],
                                                    ALU.subtract, ALU.mult))

            def split(i):
                dense.get_before(dve, f"v{LAST}", i)
                for m in range(KT):
                    turn.wait_taken(dve, f"xn{m}", i)
                    ev.up("xnhi", dve.tensor_copy(xn_hl[0][:, m, :], xn[:, m, :]))
                    ev.wait(dve, "xnhi", i, m + 1)
                    ev.up("xnlo", dve.tensor_tensor(xn_hl[1][:, m, :], xn[:, m, :],
                                                    xn_hl[0][:, m, :].bitcast(F32), ALU.subtract))

            def split_weights(pieces, first):
                for n, (src, hi, lo) in enumerate(pieces, first):
                    dve.wait_ge(s_whi, n + 1)
                    dve.tensor_tensor(lo, src, hi.bitcast(F32), ALU.subtract).then_inc(s_wlo, 1)

            def w1_parts(_):
                split_weights(w1_pieces, 0)

            def vu_parts(_):
                split_weights(vu_pieces, KT)
                dve.wait_ge(s_small, 48)

            def body(i, ahead):
                ahead("norm")
                lg = dense.get(dve, "logit", i)[:, 0:TT * E].rearrange("p (t e) -> p t e", e=E)
                dense.take("logit", dve.tensor_tensor(logit, lg, bcast(b2_sb, 1, TT), ALU.add))
                dense.wait_taken(dve, "logit", i)
                ev.up("softmax", dve.tensor_reduce(top, logit, AX, ALU.max))
                ev.wait(dve, "softmax", i, 1)
                ev.up("softmax", dve.tensor_tensor(logit, logit, bcast(top, 2, E), ALU.subtract))
                ev.wait(dve, "exp", i)
                ev.up("softmax", dve.tensor_reduce(top, logit, AX, ALU.add))
                ev.wait(dve, "softmax", i, 3)
                ev.up("softmax", dve.reciprocal(top, top))
                ev.wait(dve, "softmax", i, 4)
                ev.up("alpha", dve.tensor_tensor(alpha.rearrange("p t (e r) -> p t e r", r=R), bcast(logit, 3, R),
                                                 bcast(bcast(top, 2, E), 3, R), ALU.mult))
                ahead("split")
                dense.get_before(dve, f"u{LAST}", i)
                for m in range(KT):
                    turn.wait_taken(dve, f"alpha{m}", i)
                    dense.take(f"v{m}", dve.tensor_tensor(vx[:, m, :], dense.get(dve, f"v{m}", i), alpha_b[:, m, :],
                                                          ALU.mult))
                    dense.wait_taken(dve, f"v{m}", i)
                    ev.up("vxhi", dve.tensor_copy(vx_hl[0][:, m, :], vx[:, m, :]))
                    ev.wait(dve, "vxhi", i, m + 1)
                    ev.up("vxlo", dve.tensor_tensor(vx_hl[1][:, m, :], vx[:, m, :],
                                                    vx_hl[0][:, m, :].bitcast(F32), ALU.subtract))

            loop_parts(dve, NB, {"norm": norm, "w1": w1_parts, "split": split, "vu": vu_parts}, body)

        @block.scalar
        def _(act):
            def norm(i):
                act.preload_act_table_set(EXP_LN_SET)
                ev.wait(act, "mv", i)
                ev.up("rstd", act.activation(rstd, mv[:, :, 1], ACT.Ln, bias=eps))
                ev.wait(act, "rstd", i, 1)
                ev.up("rstd", act.activation(rstd, rstd, ACT.Exp, scale=-0.5))
                ev.wait(act, "m2", i)
                ev.up("r1", act.activation(r1, r1, ACT.Ln, bias=eps))
                ev.wait(act, "r1", i, 1)
                ev.up("r1", act.activation(r1, r1, ACT.Exp, scale=-0.5))

            def fill_xn(i):
                ev.wait_before(act, "xn_out", i)
                ev.wait_before(act, "xnlo", i)
                for m in range(KT):
                    turn.take(f"xn{m}", act.activation(xn[:, m, :], turn.get(act, f"xn{m}", i), ACT.Copy))

            def hidden(i):
                for m in range(KT):
                    dense.take(f"h{m}", act.activation(h1[:, m, :], dense.get(act, f"h{m}", i), ACT.Relu,
                                                       bias=b1_sb[:, m:m + 1]))

            def w1_parts(_):
                act.wait_ge(s_w1, 16)
                for src, hi, lo in w1_pieces:
                    act.activation(hi, src, ACT.Copy).then_inc(s_whi, 1)
                act.wait_ge(s_small, 48)

            def vu_parts(_):
                for n, (src, hi, lo) in enumerate(vu_pieces):
                    act.wait_ge(s_turned, n + 1)
                    act.activation(hi, src, ACT.Copy).then_inc(s_whi, 1)

            def body(i, ahead):
                ahead("norm")
                ev.wait(act, "softmax", i, 2)
                ev.up("exp", act.activation(logit, logit, ACT.Exp))
                ahead("xn")
                act.preload_act_table_set(SILU_SET)
                ev.wait_before(act, "gate_out", i)
                for m in range(KT):
                    turn.take(f"alpha{m}", act.activation(alpha_b[:, m, :], turn.get(act, f"alpha{m}", i), ACT.Copy))
                ahead("h")
                for m in range(KT):
                    dense.take(f"u{m}", act.activation(gate[:, m, :], dense.get(act, f"u{m}", i), ACT.Silu))
                dense.wait_taken(act, f"u{LAST}", i)
                ev.up_dma("gate_out", act.dma_start(row(gate_d, i).rearrange("o p m t -> p (o m) t"), gate))

            loop_parts(act, NB, {"norm": norm, "w1": w1_parts, "xn": fill_xn, "h": hidden, "vu": vu_parts},
                       body)
        @block.tensor
        def _(pe):
            def turn_weights(_):
                turn.wait_taken(pe, f"xn{LAST}", 0)
                for w, (s_in, need, src) in enumerate(((s_v, 16, v_in), (s_u, 16 * KT, u_in))):
                    pe.wait_ge(s_in, need)
                    for m in range(KT):
                        if w > 0:
                            pe.wait_ge(s_wlo, KT + m + 1)
                        for k in range(KT):
                            ins = pe.transpose(turned[m][:, k * P:(k + 1) * P], src[:, k, m * P:(m + 1) * P], ident)
                        ins.then_inc(s_turned, 1)
                pe.wait_ge(s_wlo, KT + len(vu_pieces))

            def turn_row(i):
                ev.wait(pe, "norm", i)
                for m in range(KT):
                    ps = turn.open(pe, f"xn{m}", i)
                    for t in range(TT):
                        ins = pe.transpose(ps[:, t * P:(t + 1) * P], xt[:, t, m * P:(m + 1) * P], ident)
                    turn.complete(f"xn{m}", ins)

            def linear(i, name, w, src, blocks, split=None):
                ps = [dense.open(pe, f"{name}{m}", i) for m in blocks]
                for k in range(KT):
                    if split:
                        ev.wait(pe, split, i, k + 1)
                    for n, m in enumerate(blocks):
                        ins = product3(pe, ps[n], [(tuple(a[:, k, m * P:(m + 1) * P] for a in w),
                                                    tuple(a[:, k, :] for a in src))], first=k == 0, last=k == LAST)
                        if k == LAST:
                            dense.complete(f"{name}{m}", ins)

            def hidden(i):
                linear(i, "h", w1, xn_hl, (0,), "xnlo")
                for m in range(1, KT):
                    linear(i, "h", w1, xn_hl, (m,))

            def body(i, ahead):
                dense.wait_taken(pe, f"h{LAST}", i)
                ps = dense.open(pe, "logit", i)
                for m in range(KT):
                    for t in range(2 * m, min(2 * m + 2, TT)):
                        for k in range(KT):
                            ins = pe.matmul(ps[:, t * E:(t + 1) * E], h1[:, k, t * P:(t + 1) * P], w2[:, k, :],
                                            start=k == 0, stop=k == LAST)
                        if t == TT - 1:
                            dense.complete("logit", ins)
                    linear(i, "v", vt, xn_hl, (m,))
                    if m == 1:
                        ahead("xn")
                ev.wait(pe, "alpha", i)
                for m in range(KT):
                    ps = turn.open(pe, f"alpha{m}", i)
                    for t in range(TT):
                        ins = pe.transpose(ps[:, t * P:(t + 1) * P], alpha[:, t, m * P:(m + 1) * P], ident)
                    turn.complete(f"alpha{m}", ins)
                ahead("h")
                linear(i, "u", ut, vx_hl, (0,), "vxlo")
                for m in range(1, KT):
                    linear(i, "u", ut, vx_hl, (m,))

            parts = {"xn": turn_row, "h": hidden, "vu": turn_weights}

            def before(part):
                if part == "h":
                    pe.wait_ge(s_wlo, KT)
                    turn.skip(pe, alphas, -1)
                if part in ("h", "body"):
                    dense.skip(pe, {"h": ["logit"] + vs, "body": us}[part], -1)

            def skip(part):
                slots, results = {"xn": (turn, xn_parts), "h": (dense, hs)}[part]
                slots.skip(pe, results, NB)

            loop_parts(pe, NB, parts, body, before=before, skip=skip)

        return ev.at("gate_out", NB - 1)


def phase_a(nc, outer, consts, gate_stored, shared, w, xn_d, r1_d, xmid_d):
    ident, hmask, causal, avg32, _, ones, eps = consts
    NB, _, KT, T = xn_d.shape
    D = KT * P
    KD = w["wkg2"].shape[1]
    GR = KD // P
    NC = T // P
    KH, VH = 16, 32
    HG = P // KH
    QD = D // P
    HQ = P // VH
    H64, H32 = P // 2, P // 4
    ctx = ExitStack()
    with ctx:
        def sb(name, shape, dt=F32):
            return ctx.enter_context(nc.sbuf_tensor("a_" + name, shape, dt))[:]

        def pair(name, shape):
            return [sb(name + part, shape, F32R) for part in ("hi", "lo")]

        wkg1, wq, wk, wv, wg, wo = (w[name] for name in ("wkg1", "wq", "wk", "wv", "wg", "wo"))
        RANK = wkg1[0].shape[2]
        wkg2, bkg2_sb, bg_sb = w["wkg2"], w["bkg2"], w["bg"]
        xn, xa, gsilu = shared
        xa_hl = pair("xa", [P, KT, T])
        r1 = sb("r1", [P, T])
        u = sb("u", [P, T], F32R)
        shape = [P, GR * NC, P]
        k_sb, q_sb = flat(w["stage"]).rearrange("p (c t) -> p c t", t=P), sb("q", shape)
        neg, soft, cum = sb("neg", shape), sb("soft", shape), sb("cum", shape)
        lv64, lv32, dq, dk = sb("lv64", shape), sb("lv32", shape), sb("dq", shape), sb("dk", shape)
        khat, qhat = soft, neg
        decay = sb("decay", [P, GR * NC])
        v_tok = sb("v_tok", [P, NC, D])
        qx64 = [sb(f"qx64_{g}", [P, HG, H64]) for g in range(GR)]
        qx32 = [sb(f"qx32_{g}", [P, 2, HG, H32]) for g in range(GR)]
        qxd = [sb(f"qxd_{g}", [P, 4, HG, H32]) for g in range(GR)]
        a_sb = [sb(f"a{g}", [P, 2, HG, H64]) for g in range(GR)]
        kt_sb = flat(w["fold"]).rearrange("p (g t) -> p g t", g=GR)
        state = [sb(f"state{n}", [P, GR, HG * VH]) for n in range(2)]
        sq, oc, rn = sb("sq", [P, QD, P]), sb("oc", [P, QD, P]), sb("rn", [P, QD, P])
        og_hl = pair("og", [P, KT, T])
        psum = [ctx.enter_context(nc.psum_tensor(f"a_ps{b}", [P, 512], F32))[:] for b in range(4)]
        ps_att = [ctx.enter_context(nc.psum_tensor(f"a_att{g}", [P, 2, HG, H64], F32))[:] for g in range(2)]

        ev = Events(nc, ctx, "a")
        for name, per in (("xa_in", 32), ("xn_in", 16), ("xa", KT), ("xahi", KT), ("xalo", KT), ("uhi", 2),
                          ("absz", GR),
                          ("expz", GR), ("softz", GR), ("logg", GR), ("cum", GR * NC), ("offs", 3),
                          ("offk", 1), ("e64", 2), ("e32", 2), ("edk", 1), ("edq", 1), ("ekh", 1), ("eqh", 1),
                          ("decay", 1), ("m64", 2), ("m32", 2), ("mdk", 1), ("mdq", 1), ("mkh", 1), ("mqh", 1),
                          ("qxs", 2 * GR * NC), ("qxd", GR * NC), ("state", GR * (NC - 2)),
                          ("sq", NC), ("rn", NC), ("og", 2 * NC), ("oghi", NC), ("oglo", NC)):
            ev.add(name, per)
        ev.add("xmid_out", 16, outer)
        zs, values = [f"z{g}" for g in range(GR)], [f"v{c}" for c in range(NC)]
        gates, outs = [f"g{m}" for m in range(KT)], [f"o{m}" for m in range(KT)]
        assert GR == 2 and NC == 4
        order = [(None, ["kt0"]), ("k0", ["k0"]), (None, ["ds0", "kt1"]), ("k1", ["k1"]),
                 (None, ["ds1", "var0", "kt2"]), ("q0", ["q0"]), ("q1", ["q1"]), (None, ["ds2", "var1"]),
                 ("u", ["u"]), (None, ["var2"]), ("z", zs), ("v0", values[:1]),
                 (None, ["var3"]), ("v1", values[1:]), ("g", gates),
                 (None, outs), ("body", [])]
        early = {part: results for part, results in order if part}
        late = {order[n + 1][0]: results for n, (part, results) in enumerate(order) if not part}
        dense = Slots(ev, "dense", psum[0:3], sum((results for _, results in order), []), sum(early.values(), []))
        att = Slots(ev, "att", ps_att, [f"{c}_{g}" for c in range(NC) for g in range(GR)])
        mix = Slots(ev, "mix", psum[3:4], list(range(NC)))
        LAST = KT - 1
        s_next = ctx.enter_context(nc.semaphore("a_next"))
        block = ctx.enter_context(nc.Block())

        def tokens(c):
            return slice(c * P, (c + 1) * P)

        @block.sync
        def _(sp):
            ev.give_credits(sp)

            def load_r1(i):
                ev.up_dma("xa_in", sp.dma_start(r1, row(r1_d, i).rearrange("o t -> (o t)").partition_broadcast(P)))

            def load(i):
                ev.wait_before(sp, "xalo", i)
                ev.up_dma("xa_in", sp.dma_start(xa, row(xn_d, i).rearrange("o p m t -> p (o m) t")))
                load_r1(i)

            def body(i, ahead):
                ahead("xa")
                ev.wait_before(sp, "xmid_out", i)
                ev.up_dma("xn_in", sp.dma_start(xn, row(xn_d, i).rearrange("o p m t -> p (o m) t")))
            def next_phase(_):
                ev.wait(sp, "xalo", NB - 1)
                sp.dma_start(xa, row(xmid_d, 0).rearrange("o p m t -> p (o m) t")).then_inc(s_next, 16)

            ev.landed("xa_in", sp)
            load_r1(0)
            loop_parts(sp, NB, {"xa": load}, body, skip=next_phase, first=False)
            sp.wait_ge(s_next, 16)

        @block.vector
        def _(dve):
            def split(i):
                for m in range(KT):
                    ev.wait(dve, "xahi", i, m + 1)
                    ev.up("xalo", dve.tensor_tensor(xa_hl[1][:, m, :], xa[:, m, :],
                                                    xa_hl[0][:, m, :].bitcast(F32), ALU.subtract))

            def spread_d(i, c, g):
                gc = g * NC + c
                q = dq[:, gc, :].rearrange("p (b t) -> p b t", t=H32)
                ev.up("qxd", dve.tensor_tensor(qxd[g], bcast(q, 2, HG), bcast(bcast(hmask, 1, 4), 3, H32), ALU.mult))

            def inner_gate(i):
                ps = dense.get(dve, "u", i)[0:RANK]
                ev.up("uhi", dve.tensor_copy(u[0:RANK], ps))
                ev.up("uhi", dve.tensor_copy(u[64:64 + RANK], ps))
                ev.wait(dve, "uhi", i)
                dense.take("u", dve.tensor_tensor(u[32:32 + RANK], ps, u[0:RANK].bitcast(F32), ALU.subtract))

            def sum_gates(i):
                def group(buf, g):
                    return flat(buf[:, g * NC:(g + 1) * NC, :])

                for g in range(GR):
                    ev.wait(dve, "absz", i, g + 1)
                    dense.take(f"z{g}", dve.tensor_scalar(group(neg, g), dense.get(dve, f"z{g}", i),
                                                          bkg2_sb[:, g:g + 1], 0.0, ALU.add, ALU.min))
                for g in range(GR):
                    dense.wait_taken(dve, f"z{g}", i)
                    ev.wait(dve, "softz", i, g + 1)
                    ev.up("logg", dve.tensor_tensor(group(neg, g), group(neg, g), group(soft, g), ALU.subtract))
                    ev.wait(dve, "logg", i, g + 1)
                    for gc in range(g * NC, (g + 1) * NC):
                        ev.up("cum", dve.tensor_tensor_scan(cum[:, gc, :], ones, neg[:, gc, :], 0.0, ALU.mult,
                                                            ALU.add))
                ev.wait(dve, "cum", i)
                for dst, n, ref in ((lv64, P, H64 - 1), (lv32, H64, H32 - 1), (dq, H32, H32 // 2 - 1)):
                    cv = flat(cum).rearrange("p (b t) -> p b t", t=n)
                    dv = flat(dst).rearrange("p (b t) -> p b t", t=n)
                    at = cv[:, :, ref]
                    ev.up("offs", dve.tensor_tensor(dv, cv, bcast(at, 2, n), ALU.subtract))

            def weigh_upper(i):
                dense.wait_taken(dve, f"q{GR - 1}", i)
                for name, buf, n in (("64", lv64, P), ("32", lv32, H64)):
                    for part, src in ((0, k_sb), (1, q_sb)):
                        b = flat(buf).rearrange("p (b a t) -> p b a t", a=2, t=n // 2)[:, :, part, :]
                        s = flat(src).rearrange("p (b a t) -> p b a t", a=2, t=n // 2)[:, :, part, :]
                        ev.wait(dve, "e" + name, i, part + 1)
                        ev.up("m" + name, dve.tensor_tensor(b, b, s, ALU.mult))

            def weigh_last(i):
                ev.wait(dve, "edk", i)
                ev.up("mdk", dve.tensor_tensor(dk, dk, k_sb, ALU.mult))
                ev.wait(dve, "edq", i)
                ev.up("mdq", dve.tensor_tensor(dq, dq, q_sb, ALU.mult))

            def first_spread(i):
                ev.wait(dve, "mdq", i)
                for g in range(GR):
                    spread_d(i, 0, g)

            def clear(_):
                dve.memset(u.bitcast(F32), 0.0)
                for ps in ps_att:
                    for half in range(2):
                        dve.memset(ps[:, half], 0.0)

            def body(i, ahead):
                ahead("split")
                for c in range(NC):
                    if c > 0:
                        mix.get(dve, c - 1, i)
                    for g in range(GR):
                        ps = att.get(dve, f"{c}_{g}", i)
                        cz = causal.rearrange("p (a t) -> p a t", a=2)
                        att.take(f"{c}_{g}", dve.tensor_tensor(a_sb[g], ps, bcast(cz, 2, HG), ALU.mult))
                        if c + 1 < NC:
                            spread_d(i, c + 1, g)
                    if c + 1 < NC:
                        new, old = state[(c + 1) % 2], state[c % 2]
                        ds = dense.get(dve, f"ds{c}", i).rearrange("p (g h v) -> p g h v", g=GR, v=VH)
                        dense.take(f"ds{c}", dve.tensor_tensor(new.rearrange("p g (h v) -> p g h v", v=VH), ds,
                                                               bcast(bcast(hmask, 1, GR), 3, VH), ALU.mult))
                        dense.wait_taken(dve, f"ds{c}", i)
                        if c > 0:
                            ev.wait(dve, "decay", i)
                            for g in range(GR):
                                gc = g * NC + c
                                ev.up("state", dve.scalar_tensor_tensor(new[:, g, :], old[:, g, :],
                                                                        decay[:, gc:gc + 1], new[:, g, :],
                                                                        ALU.mult, ALU.add))
                            ev.wait(dve, "state", i, GR * c)
                    else:
                        ahead("u")
                    if c > 0:
                        gated(i, c - 1)
                ahead("gates")
                gated(i, NC - 1)
                ahead("upper")
                ahead("last")
                ahead("spread")
                ev.wait(dve, "xn_in", i)
                for m in range(KT):
                    dense.take(f"o{m}", dve.tensor_tensor(xn[:, m, :], dense.get(dve, f"o{m}", i), xn[:, m, :],
                                                          ALU.add))

            def gated(i, c):
                ev.wait(dve, "rn", i, c + 1)
                ev.up("og", dve.tensor_tensor(rn, rn, oc, ALU.mult))
                dense.wait_taken(dve, f"g{LAST}", i)
                ev.wait(dve, "og", i, 2 * c + 1)
                ev.up("og", dve.tensor_tensor(rn, rn, gsilu[:, :, tokens(c)], ALU.mult))
                ev.wait(dve, "og", i, 2 * c + 2)
                ev.up("oghi", dve.tensor_copy(og_hl[0][:, :, tokens(c)], rn))
                ev.wait(dve, "oghi", i, c + 1)
                ev.up("oglo", dve.tensor_tensor(og_hl[1][:, :, tokens(c)], rn,
                                                og_hl[0][:, :, tokens(c)].bitcast(F32), ALU.subtract))

            loop_parts(dve, NB, {"clear": clear, "split": split, "u": inner_gate, "gates": sum_gates,
                                 "upper": weigh_upper, "last": weigh_last, "spread": first_spread}, body)

        @block.gpsimd
        def _(pool):
            def spread(i, c, g):
                gc = g * NC + c
                ev.up("qxs", pool.tensor_tensor(qx64[g], bcast(lv64[:, gc, H64:P], 1, HG), bcast(hmask, 2, H64),
                                                ALU.mult))
                q = lv32[:, gc, :].rearrange("p (b a t) -> p b a t", a=2, t=H32)[:, :, 1, :]
                ev.up("qxs", pool.tensor_tensor(qx32[g], bcast(q, 2, HG), bcast(bcast(hmask, 1, 2), 3, H32),
                                                ALU.mult))

            def scale(i):
                ev.wait(pool, "xa_in", i)
                for m in range(KT):
                    ev.up("xa", pool.tensor_tensor(xa[:, m, :], xa[:, m, :], r1, ALU.mult))

            def body(i, ahead):
                ev.wait(pool, "cum", i)
                ev.up("offk", pool.tensor_tensor(khat, cum, bcast(cum[:, :, P - 1], 2, P), ALU.subtract))
                ev.wait(pool, "m64", i)
                ev.wait(pool, "m32", i)
                for g in range(GR):
                    spread(i, 0, g)
                dense.wait_taken(pool, f"q{GR - 1}", i)
                ev.wait(pool, "ekh", i)
                ev.up("mkh", pool.tensor_tensor(khat, khat, k_sb, ALU.mult))
                ev.wait(pool, "eqh", i)
                ev.up("mqh", pool.tensor_tensor(qhat, qhat, q_sb, ALU.mult))
                ahead("scale")
                for c in range(1, NC):
                    for g in range(GR):
                        att.get(pool, f"{c - 1}_{g}", i)
                        spread(i, c, g)

            loop_parts(pool, NB, {"scale": scale}, body)

        @block.scalar
        def _(act):
            def half(buf, n, part):
                return flat(buf).rearrange("p (b a t) -> p b a t", a=2, t=n // 2)[:, :, part, :]

            def split(i):
                dense.get_before(act, f"g{LAST}", i)
                for m in range(KT):
                    ev.wait(act, "xa", i, m + 1)
                    ev.up("xahi", act.activation(xa_hl[0][:, m, :], xa[:, m, :], ACT.Copy))

            def fill(name, buf, g, scale):
                def part(i):
                    dense.take(f"{name}{g}", act.activation(flat(buf[:, g * NC:(g + 1) * NC, :]),
                                                            dense.get(act, f"{name}{g}", i), ACT.Copy, scale=scale))
                return part

            def soft_gates(i):
                def group(g):
                    return flat(soft[:, g * NC:(g + 1) * NC, :])

                for g in range(GR):
                    ps = dense.get(act, f"z{g}", i)
                    ev.up("absz", act.activation(group(g), ps, ACT.Abs, bias=bkg2_sb[:, g:g + 1]))
                for g in range(GR):
                    ev.wait(act, "absz", i, g + 1)
                    ev.up("expz", act.activation(group(g), group(g), ACT.Exp, scale=-1.0))
                    ev.wait(act, "expz", i, g + 1)
                    ev.up("softz", act.activation(group(g), group(g), ACT.Ln, bias=1.0))

            def value(i, c):
                dense.take(f"v{c}", act.activation(v_tok[:, c, :], dense.get(act, f"v{c}", i), ACT.Copy))

            def exponentials(i):
                for n, (name, buf, length) in enumerate((("e64", lv64, P), ("e32", lv32, H64))):
                    ev.wait(act, "offs", i, n + 1)
                    for part, sign in ((0, -1), (1, 1)):
                        b = half(buf, length, part)
                        ev.up(name, act.activation(b, b, ACT.Exp, scale=sign * GATE_SCALE))
                    if n > 0:
                        value(i, n)
                ev.wait(act, "offs", i, 3)
                ev.up("edk", act.activation(dk, dq, ACT.Exp, scale=-GATE_SCALE))
                ev.wait(act, "edk", i)
                ev.up("edq", act.activation(dq, dq, ACT.Exp, scale=GATE_SCALE))
                value(i, 2)
                ev.wait(act, "offk", i)
                ev.up("ekh", act.activation(khat, khat, ACT.Exp, scale=-GATE_SCALE))
                value(i, 3)
                ev.up("eqh", act.activation(qhat, cum, ACT.Exp, scale=GATE_SCALE))
                ev.up("decay", act.activation(decay, cum[:, :, P - 1], ACT.Exp, scale=GATE_SCALE))

            def output_gate(i):
                act.preload_act_table_set(SILU_SET)
                if isinstance(i, int) and i == 0:
                    act.wait_ge(*gate_stored)
                ev.wait_before(act, "oglo", i)
                for m in range(KT):
                    dense.take(f"g{m}", act.activation(gsilu[:, m, :], dense.get(act, f"g{m}", i), ACT.Silu,
                                                       bias=bg_sb[:, m:m + 1]))
                act.preload_act_table_set(EXP_LN_SET)

            def body(i, ahead):
                ahead("split")
                for c in range(NC):
                    if c + 1 < NC:
                        dense.take(f"kt{c}", act.activation(flat(kt_sb), dense.get(act, f"kt{c}", i)[:, 0:GR * P],
                                                            ACT.Copy))
                    for part in (("k0",), ("k1",), ("q0", "q1"), ())[c]:
                        ahead(part)
                    if c > 0:
                        inverse_deviation(i, c - 1)
                    ps = mix.get(act, c, i)
                    ev.up("sq", act.activation(flat(sq), ps, ACT.Square))
                    if c > 0:
                        ev.wait(act, "og", i, 2 * (c - 1) + 1)
                    mix.take(c, act.activation(flat(oc), ps, ACT.Copy))
                ahead("z")
                ahead("v0")
                inverse_deviation(i, NC - 1)
                ahead("exponentials")
                ahead("g")
                dense.wait_taken(act, f"o{LAST}", i)
                ev.up_dma("xmid_out", act.dma_start(row(xmid_d, i).rearrange("o p m t -> p (o m) t"), xn))

            def inverse_deviation(i, c):
                ps = dense.get(act, f"var{c}", i)
                if c > 0:
                    ev.wait(act, "oglo", i, c)
                dense.take(f"var{c}", act.activation(flat(rn), ps, ACT.Ln, bias=eps))
                dense.wait_taken(act, f"var{c}", i)
                ev.up("rn", act.activation(rn, rn, ACT.Exp, scale=-0.5))

            parts = {"split": split}
            for name, buf, scale in (("k", k_sb, VH ** -0.5), ("q", q_sb, 1.0)):
                for g in range(GR):
                    parts[f"{name}{g}"] = fill(name, buf, g, scale)
            parts.update({"z": soft_gates, "v0": lambda i: value(i, 0), "exponentials": exponentials, "g": output_gate})
            act.preload_act_table_set(EXP_LN_SET)
            loop_parts(act, NB, parts, body)

        @block.tensor
        def _(pe):
            def linear(i, name, w, src, m):
                ps = dense.open(pe, f"{name}{m}", i)
                dense.complete(f"{name}{m}", product3(pe, ps, [
                    (tuple(a[:, k, m * P:(m + 1) * P] for a in w), tuple(a[:, k, :] for a in src)) for k in range(KT)]))

            def weights(i, c, g):
                gc = g * NC + c
                ps = att.open(pe, f"{c}_{g}", i)
                ev.wait(pe, "m64", i)
                ev.wait(pe, "m32", i)
                ev.wait(pe, "mdk", i)
                ev.wait(pe, "qxs", i, 2 * (GR * c + g) + 2)
                ev.wait(pe, "qxd", i, GR * c + g + 1)

                def block_product(s, half, at, n, keys, q):
                    return pe.matmul(ps[s:s + H32, half, :, at:at + n], keys[:, gc, s:s + H32], q, start=True,
                                     stop=True, tile_position=(0, s))

                for s in (0, H32):
                    block_product(s, 1, 0, H64, lv64, qx64[g])
                for b in range(2):
                    block_product(H64 * b, b, H32, H32, lv32, qx32[g][:, b])
                for b in range(4):
                    ins = block_product(H32 * b, b // 2, H32 * (b % 2), H32, dk, qxd[g][:, b])
                att.complete(f"{c}_{g}", ins)

            def variance(i, c):
                ev.wait(pe, "sq", i, c + 1)
                ps = dense.open(pe, f"var{c}", i)
                dense.complete(f"var{c}", pe.matmul(ps, avg32, flat(sq), start=True, stop=True))

            def keys(i):
                ps = dense.open(pe, "k0", i)
                for k in range(KT):
                    ev.wait(pe, "xalo", i, k + 1)
                    ins = product3(pe, ps, [(tuple(a[:, k, 0:P] for a in wk), tuple(a[:, k, :] for a in xa_hl))],
                                   first=k == 0, last=k == LAST)
                dense.complete("k0", ins)

            def inner_gate(i):
                ps = dense.open(pe, "u", i)
                dense.complete("u", product3(pe, ps[0:RANK], [
                    (tuple(a[:, k, :] for a in wkg1), tuple(a[:, k, :] for a in xa_hl)) for k in range(KT)]))

            def key_gates(i):
                dense.wait_taken(pe, "u", i)
                for g in range(GR):
                    ps = dense.open(pe, f"z{g}", i)
                    dense.complete(f"z{g}", pe.matmul(ps, wkg2[:, g * P:(g + 1) * P], u, start=True, stop=True))

            def value_rows(i, chunks):
                for c in chunks:
                    ps = dense.open(pe, f"v{c}", i)
                    dense.complete(f"v{c}", product3(pe, ps, [
                        (tuple(a[:, k, tokens(c)] for a in xa_hl), tuple(a[:, k, :] for a in wv)) for k in range(KT)]))

            def output_gates(i):
                for m in range(KT):
                    linear(i, "g", wg, xa_hl, m)

            def body(i, ahead):
                for g in range(GR):
                    weights(i, 0, g)
                for c in range(NC):
                    gcs = [g * NC + c for g in range(GR)]
                    if c + 1 < NC:
                        ev.wait(pe, "mkh", i)
                        ps = dense.open(pe, f"kt{c}", i)
                        for g in range(GR):
                            ins = pe.transpose(ps[:, g * P:(g + 1) * P], khat[:, gcs[g], :], ident)
                        dense.complete(f"kt{c}", ins)
                        for part in (("k0",), ("k1",), ("q0", "q1"))[c]:
                            ahead(part)
                        for g in range(GR):
                            weights(i, c + 1, g)
                        dense.wait_taken(pe, f"kt{c}", i)
                        ps = dense.open(pe, f"ds{c}", i)
                        for g in range(GR):
                            n = HG * VH
                            ins = pe.matmul(ps[:, g * n:(g + 1) * n], kt_sb[:, g, :], v_tok[:, c, g * n:(g + 1) * n],
                                            start=True, stop=True)
                        dense.complete(f"ds{c}", ins)
                    if c + 1 == NC:
                        ahead("u")
                    if c > 0:
                        variance(i, c - 1)
                    ps = mix.open(pe, c, i).rearrange("p (q t) -> p q t", t=P)
                    for g in range(GR):
                        att.wait_taken(pe, f"{c}_{g}", i)
                    if c > 0:
                        ev.wait(pe, "mqh", i)
                    if c == 1:
                        dense.wait_taken(pe, "ds0", i)
                    if c > 1:
                        ev.wait(pe, "state", i, GR * (c - 1))
                    for quad in range(QD):
                        g, first_head = quad * HQ // HG, quad * HQ % HG
                        if c > 0:
                            pe.matmul(ps[:, quad, :], state[c % 2][:, g, first_head * VH:(first_head + HQ) * VH],
                                      qhat[:, gcs[g], :], start=True, stop=True, skip_group_check=True)
                        for j in range(HQ):
                            h = quad * HQ + j
                            ins = pe.matmul(ps[VH * j:VH * (j + 1), quad, :], v_tok[:, c, VH * h:VH * (h + 1)],
                                            a_sb[g][:, :, first_head + j, :], start=c == 0, stop=True,
                                            tile_position=(0, VH * j), skip_group_check=c > 0)
                    mix.complete(c, ins)
                ahead("z")
                ahead("v0")
                variance(i, NC - 1)
                ahead("v1")
                ahead("g")
                ev.wait(pe, "oglo", i)
                for m in range(KT):
                    linear(i, "o", wo, og_hl, m)

            parts = {"k0": keys, "k1": lambda i: linear(i, "k", wk, xa_hl, 1),
                     "q0": lambda i: linear(i, "q", wq, xa_hl, 0), "q1": lambda i: linear(i, "q", wq, xa_hl, 1),
                     "u": inner_gate, "z": key_gates, "v0": lambda i: value_rows(i, range(1)),
                     "v1": lambda i: value_rows(i, range(1, NC)), "g": output_gates}
            loop_parts(pe, NB, parts, body, before=lambda part: dense.skip(pe, late.get(part, []), -1),
                       skip=lambda part: dense.skip(pe, early[part], NB))

        return ev.at("xmid_out", NB - 1)


def phase_m(nc, consts, xmid_stored, shared, x, xmid_d, gate_d, W1, W3, W2, ln2_w, out):
    ident, avg_all, eps = consts[0], consts[4], consts[-1]
    NB, _, KT, T = xmid_d.shape
    D, F = W1.shape
    FT = F // P
    TT = T // P
    AHEAD = 2
    STAGES = 4
    ctx = ExitStack()
    with ctx:
        def sb(name, shape, dt=F32):
            return ctx.enter_context(nc.sbuf_tensor("m_" + name, shape, dt))[:]

        def pair(name, shape):
            return [sb(name + part, shape, F32R) for part in ("hi", "lo")]

        w1, w3 = pair("w1", [P, KT, F]), pair("w3", [P, KT, F])
        w2 = pair("w2", [P, FT, D])
        ln2 = sb("ln2", [P, KT])
        xres, xm, gate = shared
        xt = sb("xt", [P, TT, D])
        stage = [xt[:, n, :].rearrange("p (m n) -> p m n", n=P) for n in range(STAGES)]
        xs_hl = pair("xs", [P, KT, T])
        sq, sq_sum = [sb(f"sq{n}", [P, T]) for n in range(2)], sb("sq_sum", [P, T])
        r2 = sq_sum
        silu, h = [sb(f"silu{n}", [P, T]) for n in range(2)], [sb(f"h{n}", [P, T]) for n in range(2)]
        h_hl = [pair(f"h{n}", [P, T]) for n in range(2)]
        psum = [ctx.enter_context(nc.psum_tensor(f"m_ps{b}", [P, 512], F32))[:] for b in range(8)]

        ev = Events(nc, ctx, "m")
        for name, per in (("xm_in", 16), ("xres_in", 16), ("gate_in", 16), ("x_in", 16), ("out_out", 16), ("sq", KT),
                          ("sqsum", KT - 1), ("r2", 1), ("xs", KT), ("xshi", KT), ("xslo", KT), ("hhi", FT),
                          ("hlo", FT), ("w2", FT - 1), ("y", KT)):
            ev.add(name, per)
        mean = Slots(ev, "mean", psum[0:1], ["ms"])
        early = [f"{ab}{j}" for j in range(AHEAD) for ab in "ab"]
        late = [f"{ab}{j}" for j in range(AHEAD, FT) for ab in "ab"]
        turned = [f"t{t}" for t in range(TT)]
        dense = Slots(ev, "dense", psum[1:4], late + early + turned, early)
        acc = Slots(ev, "acc", psum[4:8], list(range(KT)))

        jobs = []
        for j in range(FT):
            cols = slice(j * P, (j + 1) * P)
            for w, parts in ((W1, w1), (W3, w3)):
                jobs.append((w[:, cols].rearrange("(kt p) n -> p kt n", p=P), ln2, *(a[:, :, cols] for a in parts)))
            jobs.append((W2[j * P:(j + 1) * P, :].rearrange("p (m n) -> p m n", n=P), None,
                         *(a[:, j, :].rearrange("p (m n) -> p m n", n=P) for a in w2)))
        s_ln2 = ctx.enter_context(nc.semaphore("m_ln2"))
        s_load = [ctx.enter_context(nc.semaphore(f"m_wload{n}")) for n in range(STAGES)]
        s_scaled, s_whi, s_wlo = (ctx.enter_context(nc.semaphore(f"m_w{n}")) for n in ("scaled", "hi", "lo"))
        block = ctx.enter_context(nc.Block())

        def scaled_so_far(n):
            return sum(scale is not None for _, scale, _, _ in jobs[:n + 1])

        @block.sync
        def _(sp):
            ev.give_credits(sp)
            sp.dma_start(ln2, ln2_w.rearrange("(m p) -> p m", p=P), allow_slow_non_contiguous=True).then_inc(s_ln2, 16)

            def load(i):
                ev.wait_before(sp, "xslo", i)
                ev.up_dma("xm_in", sp.dma_start(xm, row(xmid_d, i).rearrange("o p m t -> p (o m) t")))

            def weights(first, end):
                for n in range(first, end):
                    src = jobs[n][0]
                    if n >= STAGES:
                        sp.wait_ge(s_wlo, n - STAGES + 1)
                    sp.dma_start(stage[n % STAGES], src).then_inc(s_load[n % STAGES], 16)

            def body(i, ahead):
                ahead("xm")
                if isinstance(i, int) and i == 0:
                    weights(STAGES, len(jobs))
                    sp.wait_ge(*xmid_stored)
                sp.wait_ge(s_wlo, len(jobs))
                ev.wait_before(sp, "y", i)
                ev.up_dma("xres_in", sp.dma_start(xres, row(xmid_d, i).rearrange("o p m t -> p (o m) t")))
                dense.get_before(sp, f"t{TT - 1}", i)
                ev.up_dma("gate_in", sp.dma_start(gate, row(gate_d, i).rearrange("o p m t -> p (o m) t")))
                ev.wait_before(sp, "out_out", i)
                ev.up_dma("x_in", sp.dma_start(xt, row(x, i).rearrange("o (tt p) d -> p (o tt) d", p=P)))
                dense.wait_taken(sp, f"t{TT - 1}", i)
                ev.up_dma("out_out", sp.dma_start(row(out, i).rearrange("o (tt p) d -> p (o tt) d", p=P), xt))

            weights(0, STAGES)
            ev.landed("xm_in", sp)
            loop_parts(sp, NB, {"xm": load}, body, peel=True, first=False)
            ev.wait(sp, "out_out", NB - 1)

        @block.vector
        def _(dve):
            def weights(j):
                if j >= FT:
                    return
                for n in range(3 * j, 3 * j + 3):
                    _, scale, hi, lo = jobs[n]
                    if scale is not None:
                        dve.wait_ge(s_load[n % STAGES], 16 * (n // STAGES + 1))
                        dve.tensor_tensor(stage[n % STAGES], stage[n % STAGES], bcast(scale, 2, P),
                                          ALU.mult).then_inc(s_scaled, 1)
                for n in range(3 * j, 3 * j + 3):
                    _, scale, hi, lo = jobs[n]
                    dve.wait_ge(s_whi, n + 1)
                    dve.tensor_tensor(lo, stage[n % STAGES], hi.bitcast(F32), ALU.subtract).then_inc(s_wlo, 1)

            def scale(i):
                ev.wait(dve, "r2", i)
                for m in range(KT):
                    ev.up("xs", dve.tensor_tensor(xm[:, m, :], xm[:, m, :], r2, ALU.mult))

            def split(i):
                dense.get_before(dve, f"b{FT - 1}", i)
                for m in range(KT):
                    ev.wait(dve, "xs", i, m + 1)
                    ev.up("xshi", dve.tensor_copy(xs_hl[0][:, m, :], xm[:, m, :]))
                for m in range(KT):
                    ev.wait(dve, "xshi", i, m + 1)
                    ev.up("xslo", dve.tensor_tensor(xs_hl[1][:, m, :], xm[:, m, :],
                                                    xs_hl[0][:, m, :].bitcast(F32), ALU.subtract))

            def hidden(i, j):
                n = j % 2
                dense.wait_taken(dve, f"a{j}", i)
                dense.take(f"b{j}", dve.tensor_tensor(h[n], dense.get(dve, f"b{j}", i), silu[n], ALU.mult))
                ev.wait(dve, "hhi", i, j + 1)
                ev.up("hlo", dve.tensor_tensor(h_hl[n][1], h[n], h_hl[n][0].bitcast(F32), ALU.subtract))

            def first_hidden(i):
                for j in range(AHEAD):
                    hidden(i, j)

            def body(i, ahead):
                first = isinstance(i, int) and i == 0
                for j in range(AHEAD, FT):
                    if first:
                        weights(j + 1)
                    hidden(i, j)
                    if j == FT - 2:
                        ahead("scale")
                ahead("split")
                ev.wait(dve, "gate_in", i)
                ev.wait(dve, "xres_in", i)
                for m in range(KT):
                    acc.take(m, dve.tensor_tensor(xres[:, m, :], acc.get(dve, m, i), xres[:, m, :], ALU.add))
                for m in range(KT):
                    acc.wait_taken(dve, m, i)
                    ev.up("y", dve.tensor_tensor(gate[:, m, :], xres[:, m, :], gate[:, m, :], ALU.mult))
                ahead("hidden")
                ev.wait(dve, "x_in", i)
                for t in range(TT):
                    dense.take(f"t{t}", dve.tensor_tensor(xt[:, t, :], dense.get(dve, f"t{t}", i), xt[:, t, :],
                                                          ALU.add))

            def first_weights(_):
                dve.wait_ge(s_ln2, 16)
                weights(0)

            def second_weights(_):
                for j in range(1, AHEAD + 1):
                    weights(j)

            parts = {"weights0": first_weights, "scale": scale, "split": split, "weights": second_weights,
                     "hidden": first_hidden}
            loop_parts(dve, NB, parts, body, peel=True)

        @block.scalar
        def _(act):
            def weights(j):
                if j >= FT:
                    return
                for n in range(3 * j, 3 * j + 3):
                    _, scale, hi, _ = jobs[n]
                    if scale is not None:
                        act.wait_ge(s_scaled, scaled_so_far(n))
                    else:
                        act.wait_ge(s_load[n % STAGES], 16 * (n // STAGES + 1))
                    act.activation(hi, stage[n % STAGES], ACT.Copy).then_inc(s_whi, 1)

            def squares(i):
                ev.wait(act, "xm_in", i)
                for m in range(KT):
                    if m >= 2:
                        ev.wait(act, "sqsum", i, m - 1)
                    ev.up("sq", act.activation(sq[m % 2], xm[:, m, :], ACT.Square))

            def rms(i):
                act.preload_act_table_set(EXP_LN_SET)
                mean.take("ms", act.activation(r2, mean.get(act, "ms", i), ACT.Ln, bias=eps))
                mean.wait_taken(act, "ms", i)
                ev.up("r2", act.activation(r2, r2, ACT.Exp, scale=-0.5))
                act.preload_act_table_set(SILU_SET)

            def silu_part(i, j):
                n = j % 2
                if j >= 2:
                    dense.wait_taken(act, f"b{j - 2}", i)
                else:
                    dense.wait_taken_before(act, f"b{FT - 1}", i)
                dense.take(f"a{j}", act.activation(silu[n], dense.get(act, f"a{j}", i), ACT.Silu))

            def hi_part(i, j):
                n = j % 2
                dense.wait_taken(act, f"b{j}", i)
                if j >= 2:
                    ev.wait(act, "w2", i, j - 1)
                else:
                    acc.get_before(act, KT - 1, i)
                ev.up("hhi", act.activation(h_hl[n][0], h[n], ACT.Copy))

            def first_hidden(i):
                for j in range(AHEAD):
                    silu_part(i, j)
                for j in range(AHEAD):
                    hi_part(i, j)

            def body(i, ahead):
                first = isinstance(i, int) and i == 0
                for j in range(AHEAD, FT):
                    if first:
                        weights(j + 1)
                    silu_part(i, j)
                    hi_part(i, j)
                    if j == FT - 7:
                        ahead("squares")
                    if j == FT - 4:
                        ahead("rms")
                ahead("hidden")

            def first_weights(_):
                weights(0)

            def second_weights(_):
                for j in range(1, AHEAD + 1):
                    weights(j)

            parts = {"squares": squares, "weights0": first_weights, "rms": rms, "weights": second_weights,
                     "hidden": first_hidden}
            loop_parts(act, NB, parts, body, peel=True)

        @block.gpsimd
        def _(pool):
            def add_squares(i, ahead):
                ev.wait_before(pool, "xs", i)
                ev.wait(pool, "sq", i, 2)
                ev.up("sqsum", pool.tensor_tensor(sq_sum, sq[0], sq[1], ALU.add))
                for m in range(2, KT):
                    ev.wait(pool, "sqsum", i, m - 1)
                    ev.wait(pool, "sq", i, m + 1)
                    ev.up("sqsum", pool.tensor_tensor(sq_sum, sq_sum, sq[m % 2], ALU.add))

            loop(pool, NB, nothing, add_squares)

        @block.tensor
        def _(pe):
            def mean_square(i):
                ps = mean.open(pe, "ms", i)
                ev.wait(pe, "sqsum", i)
                mean.complete("ms", pe.matmul(ps, avg_all, sq_sum, start=True, stop=True))

            def up(i, j):
                for n, (ab, w) in enumerate((("a", w1), ("b", w3))):
                    pe.wait_ge(s_wlo, 3 * j + n + 1)
                    ps = dense.open(pe, f"{ab}{j}", i)
                    for k in range(KT):
                        if j == 0 and n == 0:
                            ev.wait(pe, "xslo", i, k + 1)
                        wh, wl = (a[:, k, j * P:(j + 1) * P] for a in w)
                        xh, xl = (a[:, k, :] for a in xs_hl)
                        pe.matmul(ps, wh, xh, start=k == 0, stop=False)
                        pe.matmul(ps, wh, xl, start=False, stop=False)
                        ins = pe.matmul(ps, wl, xh, start=False, stop=k == KT - 1)
                    dense.complete(f"{ab}{j}", ins)

            def down(i, j):
                ev.wait(pe, "hlo", i, j + 1)
                pe.wait_ge(s_wlo, 3 * j + 3)
                n = j % 2
                for m in range(KT):
                    ps = acc.open(pe, m, i) if j == 0 else acc.regions[m]
                    lh, ll = (w[:, j, m * P:(m + 1) * P] for w in w2)
                    rh, rl = h_hl[n]
                    pe.matmul(ps, lh, rh, start=j == 0, stop=False)
                    pe.matmul(ps, lh, rl, start=False, stop=False)
                    ins = pe.matmul(ps, ll, rh, start=False, stop=j == FT - 1)
                    if j == FT - 1:
                        acc.complete(m, ins)
                if j < FT - 1:
                    ev.up("w2", ins)

            def first_up(i):
                for j in range(AHEAD):
                    up(i, j)

            def body(i, ahead):
                down(i, 0)
                for j in range(AHEAD, FT):
                    up(i, j)
                    down(i, j - 1)
                    if j == FT - 4:
                        ahead("ms")
                down(i, FT - 1)
                ahead("up")
                ev.wait(pe, "y", i)
                for t in range(TT):
                    ps = dense.open(pe, f"t{t}", i)
                    for m in range(KT):
                        ins = pe.transpose(ps[:, m * P:(m + 1) * P], gate[:, m, t * P:(t + 1) * P], ident)
                    dense.complete(f"t{t}", ins)

            def before(part):
                if part in ("up", "body"):
                    dense.skip(pe, {"up": late, "body": turned}[part], -1)

            def skip(part):
                if part == "up":
                    dense.skip(pe, early, NB)

            loop_parts(pe, NB, {"ms": mean_square, "up": first_up}, body, before=before, skip=skip)


_INS = ["L0_attn_x", "L0_attn_Wq", "L0_attn_Wk", "L0_attn_Wkg1", "L0_attn_Wkg2", "L0_attn_bkg2", "L0_attn_Wv",
        "L0_attn_Wg", "L0_attn_bg", "L0_attn_Wo", "L0_attn_ln1_w", "L0_attn_ln2_w", "L0_attn_W1", "L0_attn_W3",
        "L0_attn_W2", "L0_ffn_U", "L0_ffn_V", "L0_ffn_W1", "L0_ffn_b1", "L0_ffn_W2", "L0_ffn_b2"]


def build(nc, x, Wq, Wk, Wkg1, Wkg2, bkg2, Wv, Wg, bg, Wo, ln1_w, ln2_w, W1, W3, W2, U, V, fW1, fb1, fW2, fb2, out):
    NB, T, D = x.shape
    KT = D // P
    scratch = [nc.dram_tensor(f"scratch_{n}", (NB, P, KT, T), F32, kind="Internal").ap()
               for n in ("xn", "gate", "xmid")]
    xn_d, gate_d, xmid_d = scratch
    r1_d = nc.dram_tensor("scratch_r1", (NB, T), F32, kind="Internal").ap()
    with ExitStack() as ctx:
        consts = [ctx.enter_context(nc.sbuf_tensor(n, s, F32))[:] for n, s in (
            ("ident", [P, P]), ("hmask", [P, 8]), ("causal", [P, P]), ("avg32", [P, P]), ("avg_all", [P, P]),
            ("ones", [P, P]), ("eps", [P, 1]))]
        make_constants(nc, consts, D)
        shared = [ctx.enter_context(nc.sbuf_tensor(n, [P, KT, T], F32))[:] for n in ("row0", "row1", "row2")]
        with ExitStack() as actx:
            aw = attention_weights(nc, actx, KT, D, Wk.shape[1], Wkg1.shape[1])

            def background(sems, pool):
                prepare_attention_weights(nc, sems, pool, aw, Wq, Wk, Wkg1, Wkg2, bkg2, Wv, Wg, bg, Wo, ln1_w)

            gate_stored = phase_f(nc, ctx, background, consts, shared, x, U, V, fW1, fb1, fW2, fb2, xn_d, r1_d, gate_d)
            xmid_stored = phase_a(nc, ctx, consts, gate_stored, shared, aw, xn_d, r1_d, xmid_d)
        phase_m(nc, consts, xmid_stored, shared, x, xmid_d, gate_d, W1, W3, W2, ln2_w, out)


def kernel(**inputs):
    import numpy as _np
    import concourse.bacc as _bacc
    from concourse.bass_utils import run_bass_kernel_spmd as _run

    nc = _bacc.Bacc("TRN2", target_bir_lowering=False, num_devices=1)
    arrays, args = {}, []
    for name in _INS:
        a = _np.ascontiguousarray(inputs[name])
        arrays[f"in_{name}"] = a
        args.append(nc.dram_tensor(f"in_{name}", a.shape, mybir.dt.from_np(a.dtype), kind="ExternalInput").ap())
    shape = inputs["L0_attn_x"].shape
    out = nc.dram_tensor("out", shape, F32, kind="ExternalOutput").ap()
    build(nc, *args, out)
    r = _run(nc, [arrays], core_ids=[0])
    return r.results[0]["out"]
```
